# Optimizing a Trainium2 kernel written in Bass

```python
import numpy as np
import jax
import jax.numpy as jnp

def _softmax(x, axis=-1):
    return jax.nn.softmax(x, axis=axis)

def _gelu(x):
    return jax.nn.gelu(x, approximate=True)

def _silu(x):
    return jax.nn.silu(x)

def _sigmoid(x):
    return jax.nn.sigmoid(x)

def _layernorm(x, axis=-1, eps=1e-05):
    m = jnp.mean(x, axis=axis, keepdims=True)
    v = jnp.var(x, axis=axis, keepdims=True)
    return (x - m) / jnp.sqrt(v + eps)

def _scatter_add(tgt, idx, src, axis=0):
    return tgt.at[idx].add(src)

def _segment_sum(src, seg, n):
    return jax.ops.segment_sum(src, seg, n)
kernel_name = 'mk_adaln_d2_jaxref_r8_197e6f'

def setup_inputs(seed: int=0):
    np.random.seed(seed)
    _w = jnp.asarray

    def _L0_attn_setup():
        import jax, jax.numpy as jnp
        import numpy as np
        N_HEADS = 16
        key = jax.random.key(seed)
        ks = jax.random.split(key, 6)
        B, L, D = (1, 256, 128)
        M = 256
        dh = D // N_HEADS
        s = 0.02
        return {'x': jax.random.normal(ks[0], (B, L, D), jnp.float32), 'Wqkv': jax.random.normal(ks[1], (D, 3 * D), jnp.float32) * s, 'bqkv': jax.random.normal(ks[2], (3 * D,), jnp.float32) * s, 'Wout': jax.random.normal(ks[3], (D, D), jnp.float32) * s, 'bout': jax.random.normal(ks[4], (D,), jnp.float32) * s, 'rel_emb': jax.random.normal(ks[5], (2 * M - 1, dh), jnp.float32)}
    _L0_attn_in = _L0_attn_setup()

    def _L0_ffn_setup():
        import jax, jax.numpy as jnp
        import numpy as np
        B, S, H, E, K, I = (1, 64, 128, 16, 4, 128)
        ALPHA, LIMIT = (1.702, 7.0)
        key = jax.random.key(seed)
        ks = jax.random.split(key, 7)
        return {'hidden_states': jax.random.normal(ks[0], (B, S, H), jnp.float32), 'router_w': jax.random.normal(ks[1], (H, E), jnp.float32) * 0.02, 'router_b': jax.random.normal(ks[2], (E,), jnp.float32) * 0.02, 'gate_up_proj': jax.random.normal(ks[3], (E, H, 2 * I), jnp.float32) * 0.02, 'gate_up_bias': jax.random.normal(ks[4], (E, 2 * I), jnp.float32) * 0.02, 'down_proj': jax.random.normal(ks[5], (E, I, H), jnp.float32) * 0.02, 'down_bias': jax.random.normal(ks[6], (E, H), jnp.float32) * 0.02}
    _L0_ffn_in = _L0_ffn_setup()
    _L0_c = _w((lambda *s: np.random.randn(*s).astype(np.float32) * 0.05)(16, 128))
    _L0_wmod = _w((lambda *s: np.random.randn(*s).astype(np.float32) * 0.05)(128, 6 * 128) * 128 ** (-0.5))

    def _L1_attn_setup():
        import jax, jax.numpy as jnp
        import numpy as np
        B, T, DM, H, D = (2, 512, 128, 16, 64)
        HD = H * D
        PHASE_SCALE = 10.0

        def _multiscale_phasors(num_heads, head_dim):
            d = np.arange(head_dim, dtype=np.float32) / head_dim
            base = 10000.0 ** (-d)
            head_scale = 2.0 ** (-np.arange(num_heads, dtype=np.float32))
            return jnp.asarray(2.0 * np.pi * head_scale[:, None] * base[None, :], dtype=jnp.float32)

        def _holo_fused_step(v, binder, probe):
            mem = jnp.cumsum(v * binder, axis=1)
            t = v.shape[1]
            scale = jnp.sqrt(jnp.arange(1, t + 1, dtype=jnp.float32))[None, :, None, None]
            return jnp.real(mem * probe) / scale
        key = jax.random.key(seed)
        k0, k1, k2, k3 = jax.random.split(key, 4)
        x = jax.random.normal(k0, (B, T, DM), jnp.float32)
        Wk = jax.random.normal(k1, (DM, HD), jnp.float32) / np.float32(np.sqrt(DM))
        Wv = jax.random.normal(k2, (DM, HD), jnp.float32) / np.float32(np.sqrt(DM))
        Wo = jax.random.normal(k3, (HD, DM), jnp.float32) / np.float32(np.sqrt(HD))
        gate = jnp.full((H, 2), 0.5, jnp.float32)
        freqs = _multiscale_phasors(H, D)
        return {'x': x, 'Wk': Wk, 'Wv': Wv, 'Wo': Wo, 'gate': gate, 'freqs': freqs}
    _L1_attn_in = _L1_attn_setup()

    def _L1_ffn_setup():
        import jax, jax.numpy as jnp
        import numpy as np
        DIM = 128

        def _reference_tuple_inner(x, W_r, W_k, W_v, mu_r, mu_k):
            B, T, C = x.shape
            x_prev = jnp.concatenate([jnp.zeros((B, 1, C), x.dtype), x[:, :-1, :]], axis=1)
            xr = mu_r * x + (1.0 - mu_r) * x_prev
            xk = mu_k * x + (1.0 - mu_k) * x_prev
            r = jax.nn.sigmoid(jnp.einsum('btc,dc->btd', xr, W_r))
            k = jnp.einsum('btc,dc->btd', xk, W_k)
            k_act = jnp.square(jax.nn.relu(k))
            out = r * jnp.einsum('btc,dc->btd', k_act, W_v)
            new_state = x[:, -1, :]
            return (out, new_state)
        key = jax.random.key(seed)
        ks = jax.random.split(key, 6)
        B, T, C = (8, 256, DIM)
        x = jax.random.normal(ks[0], (B, T, C), dtype=jnp.float32)
        s = 1.0 / np.sqrt(C)
        W_r = jax.random.uniform(ks[1], (C, C), jnp.float32, -s, s)
        W_k = jax.random.uniform(ks[2], (C, C), jnp.float32, -s, s)
        W_v = jax.random.uniform(ks[3], (C, C), jnp.float32, -s, s)
        mu_r = jax.random.uniform(ks[4], (C,), jnp.float32)
        mu_k = jax.random.uniform(ks[5], (C,), jnp.float32)
        return {'x': x, 'W_r': W_r, 'W_k': W_k, 'W_v': W_v, 'mu_r': mu_r, 'mu_k': mu_k}
    _L1_ffn_in = _L1_ffn_setup()
    _L1_c = _w((lambda *s: np.random.randn(*s).astype(np.float32) * 0.05)(16, 128))
    _L1_wmod = _w((lambda *s: np.random.randn(*s).astype(np.float32) * 0.05)(128, 6 * 128) * 128 ** (-0.5))
    _d = {'L0_attn_x': _L0_attn_in['x'], 'L0_attn_Wqkv': _L0_attn_in['Wqkv'], 'L0_attn_bqkv': _L0_attn_in['bqkv'], 'L0_attn_Wout': _L0_attn_in['Wout'], 'L0_attn_bout': _L0_attn_in['bout'], 'L0_attn_rel_emb': _L0_attn_in['rel_emb'], 'L0_ffn_router_w': _L0_ffn_in['router_w'], 'L0_ffn_router_b': _L0_ffn_in['router_b'], 'L0_ffn_gate_up_proj': _L0_ffn_in['gate_up_proj'], 'L0_ffn_gate_up_bias': _L0_ffn_in['gate_up_bias'], 'L0_ffn_down_proj': _L0_ffn_in['down_proj'], 'L0_ffn_down_bias': _L0_ffn_in['down_bias'], 'L0_c': _L0_c, 'L0_wmod': _L0_wmod, 'L1_attn_Wk': _L1_attn_in['Wk'], 'L1_attn_Wv': _L1_attn_in['Wv'], 'L1_attn_Wo': _L1_attn_in['Wo'], 'L1_attn_gate': _L1_attn_in['gate'], 'L1_attn_freqs': _L1_attn_in['freqs'], 'L1_ffn_W_r': _L1_ffn_in['W_r'], 'L1_ffn_W_k': _L1_ffn_in['W_k'], 'L1_ffn_W_v': _L1_ffn_in['W_v'], 'L1_ffn_mu_r': _L1_ffn_in['mu_r'], 'L1_ffn_mu_k': _L1_ffn_in['mu_k'], 'L1_c': _L1_c, 'L1_wmod': _L1_wmod}
    _x0 = _d['L0_attn_x']
    _d['L0_attn_x'] = jax.random.normal(jax.random.fold_in(jax.random.key(seed), 1), (16, 256, 128), dtype=_x0.dtype)
    del _x0
    return _d

def reference(L0_attn_x, L0_attn_Wqkv, L0_attn_bqkv, L0_attn_Wout, L0_attn_bout, L0_attn_rel_emb, L0_ffn_router_w, L0_ffn_router_b, L0_ffn_gate_up_proj, L0_ffn_gate_up_bias, L0_ffn_down_proj, L0_ffn_down_bias, L0_c, L0_wmod, L1_attn_Wk, L1_attn_Wv, L1_attn_Wo, L1_attn_gate, L1_attn_freqs, L1_ffn_W_r, L1_ffn_W_k, L1_ffn_W_v, L1_ffn_mu_r, L1_ffn_mu_k, L1_c, L1_wmod):

    def _L0_attn_ref(x, Wqkv, bqkv, Wout, bout, rel_emb):
        import jax, jax.numpy as jnp
        import numpy as np
        N_HEADS = 16
        B, L, D = x.shape
        H = N_HEADS
        dh = D // H
        qkv = x @ Wqkv + bqkv
        q, k, v = jnp.split(qkv, 3, axis=-1)
        q = q.reshape(B, L, H, dh).transpose(0, 2, 1, 3)
        k = k.reshape(B, L, H, dh).transpose(0, 2, 1, 3)
        v = v.reshape(B, L, H, dh).transpose(0, 2, 1, 3)
        content = jnp.einsum('bhid,bhjd->bhij', q, k)
        rel = jnp.einsum('bhid,rd->bhir', q, rel_emb)
        rel = jnp.pad(rel, ((0, 0), (0, 0), (0, 0), (1, 0)))[..., :L]
        scores = (content + rel) / jnp.sqrt(jnp.asarray(dh, x.dtype))
        attn = jax.nn.softmax(scores, axis=-1)
        out = jnp.einsum('bhij,bhjd->bhid', attn, v)
        out = out.transpose(0, 2, 1, 3).reshape(B, L, D)
        return out @ Wout + bout

    def _L0_ffn_ref(hidden_states, router_w, router_b, gate_up_proj, gate_up_bias, down_proj, down_bias):
        import jax, jax.numpy as jnp
        import numpy as np
        B, S, H, E, K, I = (1, 64, 128, 16, 4, 128)
        ALPHA, LIMIT = (1.702, 7.0)
        b, s, h = hidden_states.shape
        x = hidden_states.reshape(-1, h)
        logits = x @ router_w + router_b
        topv, topi = jax.lax.top_k(logits, K)
        topw = jax.nn.softmax(topv, axis=-1)
        one_hot = (topi[..., None] == jnp.arange(E)).astype(topw.dtype)
        scores = jnp.einsum('tk,tke->te', topw, one_hot)
        gu = jnp.einsum('th,ehf->tef', x, gate_up_proj) + gate_up_bias
        gate = jnp.minimum(gu[..., ::2], LIMIT)
        up = jnp.clip(gu[..., 1::2], -LIMIT, LIMIT)
        glu = gate * jax.nn.sigmoid(gate * ALPHA)
        act = (up + 1.0) * glu
        expert_out = jnp.einsum('tei,eih->teh', act, down_proj) + down_bias
        out = jnp.einsum('te,teh->th', scores, expert_out)
        return out.reshape(b, s, h)

    def _L1_attn_ref(x, Wk, Wv, Wo, gate, freqs):
        import jax, jax.numpy as jnp
        import numpy as np
        B, T, DM, H, D = (2, 512, 128, 16, 64)
        HD = H * D
        PHASE_SCALE = 10.0

        def _multiscale_phasors(num_heads, head_dim):
            d = np.arange(head_dim, dtype=np.float32) / head_dim
            base = 10000.0 ** (-d)
            head_scale = 2.0 ** (-np.arange(num_heads, dtype=np.float32))
            return jnp.asarray(2.0 * np.pi * head_scale[:, None] * base[None, :], dtype=jnp.float32)

        def _holo_fused_step(v, binder, probe):
            mem = jnp.cumsum(v * binder, axis=1)
            t = v.shape[1]
            scale = jnp.sqrt(jnp.arange(1, t + 1, dtype=jnp.float32))[None, :, None, None]
            return jnp.real(mem * probe) / scale
        Bb, Tt, _ = x.shape
        k_real = (x @ Wk).reshape(Bb, Tt, H, D)
        v = (x @ Wv).reshape(Bb, Tt, H, D).astype(jnp.complex64)
        k = jnp.exp(1j * (k_real * PHASE_SCALE))
        t = jnp.arange(Tt, dtype=jnp.float32)
        rotors = jnp.exp(1j * (t[:, None, None] * freqs))[None]
        out_pos = _holo_fused_step(v, rotors, jnp.conj(rotors))
        k_shifted = jnp.roll(k, 1, axis=1).at[:, 0].set(0.0)
        out_assoc = _holo_fused_step(v, jnp.conj(k_shifted), k)
        g_pos = gate[:, 0][None, None, :, None]
        g_assoc = gate[:, 1][None, None, :, None]
        out = out_pos * g_pos + out_assoc * g_assoc
        return out.reshape(Bb, Tt, HD) @ Wo

    def _L1_ffn_ref(x, W_r, W_k, W_v, mu_r, mu_k):
        import jax, jax.numpy as jnp
        import numpy as np
        DIM = 128

        def _reference_tuple_inner(x, W_r, W_k, W_v, mu_r, mu_k):
            B, T, C = x.shape
            x_prev = jnp.concatenate([jnp.zeros((B, 1, C), x.dtype), x[:, :-1, :]], axis=1)
            xr = mu_r * x + (1.0 - mu_r) * x_prev
            xk = mu_k * x + (1.0 - mu_k) * x_prev
            r = jax.nn.sigmoid(jnp.einsum('btc,dc->btd', xr, W_r))
            k = jnp.einsum('btc,dc->btd', xk, W_k)
            k_act = jnp.square(jax.nn.relu(k))
            out = r * jnp.einsum('btc,dc->btd', k_act, W_v)
            new_state = x[:, -1, :]
            return (out, new_state)
        return _reference_tuple_inner(x, W_r, W_k, W_v, mu_r, mu_k)[0]
    x = L0_attn_x
    mod = (_silu(L0_c) @ L0_wmod).reshape(L0_c.shape[0], 6, 1, -1)
    sa, ca, ga, sb, cb, gb = (mod[:, 0], mod[:, 1], mod[:, 2], mod[:, 3], mod[:, 4], mod[:, 5])
    ga = (2 * (ga >= 0) - 1) * jnp.maximum(jnp.abs(ga), 0.25)
    gb = (2 * (gb >= 0) - 1) * jnp.maximum(jnp.abs(gb), 0.25)
    h = _layernorm(x, axis=-1) * (1 + ca) + sa
    x = x + ga * _L0_attn_ref(h, L0_attn_Wqkv, L0_attn_bqkv, L0_attn_Wout, L0_attn_bout, L0_attn_rel_emb)
    h = _layernorm(x, axis=-1) * (1 + cb) + sb
    x = x + gb * _L0_ffn_ref(h, L0_ffn_router_w, L0_ffn_router_b, L0_ffn_gate_up_proj, L0_ffn_gate_up_bias, L0_ffn_down_proj, L0_ffn_down_bias)
    mod = (_silu(L1_c) @ L1_wmod).reshape(L1_c.shape[0], 6, 1, -1)
    sa, ca, ga, sb, cb, gb = (mod[:, 0], mod[:, 1], mod[:, 2], mod[:, 3], mod[:, 4], mod[:, 5])
    ga = (2 * (ga >= 0) - 1) * jnp.maximum(jnp.abs(ga), 0.25)
    gb = (2 * (gb >= 0) - 1) * jnp.maximum(jnp.abs(gb), 0.25)
    h = _layernorm(x, axis=-1) * (1 + ca) + sa
    x = x + ga * _L1_attn_ref(h, L1_attn_Wk, L1_attn_Wv, L1_attn_Wo, L1_attn_gate, L1_attn_freqs)
    h = _layernorm(x, axis=-1) * (1 + cb) + sb
    x = x + gb * _L1_ffn_ref(h, L1_ffn_W_r, L1_ffn_W_k, L1_ffn_W_v, L1_ffn_mu_r, L1_ffn_mu_k)
    return x

_drawn_inputs = setup_inputs


def setup_inputs(seed=0):
    import zlib

    import numpy as np

    out = dict(_drawn_inputs(seed))
    spreads = {'L1_attn_gate': (0.5, 0.589)}
    factors = {'L0_attn_Wqkv': 8.0,
     'L0_attn_bqkv': 8.0,
     'L0_attn_Wout': 8.0,
     'L0_attn_bout': 6.715,
     'L0_attn_rel_emb': 8.0,
     'L0_ffn_router_w': 8.0,
     'L0_ffn_router_b': 8.0,
     'L0_ffn_gate_up_proj': 8.0,
     'L0_ffn_gate_up_bias': 8.0,
     'L0_ffn_down_proj': 8.0,
     'L0_ffn_down_bias': 8.0,
     'L0_c': 5.291,
     'L0_wmod': 5.152,
     'L1_ffn_W_r': 8.0,
     'L1_ffn_W_k': 2.984,
     'L1_ffn_W_v': 2.752,
     'L1_ffn_mu_r': 8.0,
     'L1_ffn_mu_k': 4.689}
    for name, (base, spread) in spreads.items():
        noise = np.random.default_rng([zlib.crc32(name.encode()), seed]).standard_normal(out[name].shape)
        drawn = base * np.exp(spread * noise) if base else spread * noise
        out[name] = jnp.asarray(drawn.astype(out[name].dtype))
    for name, factor in factors.items():
        out[name] = (out[name] * factor).astype(out[name].dtype)
    return out
```

```python
from contextlib import ExitStack

import concourse.bass as bass
from concourse import mybir

F32 = mybir.dt.float32
BF16 = mybir.dt.bfloat16
I32 = mybir.dt.int32
ALU = mybir.AluOpType
ACT = mybir.ActivationFunctionType
AX_X = mybir.AxisListType.X

P = 128
B = 16
L = 256
D = 128
NT = L // P
H = 16
DH = D // H
E = 16
TOPK = 4
HD = 1024
CT = HD // P
CC = 4
ST = 8
NPT = 3
EPS = 1e-5
ALPHA, LIMIT = 1.702, 7.0
TWO_PI = 6.283185307179586
TWO_PI_IN = 6.283185
PI_IN = 3.1415925
MAGIC = 12582912.0
C1, C2, C3 = 6.28125, 0.0019350051879882812, 3.0199159819567e-07
BIG = 3.0e38

PER = dict(
    x_in=16, xt_ps=1, xt=1, mean1=1, cent1=1, sq1=1, var1=1, veps1=1, rstd1=1, rbc1=1, norm1=1, h1=1,
    qk_ps=1, v_ps=1, q_sb=1, k_sb=1, v_sb=NT, part0=1, rest0=1, part1=1, part2=1, qk_rows=16 * 18,
    s_ps=ST, s_max=ST, neg=1, mp0=1, mr0=1, mp1=1, mp2=1, m_ps=1, m_sb=1, m_rows=16,
    st_ps=ST, prob=ST, pv=ST, den=1, o_sb=NT, ot_ps=1, ot_sb=1, y_ps=1, ya=1, x1=1,
    mean2=1, cent2=1, sq2=1, var2=1, veps2=1, rstd2=1, rbc2=1, norm2=1, h2=1,
    lg_ps=1, lg=1, top8=NT, shift=1, repl=NT, ex=1, exm=NT, esum=1, rsum=1, sc=1,
    sp0=1, sr0=1, sp1=1, sp2=1, sct_ps=1, sctf=1, sctb=1, bc_ps=4, bc=4,
    gu_ps=8, gc=8, sig=8, gsc=8, upc=8, gl=8, act=8, dn=8, y2=1, x2=1, mod_a=1,
    mod_b=1, mean3=1, cent3=1, sq3=1, var3=1, veps3=1, rstd3=1, rbc3=1, norm3=1, h3=1,
    k_ps=CC, v2_ps=CC, turn=CC, frac=CC, sin=CC, fabs=CC, cos=CC, vpos=2 * CC, vas=2 * CC,
    in1=CC, in2=CC, in3=CC, in4=CC, cu1=CC, cu2=CC, cu3=CC, cu4=CC,
    pr1=CC, pr2=CC, pr3=CC, pr4=CC, sum12=CC, sum34=CC, wo=CC, yv=1, x3=1,
    mean4=1, cent4=1, sq4=1, var4=1, veps4=1, rstd4=1, rbc4=1, norm4=1, h4=1,
    dif=1, xr=1, xk=1, rk_ps=1, rsig=1, krel=1, ksq=1, vv_ps=1, rv=1, x4=1, xo_ps=1, xo=1, out=16,
)


def build(nc, x, Wqkv, bqkv, Wout, bout, rel_emb, router_w, router_b, gup, gub, down, downb, c0, wmod0,
          Wk, Wv, Wo, gate, freqs, W_r, W_k, W_v, mu_r, mu_k, c1, wmod1, out):
    with ExitStack() as ctx:
        def sb(name, shape, dt=F32):
            return ctx.enter_context(nc.sbuf_tensor(name, shape, dt))

        wqkv = sb("wqkv", [P, 3 * D])
        wout = sb("wout", [P, D])
        wgu = sb("wgu", [P, E, 2, D])
        wdown = sb("wdown", [P, E, D])
        wrout = sb("wrout", [P, E])
        wk = sb("wk", [P, HD])
        wv = sb("wv", [P, HD])
        wo = sb("wo", [P, CT, D])
        ffn_w = sb("ffn_w", [P, 3, D])
        ident = sb("ident", [P, P])
        identb = sb("identb", [P, P], BF16)
        mean_w = sb("mean_w", [P, P])
        bcol = sb("bcol", [P, 4])
        mu = sb("mu", [P, 2])
        vbias = sb("vbias", [P, D])
        rbias = sb("rbias", [P, E])
        rel_in = sb("rel_in", [P, NT, DH])
        rel_rep = sb("rel_rep", [P, NT, DH, H])
        wqk = sb("wqk", [P, 2, DH, H])
        relb = sb("relb", [P, L])
        c_in = sb("c_in", [B, 2, D])
        c_sig = sb("c_sig", [B, 2, D])
        c_t = sb("c_t", [P, 2, B])
        mods = sb("mods", [P, 13, B])
        mod_abs = sb("mod_abs", [P, 2, B])
        mod_sgn = sb("mod_sgn", [P, 2, B])
        bias_rows = sb("bias_rows", [P, E, 2, D], BF16)
        ones_b = sb("ones_b", [P, L], BF16)
        sel = sb("sel", [P, E, P], BF16)
        dbias = sb("dbias", [P, D])
        t_int = sb("t_int", [P, L], I32)
        t_f = sb("t_f", [P, L])
        inv_s = sb("inv_s", [P, L])
        mhalf = sb("mhalf", [P, NT])
        veps = sb("veps", [P, NT])
        rstd = sb("rstd", [P, NT])
        vepsb = sb("vepsb", [P, NT])
        rstdb = sb("rstdb", [P, NT])
        fcol = sb("fcol", [P, CT])
        gcol = sb("gcol", [P, 2, CT])
        cos_r = sb("cos_r", [P, CT, L])
        sin_r = sb("sin_r", [P, CT, L])
        keep = sb("keep", [P, 2 * L])
        half_pi = sb("half_pi", [P, 1])
        magic = sb("magic", [P, 1])

        x_in = sb("x_in", [P, NT, D])
        xt = sb("xt", [P, L])
        cent = sb("cent", [P, L])
        sq = sb("sq", [P, L])
        ht = sb("ht", [P, L])
        mod_a = sb("mod_a", [P, 13])
        qk = sb("qk", [P, 2, L])
        qk_part = sb("qk_part", [P, 3, 2, L], BF16)
        vt = sb("vt", [P, NT, H, DH + 1])
        q_rows = sb("q_rows", [75, H, L], BF16)
        k_rows = sb("k_rows", [75, H, L], BF16)
        smax = sb("smax", [P, NT, H])
        negm = sb("negm", [P, NT, H])
        mrest = sb("mrest", [P, NT, H])
        mpart = sb("mpart", [P, NT, 3, H], BF16)
        m_sb = sb("m_sb", [3 * H, L], BF16)
        prob = sb("prob", [P, NPT, 2, NT, L])
        rden = sb("rden", [P, NT, H])
        o_tok = sb("o_tok", [P, NT, H, DH])
        o_t = sb("o_t", [P, L])
        ya = sb("ya", [P, L])
        x1 = sb("x1", [P, L])
        lg = sb("lg", [P, NT, TOPK + E])
        top8 = sb("top8", [P, NT, 8])
        repl = sb("repl", [P, NT, TOPK + E])
        lsh = sb("lsh", [P, NT, E])
        ex = sb("ex", [P, NT, E])
        exm = sb("exm", [P, NT, E])
        esum = sb("esum", [P, NT])
        rsum = sb("rsum", [P, NT])
        sc = sb("sc", [P, NT, P])
        srest = sb("srest", [P, NT, E])
        sc_part = sb("sc_part", [P, NT, P], BF16)
        sct = sb("sct", [P, L])
        sctb = sb("sctb", [P, L], BF16)
        sc_all = sb("sc_all", [P, E, L])
        sig = sb("sig", [P, 2, 2 * L])
        gsc = sb("gsc", [P, 2, 2 * L])
        upc = sb("upc", [P, 2, 2 * L])
        x2 = sb("x2", [P, L])

        wmod = prob[:, :, :, :, :].rearrange("p s i k q -> p (s i k q)")[:, 0:12 * D].rearrange("p (l n) -> p l n", l=2)
        ffn_raw = sig[:, 0, 0:3 * D].rearrange("p (n c) -> p n c", n=3)
        bl = gsc[0:E, 0, 0:2 * D].rearrange("e (f g) -> e f g", g=2)
        bd = gsc[0:E, 0, 2 * D:4 * D].rearrange("e (g f) -> e g f", g=2)
        brest = gsc[0:E, 1, 0:2 * D]
        bp = upc[0:E, 0, :].bitcast(BF16)[:, 0:6 * D].rearrange("e (n f) -> e n f", n=3)

        t_next = cent
        mhalf_w = sq

        mod_b = sb("mod_b", [P, 13])
        centb = sb("centb", [P, L])
        sqb = sb("sqb", [P, L])
        hb = sb("hb", [P, L + 1])
        xb = sb("xb", [P, L])
        turn = sb("turn", [P, 2 * L])
        frac = sb("frac", [P, 2, 2 * L])
        fabs = sb("fabs", [P, 2 * L])
        sin_t = sb("sin_t", [P, 2, 2, L + 1])
        cos_t = sb("cos_t", [P, 2, 2, L + 1])
        vpos = sb("vpos", [P, 2 * L])
        vas = sb("vas", [P, 2 * L])
        prod = sb("prod", [P, 2, 4, 2 * L])
        x3 = sb("x3", [P, L])
        dif = sb("dif", [P, L])
        xr = sb("xr", [P, L])
        xk = sb("xk", [P, L])
        rsig = sb("rsig", [P, L])
        ksq = sb("ksq", [P, L])
        x4 = sb("x4", [P, L])
        xo = sb("xo", [P, NT, D])

        ring = ctx.enter_context(nc.psum_tensor("ring", [P, 2, 1024], F32))
        pa = ctx.enter_context(nc.psum_tensor("pa", [P, 512], F32))
        pb_k = ctx.enter_context(nc.psum_tensor("pb_k", [P, 512], F32))
        pb_v = ctx.enter_context(nc.psum_tensor("pb_v", [P, 512], F32))
        pb = ctx.enter_context(nc.psum_tensor("pb", [P, 512], F32))
        pv_ps = pa[:, 0:NT * H * (DH + 1)].rearrange("p (n h d) -> p n h d", n=NT, h=H)

        S = {name: ctx.enter_context(nc.semaphore(name)) for name in PER}

        def setup_sem(name):
            return ctx.enter_context(nc.semaphore("set_" + name))

        ld_w, ld_mod, ld_gu, ld_bias, ld_small, ld_rows = (
            setup_sem(n) for n in ("ld_w", "ld_mod", "ld_gu", "ld_bias", "ld_small", "ld_rows"))
        c_zero, c_pool, c_act, c_pe, c_dve, c_split, c_fill = (
            setup_sem(n) for n in ("zero", "pool", "act", "pe", "dve", "split", "fill"))
        N_W, N_SMALL = 9, 27

        def need(eng, name, b, k):
            v = b * PER[name] + k
            if not isinstance(v, int) or v > 0:
                eng.wait_ge(S[name], v)

        block = ctx.enter_context(nc.Block())

        @block.sync
        def _(sp):
            sp.dma_start(c_in[:, 0, :], c0).then_inc(ld_mod, 16)
            sp.dma_start(c_in[:, 1, :], c1).then_inc(ld_mod, 16)
            sp.dma_start(wmod[:, 0, :], wmod0).then_inc(ld_mod, 16)
            sp.dma_start(wmod[:, 1, :], wmod1).then_inc(ld_mod, 16)
            sp.dma_start(wqkv[:, :], Wqkv).then_inc(ld_w, 16)
            sp.dma_start(wout[:, :], Wout).then_inc(ld_w, 16)
            sp.dma_start(wrout[:, :], router_w).then_inc(ld_w, 16)
            sp.dma_start(wk[:, :], Wk).then_inc(ld_w, 16)
            sp.dma_start(wv[:, :], Wv).then_inc(ld_w, 16)
            sp.dma_start(wo[:, :, :], Wo.rearrange("(k p) m -> p k m", p=P)).then_inc(ld_w, 16)
            for n, w in enumerate((W_r, W_k, W_v)):
                sp.dma_start(ffn_raw[:, n, :], w).then_inc(ld_w, 16)
            sp.dma_start(sc_all[:, :, :], gup.rearrange("e h f -> h e f")).then_inc(ld_gu, 16)
            sp.dma_start(wdown[:, :, :], down.rearrange("e i h -> i e h")).then_inc(ld_gu, 16)
            sp.wait_ge(c_split, 5)
            sp.wait_ge(c_zero, 1)
            for n in range(3):
                sp.dma_start(bias_rows[n:n + 1, :, :, :].rearrange("p e g f -> p e (g f)"),
                             bp[:, n, :]).then_inc(ld_rows, 16)

            def load_x(b):
                sp.wait_ge(ld_gu, 32)
                need(sp, "xt_ps", b, 0)
                src = x[bass.ds(b, 1)] if not isinstance(b, int) else x[b:b + 1]
                sp.dma_start(x_in[:, :, :], src.rearrange("a (n p) f -> p (a n) f", p=P)).then_inc(S["x_in"], 16)

            def spread(b):
                sp.wait_ge(ld_gu, 32)
                need(sp, "part2", b, 1)
                need(sp, "den", b, 0)
                for a in range(3):
                    for c in range(3):
                        r = (a * 3 + c) * DH
                        for rows, n, m in ((q_rows, 0, a), (k_rows, 1, c)):
                            sp.dma_start(rows[r:r + DH, :, :],
                                         qk_part[:, m, n, :]).then_inc(S["qk_rows"], 16)

            def spread_max(b):
                need(sp, "m_sb", b, 1)
                sp.dma_start(q_rows[72:75, :, :], m_sb[:, :]).then_inc(S["m_rows"], 16)

            def store(b):
                sp.wait_ge(ld_gu, 32)
                need(sp, "xo", b, 1)
                dst = out[bass.ds(b, 1)] if not isinstance(b, int) else out[b:b + 1]
                sp.dma_start(dst.rearrange("a (n p) f -> p (a n) f", p=P), xo[:, :, :]).then_inc(S["out"], 16)

            def step(a, b):
                if a is not None:
                    load_x(a)
                    spread(a)
                    spread_max(a)
                if b is not None:
                    store(b)

            run(sp, step)
            sp.wait_ge(S["out"], 16 * B)

        @block.gpsimd
        def _(pool):
            pool.memset(bias_rows[:, :, :, :], 0.0).then_inc(c_zero, 1)
            for t in (ident, identb, sel):
                pool.memset(t[tuple(slice(None) for _ in t.shape)], 0.0).then_inc(c_pool, 1)
            pool.wait_ge(c_pool, 3)
            for t in (ident, identb):
                pool.affine_select(out=t[:, :], in_=t[:, :], compare_op=ALU.not_equal, fill=1.0, base=0,
                                   pattern=[[-1, P]], channel_multiplier=1).then_inc(c_pool, 1)
            for n in range(3):
                pool.wait_ge(c_pool, 5 + n)
                pool.affine_select(out=sel[:, :, :], in_=sel[:, :, :], compare_op=ALU.not_equal, fill=1.0,
                                   base=-16 * n, pattern=[[-1, E], [0, P]], channel_multiplier=1).then_inc(c_pool, 1)
            pool.iota(t_int[:, :], pattern=[[1, L]], base=0, channel_multiplier=0).then_inc(c_pool, 1)
            pool.wait_ge(ld_gu, 32)
            pool.tensor_copy(wgu[:, :, 0, :], sc_all[:, :, 0:L:2]).then_inc(c_pool, 1)
            pool.tensor_copy(wgu[:, :, 1, :], sc_all[:, :, 1:L:2]).then_inc(c_pool, 1)

            pool.wait_ge(c_dve, DVE_TRIG + 1)
            pool.tensor_tensor(inv_s[:, :], t_next[:, :], mhalf_w[:, :], ALU.pow).then_inc(c_pool, 1)

            def deviation(b, n, v, r):
                need(pool, "veps" + n, b, 1)
                pool.tensor_tensor(r[:, :], v[:, :], mhalf[:, 0:NT], ALU.pow).then_inc(S["rstd" + n], 1)

            def rest_q(b):
                need(pool, "part0", b, 1)
                need(pool, "q_sb", b, 1)
                need(pool, "k_sb", b, 1)
                pool.tensor_tensor(qk[:, :, :], qk[:, :, :], qk_part[:, 0, :, :], ALU.subtract).then_inc(S["rest0"], 1)
                need(pool, "part1", b, 1)
                need(pool, "rest0", b, 1)
                pool.tensor_tensor(qk_part[:, 2, :, :], qk[:, :, :], qk_part[:, 1, :, :], ALU.subtract).then_inc(S["part2"], 1)

            def residual1(b):
                need(pool, "ya", b, 1)
                need(pool, "xt", b, 1)
                need(pool, "x2", b, 0)
                pool.tensor_tensor(x1[:, :], xt[:, :], ya[:, :], ALU.add).then_inc(S["x1"], 1)

            def expert_pair(b, n):
                sca = sc_all[:, 2 * n:2 * n + 2, :].rearrange("p e t -> p (e t)")
                if n % 2 == 0:
                    need(pool, "bc", b, n // 2 + 1)
                need(pool, "sig", b, n + 1)
                pool.tensor_tensor(gsc[:, n % 2, :], gsc[:, n % 2, :], sca, ALU.mult).then_inc(S["gsc"], 1)
                need(pool, "gsc", b, n + 1)
                pool.tensor_tensor(gsc[:, n % 2, :], sig[:, n % 2, :], gsc[:, n % 2, :], ALU.mult).then_inc(S["gl"], 1)
                need(pool, "upc", b, n + 1)
                need(pool, "gl", b, n + 1)
                pool.tensor_tensor(upc[:, n % 2, :], upc[:, n % 2, :], gsc[:, n % 2, :], ALU.mult).then_inc(S["act"], 1)

            def memory_in(b, c):
                h = c % 2
                need(pool, "vpos", b, 2 * c + 2)
                need(pool, "wo", b, c - 1)
                pool.tensor_tensor(prod[:, h, 0, :], vpos[:, :],
                                   cos_r[:, 2 * c:2 * c + 2, :].rearrange("p k t -> p (k t)"), ALU.mult).then_inc(S["in1"], 1)
                pool.tensor_tensor(prod[:, h, 1, :], vpos[:, :],
                                   sin_r[:, 2 * c:2 * c + 2, :].rearrange("p k t -> p (k t)"), ALU.mult).then_inc(S["in2"], 1)

            def memory_out(b, c):
                h = c % 2
                for n, t in ((0, cos_r), (1, sin_r)):
                    need(pool, "cu" + str(n + 1), b, c + 1)
                    pool.tensor_tensor(prod[:, h, n, :], prod[:, h, n, :],
                                       t[:, 2 * c:2 * c + 2, :].rearrange("p k t -> p (k t)"), ALU.mult).then_inc(S["pr" + str(n + 1)], 1)
                need(pool, "pr1", b, c + 1)
                need(pool, "pr2", b, c + 1)
                pool.tensor_tensor(prod[:, h, 0, :], prod[:, h, 0, :], prod[:, h, 1, :], ALU.add).then_inc(S["sum12"], 1)

            def step(a, b):
                if a is not None:
                    deviation(a, "1", veps, rstd)
                    rest_q(a)
                if b is not None:
                    deviation(b, "3", vepsb, rstdb)
                    memory_in(b, 0)
                    memory_in(b, 1)
                    memory_out(b, 0)
                    memory_out(b, 1)
                    memory_in(b, 2)
                if a is not None:
                    residual1(a)
                    deviation(a, "2", veps, rstd)
                if b is not None:
                    memory_in(b, 3)
                    memory_out(b, 2)
                    memory_out(b, 3)
                    deviation(b, "4", vepsb, rstdb)
                if a is not None:
                    for n in range(8):
                        expert_pair(a, n)

            run(pool, step)

        @block.tensor
        def _(pe):
            mm = nc.tensor.matmul
            tr = nc.tensor.transpose
            pe.wait_ge(c_pool, 5)
            pe.wait_ge(c_dve, 1)
            for l in range(2):
                last = tr(pa[:, l * B:(l + 1) * B], c_in[:, l, :], ident[0:B, 0:B])
            last.then_inc(c_pe, 1)
            pe.wait_ge(c_dve, 2)
            for l in range(2):
                for k in range(6):
                    last = mm(pa[:, 64 + (l * 6 + k) * B:64 + (l * 6 + k + 1) * B], lhsT=wmod[:, l, k * D:(k + 1) * D],
                              rhs=c_t[:, l, :], start=True, stop=True, skip_group_check=True)
            last.then_inc(c_pe, 1)
            pe.wait_ge(ld_w, 16 * N_W)
            for n in range(3):
                last = tr(pb_k[:, n * D:(n + 1) * D], ffn_raw[:, n, :], ident[:, :])
            last.then_inc(c_pe, 1)
            pe.wait_ge(c_dve, 3)
            for n in range(NT):
                last = tr(pb_v[:, n * P:(n + 1) * P], rel_rep[:, n, :, :].rearrange("p d h -> p (d h)"), ident[:, :])
            last.then_inc(c_pe, 1)
            pe.wait_ge(c_dve, DVE_SETUP)

            def stats(b, n, src, src_sem, ps, free, sqt, rs):
                need(pe, src_sem, b, 1)
                for s in free:
                    need(pe, s[0], b, s[1])
                mm(ps[:, 0:L], lhsT=mean_w[:, :], rhs=src, start=True, stop=True,
                   skip_group_check=True).then_inc(S["mean" + n], 1)
                need(pe, "sq" + n, b, 1)
                for t in range(NT):
                    last = mm(ps[:, L + t:L + t + 1], lhsT=sqt[:, t * P:(t + 1) * P], rhs=mean_w[:, 0:1], start=True,
                              stop=True, skip_group_check=True)
                last.then_inc(S["var" + n], 1)
                need(pe, "rstd" + n, b, 1)
                for t in range(NT):
                    last = mm(ps[:, L + t * P:L + (t + 1) * P], lhsT=rs[:, t:t + 1].to_broadcast([P, P]), rhs=ident[:, :],
                              start=True, stop=True, skip_group_check=True)
                last.then_inc(S["rbc" + n], 1)

            def turn_x(b):
                need(pe, "x_in", b, 16)
                need(pe, "gc", b, 0)
                need(pe, "upc", b, 0)
                for n in range(NT):
                    last = tr(ring[:, 0, n * P:(n + 1) * P], x_in[:, n, :], ident[:, :])
                last.then_inc(S["xt_ps"], 1)

            def project(b):
                need(pe, "h1", b, 1)
                for n in range(2):
                    last = mm(ring[:, 1, n * L:(n + 1) * L], lhsT=wqk[:, n, :, :].rearrange("p d h -> p (d h)"), rhs=ht[:, :],
                              start=True, stop=True, skip_group_check=True)
                last.then_inc(S["qk_ps"], 1)
                for n in range(NT):
                    last = mm(ring[:, 1, 512 + n * D:512 + (n + 1) * D], lhsT=ht[:, n * P:(n + 1) * P],
                              rhs=wqkv[:, 2 * D:3 * D], start=True, stop=True, skip_group_check=True)
                last.then_inc(S["v_ps"], 1)

            def scores(b, n):
                if n == 0:
                    need(pe, "qk_rows", b, 16 * 18)
                    need(pe, "xt", b, 1)
                if n == 1:
                    need(pe, "q_sb", b, 1)
                    need(pe, "k_sb", b, 1)
                    need(pe, "v_sb", b, NT)
                if n >= 2:
                    need(pe, "s_max", b, n - 1)
                for j in range(4):
                    h = 4 * (n % 4) + j
                    last = mm(ring[:, n % 2, j * L:(j + 1) * L], lhsT=q_rows[0:72, h, (n // 4) * P:(n // 4 + 1) * P],
                              rhs=k_rows[0:72, h, :], start=True, stop=True, skip_group_check=True)
                last.then_inc(S["s_ps"], 1)

            def turn_max(b):
                pe.wait_ge(c_dve, DVE_SETUP)
                need(pe, "mp2", b, 1)
                for n in range(NT):
                    last = tr(ring[0:3 * H, 0, :].bitcast(BF16)[:, n * P:(n + 1) * P],
                              mpart[:, n, :, :].rearrange("p a h -> p (a h)"), identb[:, :])
                last.then_inc(S["m_ps"], 1)

            def scores_t(b, n):
                if n == 0:
                    need(pe, "m_rows", b, 16)
                    need(pe, "s_max", b, ST)
                if n == 1:
                    need(pe, "m_sb", b, 1)
                if n >= 2:
                    need(pe, "prob", b, n - 1)
                for j in range(4):
                    h = 2 * n + j // 2
                    last = mm(ring[:, (n + 1) % 2, j * L:(j + 1) * L], lhsT=k_rows[0:75, h, (j % 2) * P:(j % 2 + 1) * P],
                              rhs=q_rows[0:75, h, :], start=True, stop=True, skip_group_check=True)
                last.then_inc(S["st_ps"], 1)

            def values(b, n):
                if n == 0:
                    need(pe, "norm1", b, 1)
                need(pe, "prob", b, n + 1)
                for i in range(2):
                    for q in range(NT):
                        for k in range(NT):
                            last = mm(pv_ps[:, q, 2 * n + i, :], lhsT=prob[:, n % NPT, i, k, q * P:(q + 1) * P],
                                      rhs=vt[:, k, 2 * n + i, :], start=(k == 0), stop=(k == NT - 1), skip_group_check=True)
                last.then_inc(S["pv"], 1)

            def attn_out(b):
                need(pe, "o_sb", b, NT)
                need(pe, "prob", b, ST)
                for n in range(NT):
                    last = tr(ring[:, 1, n * P:(n + 1) * P], o_tok[:, n, :, :].rearrange("p h d -> p (h d)"), ident[:, :])
                last.then_inc(S["ot_ps"], 1)
                need(pe, "ot_sb", b, 1)
                mm(ring[:, 0, 0:L], lhsT=wout[:, :], rhs=o_t[:, :], start=True, stop=True,
                   skip_group_check=True).then_inc(S["y_ps"], 1)

            def router(b):
                need(pe, "h2", b, 1)
                for n in range(NT):
                    last = mm(ring[:, 1, n * E:(n + 1) * E], lhsT=ht[:, n * P:(n + 1) * P], rhs=wrout[:, :],
                              start=True, stop=True, skip_group_check=True)
                last.then_inc(S["lg_ps"], 1)

            def turn_scores(b):
                need(pe, "sp2", b, 1)
                need(pe, "sc", b, 1)
                need(pe, "ya", b, 1)
                for n in range(NT):
                    tr(ring[:, 0, n * P:(n + 1) * P], sc[:, n, :], ident[:, :])
                for n in range(NT):
                    last = tr(ring[:, 0, 512:1024].bitcast(BF16)[:, n * P:(n + 1) * P], sc_part[:, n, :], identb[:, :])
                last.then_inc(S["sct_ps"], 1)

            def broadcast(b, n):
                if n == 0:
                    need(pe, "sctb", b, 1)
                    need(pe, "lg", b, 1)
                if n == 1:
                    need(pe, "sctf", b, 1)
                if n >= 2:
                    need(pe, "bc", b, n - 1)
                for j in range(4):
                    last = mm(ring[:, (n + 1) % 2, j * L:(j + 1) * L], lhsT=sel[:, 4 * n + j, :], rhs=sctb[:, :],
                              start=True, stop=True, skip_group_check=True)
                last.then_inc(S["bc_ps"], 1)

            def gate_up(b, n):
                if n < 2:
                    need(pe, "bc", b, n + 3)
                else:
                    need(pe, "gc", b, n - 1)
                    need(pe, "upc", b, n - 1)
                for g in range(2):
                    for j in range(2):
                        o = ring[:, (n + 1) % 2, g * 512 + j * L:g * 512 + (j + 1) * L]
                        mm(o, lhsT=bias_rows[:, 2 * n + j, g, :], rhs=ones_b[:, :], start=True, stop=False, skip_group_check=True)
                        last = mm(o, lhsT=wgu[:, 2 * n + j, g, :], rhs=ht[:, :], start=False, stop=True, skip_group_check=True)
                last.then_inc(S["gu_ps"], 1)

            def down_bias(b):
                need(pe, "norm2", b, 1)
                need(pe, "sctf", b, 1)
                mm(pa[:, 0:L], lhsT=dbias[:, :], rhs=sct[:, :], start=True, stop=False, skip_group_check=True)

            def down_pair(b, n):
                need(pe, "act", b, n + 1)
                for j in range(2):
                    last = mm(pa[:, 0:L], lhsT=wdown[:, 2 * n + j, :], rhs=upc[:, n % 2, j * L:(j + 1) * L],
                              start=False, stop=(n == 7 and j == 1), skip_group_check=True)
                last.then_inc(S["dn"], 1)

            def phases(b, c):
                if c == 0:
                    need(pe, "h3", b, 1)
                    need(pe, "ksq", b, 0)
                    need(pe, "rsig", b, 0)
                    need(pe, "krel", b, 0)
                    need(pe, "rv", b, 0)
                    need(pe, "xo", b, 0)
                else:
                    need(pe, "turn", b, c)
                    need(pe, "frac", b, c)
                for j in range(2):
                    last = mm(pb_k[:, j * L:(j + 1) * L], lhsT=wk[:, (2 * c + j) * P:(2 * c + j + 1) * P], rhs=hb[:, 1:L + 1],
                              start=True, stop=True, skip_group_check=True)
                last.then_inc(S["k_ps"], 1)
                if c:
                    need(pe, "vpos", b, 2 * c)
                    need(pe, "vas", b, 2 * c)
                for j in range(2):
                    last = mm(pb_v[:, j * L:(j + 1) * L], lhsT=wv[:, (2 * c + j) * P:(2 * c + j + 1) * P], rhs=hb[:, 1:L + 1],
                              start=True, stop=True, skip_group_check=True)
                last.then_inc(S["v2_ps"], 1)

            def memory_wo(b, c):
                if c == 0:
                    need(pe, "norm3", b, 1)
                for m, s in ((0, "sum12"), (2, "sum34")):
                    need(pe, s, b, c + 1)
                    for j in range(2):
                        last = mm(pb[:, 0:L], lhsT=wo[:, 2 * c + j, :], rhs=prod[:, c % 2, m, j * L:(j + 1) * L],
                                  start=(c == 0 and m == 0 and j == 0), stop=(c == CC - 1 and m == 2 and j == 1),
                                  skip_group_check=True)
                last.then_inc(S["wo"], 1)

            def channel_mix(b):
                need(pe, "xr", b, 1)
                need(pe, "frac", b, CC)
                need(pe, "turn", b, CC)
                mm(pb_k[:, 0:L], lhsT=ffn_w[:, 0, :], rhs=xr[:, :], start=True, stop=True, skip_group_check=True)
                need(pe, "xk", b, 1)
                mm(pb_k[:, L:2 * L], lhsT=ffn_w[:, 1, :], rhs=xk[:, :], start=True, stop=True,
                   skip_group_check=True).then_inc(S["rk_ps"], 1)
                need(pe, "ksq", b, 1)
                need(pe, "vpos", b, 2 * CC)
                need(pe, "vas", b, 2 * CC)
                mm(pb_v[:, 0:L], lhsT=ffn_w[:, 2, :], rhs=ksq[:, :], start=True, stop=True,
                   skip_group_check=True).then_inc(S["vv_ps"], 1)
                need(pe, "x4", b, 1)
                for n in range(NT):
                    last = tr(pb_v[:, L + n * P:L + (n + 1) * P], x4[:, n * P:(n + 1) * P], ident[:, :])
                last.then_inc(S["xo_ps"], 1)

            def step(a, b):
                if a is not None:
                    turn_x(a)
                    stats(a, "1", xt[:, :], "xt", pa, (("y2", 0),), sq, rstd)
                    project(a)
                if b is not None:
                    stats(b, "3", xb[:, :], "mod_b", pb, (("norm4", 0),), sqb, rstdb)
                    phases(b, 0)
                if a is not None:
                    for n in range(ST):
                        scores(a, n)
                    turn_max(a)
                if b is not None:
                    phases(b, 1)
                    memory_wo(b, 0)
                if a is not None:
                    for n in range(ST):
                        scores_t(a, n)
                        if n:
                            values(a, n - 1)
                    values(a, ST - 1)
                if b is not None:
                    phases(b, 2)
                    memory_wo(b, 1)
                if a is not None:
                    attn_out(a)
                    stats(a, "2", x1[:, :], "x1", pa, (("den", 1), ("o_sb", NT)), sq, rstd)
                    router(a)
                if b is not None:
                    phases(b, 3)
                    memory_wo(b, 2)
                    memory_wo(b, 3)
                    stats(b, "4", x3[:, :], "x3", pb, (("yv", 1),), sqb, rstdb)
                if a is not None:
                    turn_scores(a)
                    for n in range(4):
                        broadcast(a, n)
                    down_bias(a)
                    for n in range(8):
                        gate_up(a, n)
                        if n:
                            down_pair(a, n - 1)
                    down_pair(a, 7)
                if b is not None:
                    channel_mix(b)

            run(pe, step)

        @block.scalar
        def _(act):
            af = nc.scalar.activation
            for n in range(2):
                for d in range(DH):
                    act.dma_start(bcol[d * H:(d + 1) * H, n:n + 1],
                                  bqkv[n * D:(n + 1) * D].rearrange("(h d) -> h d", d=DH)[:, d:d + 1], allow_slow_non_contiguous=True).then_inc(ld_small, 16)
            act.dma_start(bcol[:, 3:4], bout.rearrange("(k p) -> p k", p=P), allow_slow_non_contiguous=True).then_inc(ld_small, 16)
            act.dma_start(mu[:, 0:1], mu_r.rearrange("(k p) -> p k", p=P), allow_slow_non_contiguous=True).then_inc(ld_small, 16)
            act.dma_start(mu[:, 1:2], mu_k.rearrange("(k p) -> p k", p=P), allow_slow_non_contiguous=True).then_inc(ld_small, 16)
            act.dma_start(vbias[:, :], bqkv[2 * D:3 * D].rearrange("(a n) -> a n", a=1).to_broadcast([P, D])).then_inc(ld_small, 16)
            act.dma_start(rbias[:, :], router_b.rearrange("(a n) -> a n", a=1).to_broadcast([P, E])).then_inc(ld_small, 16)
            act.dma_start(fcol[:, :], freqs.rearrange("(k a) d -> (a d) k", a=2), allow_slow_non_contiguous=True).then_inc(ld_small, 16)
            for g in range(2):
                for a in range(2):
                    act.dma_start(gcol[64 * a:64 * (a + 1), g, :],
                                  gate[a:H:2, g:g + 1].rearrange("k a -> a k").to_broadcast([64, CT]), allow_slow_non_contiguous=True).then_inc(ld_small, 16)
            act.dma_start(bl[:, :, :], gub.rearrange("e (f g) -> e f g", g=2)).then_inc(ld_bias, 16)
            act.wait_ge(c_fill, 1)
            act.dma_start(dbias[0:E, :], downb).then_inc(ld_small, 16)
            act.dma_start(rel_in[1:P, 0, :], rel_emb[0:P - 1, :]).then_inc(ld_bias, 16)
            act.dma_start(rel_in[:, 1, :], rel_emb[P - 1:2 * P - 1, :]).then_inc(ld_bias, 16)
            act.wait_ge(ld_mod, 64)
            af(c_sig[:, :, :], c_in[:, :, :], ACT.Sigmoid).then_inc(c_act, 1)
            act.wait_ge(c_dve, DVE_TRIG)
            ang = prod[:, 0, :, :].rearrange("p a b -> p (a b)")
            tmp = prod[:, 1, :, :].rearrange("p a b -> p (a b)")
            af(sin_r[:, :, :].rearrange("p k t -> p (k t)"), ang, ACT.Sin).then_inc(c_act, 1)
            af(tmp, ang, ACT.Abs).then_inc(c_act, 1)
            act.wait_ge(c_act, 3)
            af(cos_r[:, :, :].rearrange("p k t -> p (k t)"), tmp, ACT.Sin, scale=-1.0, bias=half_pi[:, 0:1]).then_inc(c_act, 1)
            act.wait_ge(c_dve, DVE_SETUP)

            def square(b, n, c, s):
                need(act, "cent" + n, b, 1)
                af(s[:, :], c[:, :], ACT.Square).then_inc(S["sq" + n], 1)

            def modulate(b, n, src, dst, mod, k):
                need(act, "norm" + n, b, 1)
                af(dst, src[:, :], ACT.Identity, scale=mod[:, k + 1:k + 2], bias=mod[:, k:k + 1]).then_inc(S["h" + n], 1)

            def head(b):
                square(b, "1", cent, sq)
                need(act, "dn", b, 0)
                need(act, "mod_a", b, 1)
                modulate(b, "1", cent, ht[:, :], mod_a, 0)

            def part(b):
                need(act, "q_sb", b, 1)
                need(act, "k_sb", b, 1)
                need(act, "qk_rows", b, 0)
                af(qk_part[:, 0, :, :], qk[:, :, :], ACT.Copy).then_inc(S["part0"], 1)
                need(act, "rest0", b, 1)
                af(qk_part[:, 1, :, :], qk[:, :, :], ACT.Copy).then_inc(S["part1"], 1)

            def copy_max(b):
                need(act, "m_ps", b, 1)
                need(act, "m_rows", b, 0)
                af(m_sb[:, :], ring[0:3 * H, 0, :].bitcast(BF16)[:, 0:L], ACT.Copy).then_inc(S["m_sb"], 1)

            def exps(b, n):
                need(act, "st_ps", b, n + 1)
                if n < NPT:
                    need(act, "pv", b, 0)
                else:
                    need(act, "pv", b, n - NPT + 1)
                af(prob[:, n % NPT, :, :, :].rearrange("p i k q -> p (i k q)"), ring[:, (n + 1) % 2, :],
                   ACT.Exp).then_inc(S["prob"], 1)

            def attn_tail(b):
                need(act, "ot_ps", b, 1)
                need(act, "y_ps", b, 0)
                af(o_t[:, :], ring[:, 1, 0:L], ACT.Copy).then_inc(S["ot_sb"], 1)
                need(act, "y_ps", b, 1)
                need(act, "x1", b, 0)
                af(ya[:, :], ring[:, 0, 0:L], ACT.Identity, scale=mod_a[:, 2:3], bias=mod_a[:, 12:13]).then_inc(S["ya"], 1)
                square(b, "2", cent, sq)
                modulate(b, "2", cent, ht[:, :], mod_a, 3)

            def route(b):
                need(act, "shift", b, 1)
                need(act, "exm", b, 0)
                af(ex[:, :, :], lsh[:, :, :], ACT.Exp).then_inc(S["ex"], 1)
                need(act, "sct_ps", b, 1)
                need(act, "bc_ps", b, 0)
                af(sctb[:, :], ring[:, 0, 512:1024].bitcast(BF16)[:, 0:L], ACT.Copy).then_inc(S["sctb"], 1)
                need(act, "dn", b, 0)
                af(sct[:, :], ring[:, 0, 0:L], ACT.Copy).then_inc(S["sctf"], 1)
                for n in range(4):
                    need(act, "bc_ps", b, n + 1)
                    need(act, "gsc", b, 0)
                    af(sc_all[:, 4 * n:4 * n + 4, :].rearrange("p e t -> p (e t)"), ring[:, (n + 1) % 2, :],
                       ACT.Copy).then_inc(S["bc"], 1)

            def sigmoid(b, n):
                need(act, "gc", b, n + 1)
                need(act, "gl", b, n - 1)
                af(sig[:, n % 2, :], gsc[:, n % 2, :], ACT.Sigmoid, scale=ALPHA).then_inc(S["sig"], 1)

            def head_b(b):
                square(b, "3", centb, sqb)
                need(act, "dif", b, 0)
                need(act, "xr", b, 0)
                need(act, "xk", b, 0)
                modulate(b, "3", centb, hb[:, 1:L + 1], mod_b, 6)

            def phase(b, c):
                h = c % 2
                need(act, "k_ps", b, c + 1)
                need(act, "frac", b, c)
                af(turn[:, :], pb_k[:, :], ACT.Identity, bias=magic[:, 0:1]).then_inc(S["turn"], 1)
                need(act, "v2_ps", b, c + 1)
                need(act, "in1", b, c)
                need(act, "in2", b, c)
                for j in range(2):
                    af(vpos[:, j * L:(j + 1) * L], pb_v[:, j * L:(j + 1) * L], ACT.Copy,
                       scale=gcol[:, 0, 2 * c + j:2 * c + j + 1]).then_inc(S["vpos"], 1)
                need(act, "in3", b, c)
                need(act, "in4", b, c)
                for j in range(2):
                    af(vas[:, j * L:(j + 1) * L], pb_v[:, j * L:(j + 1) * L], ACT.Copy,
                       scale=gcol[:, 1, 2 * c + j:2 * c + j + 1]).then_inc(S["vas"], 1)
                need(act, "frac", b, c + 1)
                need(act, "pr4", b, c - 1)
                need(act, "in4", b, c - 1)
                af(sin_t[:, h, :, 1:L + 1], frac[:, h, :].rearrange("p (k t) -> p k t", k=2), ACT.Sin,
                   scale=-TWO_PI_IN).then_inc(S["sin"], 1)
                need(act, "cos", b, c)
                af(fabs[:, :], frac[:, h, :], ACT.Abs).then_inc(S["fabs"], 1)
                need(act, "fabs", b, c + 1)
                need(act, "pr3", b, c - 1)
                need(act, "in3", b, c - 1)
                af(cos_t[:, h, :, 1:L + 1], fabs[:, :].rearrange("p (k t) -> p k t", k=2), ACT.Sin,
                   scale=-TWO_PI_IN, bias=half_pi[:, 0:1]).then_inc(S["cos"], 1)

            def mix(b):
                square(b, "4", centb, sqb)
                modulate(b, "4", centb, hb[:, 1:L + 1], mod_b, 9)

            def mix_out(b):
                need(act, "rk_ps", b, 1)
                need(act, "rv", b, 0)
                af(rsig[:, :], pb_k[:, 0:L], ACT.Sigmoid).then_inc(S["rsig"], 1)
                need(act, "ksq", b, 0)
                af(ksq[:, :], pb_k[:, L:2 * L], ACT.Relu).then_inc(S["krel"], 1)
                need(act, "krel", b, 1)
                need(act, "vv_ps", b, 0)
                af(ksq[:, :], ksq[:, :], ACT.Square).then_inc(S["ksq"], 1)
                need(act, "xo_ps", b, 1)
                need(act, "out", b, 0)
                af(xo[:, :, :].rearrange("p n f -> p (n f)"), pb_v[:, L:2 * L], ACT.Copy).then_inc(S["xo"], 1)

            def step(a, b):
                if a is not None:
                    head(a)
                    part(a)
                if b is not None:
                    head_b(b)
                    phase(b, 0)
                    phase(b, 1)
                if a is not None:
                    copy_max(a)
                    for n in range(ST):
                        exps(a, n)
                if b is not None:
                    phase(b, 2)
                if a is not None:
                    attn_tail(a)
                if b is not None:
                    phase(b, 3)
                    mix(b)
                if a is not None:
                    route(a)
                    for n in range(8):
                        sigmoid(a, n)
                if b is not None:
                    mix_out(b)

            run(act, step)

        @block.vector
        def _(dve):
            tt = nc.vector.tensor_tensor
            ts = nc.vector.tensor_scalar
            stt = nc.vector.scalar_tensor_tensor
            count = [0]

            def done(ins, wait=True):
                count[0] += 1
                ins.then_inc(c_dve, 1)
                if wait:
                    dve.wait_ge(c_dve, count[0])

            dve.memset(mean_w[:, :], 1.0 / D)
            dve.memset(ones_b[:, :], 1.0)
            dve.memset(q_rows[64:75, :, :], 1.0)
            dve.memset(k_rows[64:75, :, :], 1.0)
            dve.memset(vt[:, :, :, DH:DH + 1], 1.0)
            dve.memset(lg[:, :, 0:TOPK], BIG)
            dve.memset(sc[:, :, :], 0.0)
            dve.memset(sc_part[:, :, :], 0.0)
            dve.memset(hb[:, 0:1], 0.0)
            dve.memset(sin_t[:, :, :, 0:1], 0.0)
            dve.memset(cos_t[:, :, :, 0:1], 0.0)
            dve.memset(keep[:, :], 1.0)
            dve.memset(half_pi[:, :], TWO_PI / 4)
            dve.memset(magic[:, :], MAGIC)
            dve.memset(rel_in[:, :, :], 0.0)
            dve.memset(mhalf[:, :], -0.5)
            dve.memset(mhalf_w[:, :], -0.5)
            dve.memset(dbias[:, :], 0.0).then_inc(c_fill, 1)
            dve.wait_ge(c_act, 1)
            done(tt(c_in[:, :, :], c_in[:, :, :], c_sig[:, :, :], ALU.mult))
            dve.wait_ge(c_pe, 1)
            done(nc.vector.tensor_copy(c_t[:, :, :].rearrange("p l b -> p (l b)"), pa[:, 0:2 * B]))
            dve.wait_ge(ld_bias, 48)
            done(nc.vector.tensor_copy(rel_rep[:, :, :, :], rel_in[:, :, :].rearrange("p n (d a) -> p n d a", a=1)
                                       .to_broadcast([P, NT, DH, H])))
            dve.memset(keep[:, 0:2 * L:L], 0.0)
            ang = prod[:, 0, :, :].rearrange("p a b -> p (a b)")
            tmp = prod[:, 1, :, :].rearrange("p a b -> p (a b)")
            dve.wait_ge(c_pool, 9)
            done(nc.vector.tensor_copy(t_f[:, :], t_int[:, :]))
            dve.wait_ge(ld_small, 16 * N_SMALL)
            for k in range(CT):
                last = ts(ang[:, k * L:(k + 1) * L], t_f[:, :], fcol[:, k:k + 1], None, ALU.mult)
            done(last)
            done(ts(tmp, ang, 1.0 / TWO_PI, MAGIC, ALU.mult, ALU.add))
            done(ts(tmp, tmp, MAGIC, None, ALU.subtract))
            for c in (C1, C2, C3):
                done(stt(out=ang, in0=tmp, scalar=-c, in1=ang, op0=ALU.mult, op1=ALU.add))
            done(ts(ang, ang, PI_IN, -PI_IN, ALU.min, ALU.max))
            assert count[0] == DVE_TRIG
            done(ts(t_next[:, :], t_f[:, :], 1.0, None, ALU.add))
            done(nc.vector.tensor_copy(bd[:, :, :], bl[:, :, :].rearrange("e f g -> e g f")))
            done(ts(bd[:, 1, :], bd[:, 1, :], 1.0, None, ALU.add))
            bdf = bd[:, :, :].rearrange("e g f -> e (g f)")
            nc.vector.tensor_copy(bp[:, 0, :], bdf).then_inc(c_split, 1)
            dve.wait_ge(c_split, 1)
            tt(brest[:, :], bdf, bp[:, 0, :], ALU.subtract).then_inc(c_split, 1)
            dve.wait_ge(c_split, 2)
            nc.vector.tensor_copy(bp[:, 1, :], brest[:, :]).then_inc(c_split, 1)
            dve.wait_ge(c_split, 3)
            tt(brest[:, :], brest[:, :], bp[:, 1, :], ALU.subtract).then_inc(c_split, 1)
            dve.wait_ge(c_split, 4)
            nc.vector.tensor_copy(bp[:, 2, :], brest[:, :]).then_inc(c_split, 1)
            dve.wait_ge(c_pe, 2)
            done(nc.vector.tensor_copy(mods[:, 0:12, :].rearrange("p k b -> p (k b)"), pa[:, 64:64 + 12 * B]))
            done(ts(mods[:, 1:12:3, :], mods[:, 1:12:3, :], 1.0, None, ALU.add))
            g4 = mods[:, 2:12:3, :]
            for l in range(2):
                g2 = mods[:, 6 * l + 2:6 * l + 6:3, :]
                done(ts(mod_abs[:, :, :], g2, -1.0, 0.25, ALU.mult, ALU.max))
                done(tt(mod_abs[:, :, :], mod_abs[:, :, :], g2, ALU.max))
                done(ts(mod_sgn[:, :, :], g2, 0.0, 2.0, ALU.is_ge, ALU.mult))
                done(stt(out=g2, in0=mod_sgn[:, :, :], scalar=1.0, in1=mod_abs[:, :, :], op0=ALU.subtract, op1=ALU.mult))
            done(ts(mods[:, 12, :], mods[:, 2, :], bcol[:, 3:4], None, ALU.mult))
            dve.wait_ge(c_pe, 4)
            done(nc.vector.tensor_copy(ffn_w[:, :, :].rearrange("p n c -> p (n c)"), pb_k[:, 0:3 * D]))
            done(nc.vector.tensor_copy(wqk[:, :, :, :], wqkv[:, 0:2 * D].rearrange("p (n h d) -> p n d h", n=2, d=DH)))
            done(ts(wk[:, :], wk[:, :], 10.0 / TWO_PI, None, ALU.mult))
            dve.wait_ge(c_act, 4)
            dve.wait_ge(c_pool, 12)
            dve.wait_ge(ld_rows, 48)
            done(ts(relb[:, :], pb_v[:, 0:L], bcol[:, 1:2], None, ALU.add))
            assert count[0] == DVE_SETUP, count[0]

            def centre(b, n, src, dst, ps):
                need(dve, "mean" + n, b, 1)
                other, same = {"1": ("h2", 0), "2": ("h1", 1), "3": ("h4", 0), "4": ("h3", 1)}[n]
                need(dve, other, b, same)
                tt(dst[:, :], src[:, :], ps[:, 0:L], ALU.subtract).then_inc(S["cent" + n], 1)

            def scale(b, n, c, v, ps):
                need(dve, "var" + n, b, 1)
                ts(v[:, :], ps[:, L:L + NT], EPS, None, ALU.add).then_inc(S["veps" + n], 1)
                need(dve, "rbc" + n, b, 1)
                tt(c[:, :], c[:, :], ps[:, L:2 * L], ALU.mult).then_inc(S["norm" + n], 1)

            def at_batch(t, b):
                return t[:, :, b:b + 1] if isinstance(b, int) else t[:, :, bass.ds(b, 1)]

            def head(b):
                need(dve, "xt_ps", b, 1)
                need(dve, "x1", b, 0)
                nc.vector.tensor_copy(xt[:, :], ring[:, 0, 0:L]).then_inc(S["xt"], 1)
                need(dve, "xt", b, 1)
                need(dve, "x2", b, 0)
                nc.vector.tensor_copy(mod_a[:, :].rearrange("p (k a) -> p k a", a=1), at_batch(mods, b)).then_inc(S["mod_a"], 1)
                centre(b, "1", xt, cent, pa)
                scale(b, "1", cent, veps, pa)

            def project(b):
                need(dve, "qk_ps", b, 1)
                need(dve, "part2", b, 0)
                ts(qk[:, 0, :], ring[:, 1, 0:L], bcol[:, 0:1], float(DH) ** -0.5, ALU.add, ALU.mult).then_inc(S["q_sb"], 1)
                tt(qk[:, 1, :], ring[:, 1, L:2 * L], relb[:, :], ALU.add).then_inc(S["k_sb"], 1)
                need(dve, "v_ps", b, 1)
                need(dve, "pv", b, 0)
                for n in range(NT):
                    tt(vt[:, n, :, 0:DH], ring[:, 1, 512 + n * D:512 + (n + 1) * D].rearrange("p (h d) -> p h d", d=DH),
                       vbias[:, :].rearrange("p (h d) -> p h d", d=DH), ALU.add).then_inc(S["v_sb"], 1)

            def maxima(b, n):
                need(dve, "s_ps", b, n + 1)
                nc.vector.tensor_reduce(smax[:, n // 4, 4 * (n % 4):4 * (n % 4) + 4],
                                        ring[:, n % 2, :].rearrange("p (h k) -> p h k", h=4), AX_X, ALU.max).then_inc(S["s_max"], 1)

            def split_max(b):
                need(dve, "s_max", b, ST)
                ts(negm[:, :, :], smax[:, :, :], -1.0, None, ALU.mult).then_inc(S["neg"], 1)
                need(dve, "neg", b, 1)
                nc.vector.tensor_copy(mpart[:, :, 0, :], negm[:, :, :]).then_inc(S["mp0"], 1)
                need(dve, "mp0", b, 1)
                tt(mrest[:, :, :], negm[:, :, :], mpart[:, :, 0, :], ALU.subtract).then_inc(S["mr0"], 1)
                need(dve, "mr0", b, 1)
                nc.vector.tensor_copy(mpart[:, :, 1, :], mrest[:, :, :]).then_inc(S["mp1"], 1)
                need(dve, "mp1", b, 1)
                tt(mpart[:, :, 2, :], mrest[:, :, :], mpart[:, :, 1, :], ALU.subtract).then_inc(S["mp2"], 1)

            def attn_norm(b):
                need(dve, "pv", b, ST)
                nc.vector.reciprocal(rden[:, :, :], pv_ps[:, :, :, DH]).then_inc(S["den"], 1)
                need(dve, "den", b, 1)
                need(dve, "ot_ps", b, 0)
                for n in range(NT):
                    tt(o_tok[:, n, :, :], pv_ps[:, n, :, 0:DH],
                       rden[:, n, :].rearrange("p (h a) -> p h a", a=1).to_broadcast([P, H, DH]), ALU.mult).then_inc(S["o_sb"], 1)

            def norm2(b):
                centre(b, "2", x1, cent, pa)
                scale(b, "2", cent, veps, pa)

            def route(b):
                need(dve, "lg_ps", b, 1)
                rb = rbias[:, :].rearrange("p (a e) -> p a e", a=1).to_broadcast([P, NT, E])
                tt(lg[:, :, TOPK:], ring[:, 1, 0:NT * E].rearrange("p (n e) -> p n e", e=E), rb, ALU.add).then_inc(S["lg"], 1)
                dve.wait_ge(c_dve, DVE_SETUP)
                need(dve, "lg", b, 1)
                for n in range(NT):
                    nc.vector.max(top8[:, n, :], lg[:, n, :]).then_inc(S["top8"], 1)
                need(dve, "top8", b, NT)
                tt(lsh[:, :, :], lg[:, :, TOPK:], top8[:, :, 4:5].to_broadcast([P, NT, E]), ALU.subtract).then_inc(S["shift"], 1)
                for n in range(NT):
                    nc.vector.match_replace(out=repl[:, n, :], in_to_replace=top8[:, n, :], in_values=lg[:, n, :],
                                            imm_value=-BIG).then_inc(S["repl"], 1)
                need(dve, "repl", b, NT)
                need(dve, "ex", b, 1)
                for n in range(NT):
                    stt(out=exm[:, n, :], in0=repl[:, n, TOPK:], scalar=-BIG, in1=ex[:, n, :], op0=ALU.is_equal,
                        op1=ALU.mult).then_inc(S["exm"], 1)
                need(dve, "exm", b, NT)
                nc.vector.tensor_reduce(esum[:, :], exm[:, :, :], AX_X, ALU.add).then_inc(S["esum"], 1)
                need(dve, "esum", b, 1)
                nc.vector.reciprocal(rsum[:, :], esum[:, :]).then_inc(S["rsum"], 1)
                need(dve, "rsum", b, 1)
                need(dve, "sct_ps", b, 0)
                tt(sc[:, :, 0:E], exm[:, :, :], rsum[:, :].rearrange("p (n a) -> p n a", a=1).to_broadcast([P, NT, E]),
                   ALU.mult).then_inc(S["sc"], 1)
                need(dve, "sc", b, 1)
                nc.vector.tensor_copy(sc_part[:, :, 0:E], sc[:, :, 0:E]).then_inc(S["sp0"], 1)
                need(dve, "sp0", b, 1)
                tt(srest[:, :, :], sc[:, :, 0:E], sc_part[:, :, 0:E], ALU.subtract).then_inc(S["sr0"], 1)
                need(dve, "sr0", b, 1)
                nc.vector.tensor_copy(sc_part[:, :, E:2 * E], srest[:, :, :]).then_inc(S["sp1"], 1)
                need(dve, "sp1", b, 1)
                tt(sc_part[:, :, 2 * E:3 * E], srest[:, :, :], sc_part[:, :, E:2 * E], ALU.subtract).then_inc(S["sp2"], 1)

            def expert_pair(b, n):
                need(dve, "gu_ps", b, n + 1)
                need(dve, "act", b, n - 1)
                ts(gsc[:, n % 2, :], ring[:, (n + 1) % 2, 0:512], LIMIT, None, ALU.min).then_inc(S["gc"], 1)
                need(dve, "dn", b, n - 1)
                ts(upc[:, n % 2, :], ring[:, (n + 1) % 2, 512:1024], LIMIT + 1.0, 1.0 - LIMIT, ALU.min,
                   ALU.max).then_inc(S["upc"], 1)

            def experts_out(b):
                need(dve, "dn", b, 8)
                ts(ya[:, :], pa[:, 0:L], mod_a[:, 5:6], None, ALU.mult).then_inc(S["y2"], 1)
                need(dve, "y2", b, 1)
                need(dve, "mod_b", b, 0)
                tt(x2[:, :], x1[:, :], ya[:, :], ALU.add).then_inc(S["x2"], 1)

            def head_b(b):
                need(dve, "x2", b, 1)
                nc.vector.tensor_copy(mod_b[:, :].rearrange("p (k a) -> p k a", a=1), at_batch(mods, b))
                nc.vector.tensor_copy(xb[:, :], x2[:, :]).then_inc(S["mod_b"], 1)
                need(dve, "mod_b", b, 1)
                centre(b, "3", xb, centb, pb)
                scale(b, "3", centb, vepsb, pb)

            def memory_a(b, c):
                h = c % 2
                need(dve, "turn", b, c + 1)
                need(dve, "fabs", b, c - 1)
                stt(out=frac[:, h, :], in0=turn[:, :], scalar=MAGIC, in1=pb_k[:, :], op0=ALU.subtract,
                    op1=ALU.subtract).then_inc(S["frac"], 1)

            def memory_b(b, c):
                h = c % 2
                need(dve, "wo", b, c - 1)
                for n, s in ((0, "cu1"), (1, "cu2")):
                    need(dve, "in" + str(n + 1), b, c + 1)
                    nc.vector.tensor_tensor_scan(prod[:, h, n, :], keep[:, :], prod[:, h, n, :], 0.0, ALU.mult,
                                                 ALU.add).then_inc(S[s], 1)
                need(dve, "vas", b, 2 * c + 2)
                v = vas[:, :].rearrange("p (k t) -> p k t", k=2)
                need(dve, "cos", b, c + 1)
                for n, t in ((2, cos_t), (3, sin_t)):
                    tt(prod[:, h, n, :].rearrange("p (k t) -> p k t", k=2), v, t[:, h, :, 0:L], ALU.mult).then_inc(S["in" + str(n + 1)], 1)
                for n in (2, 3):
                    need(dve, "in" + str(n + 1), b, c + 1)
                    nc.vector.tensor_tensor_scan(prod[:, h, n, :], keep[:, :], prod[:, h, n, :], 0.0, ALU.mult,
                                                 ALU.add).then_inc(S["cu" + str(n + 1)], 1)
                for n, t in ((2, cos_t), (3, sin_t)):
                    need(dve, "cu" + str(n + 1), b, c + 1)
                    cv = prod[:, h, n, :].rearrange("p (k t) -> p k t", k=2)
                    tt(cv, cv, t[:, h, :, 1:L + 1], ALU.mult).then_inc(S["pr" + str(n + 1)], 1)
                need(dve, "pr3", b, c + 1)
                need(dve, "pr4", b, c + 1)
                tt(prod[:, h, 2, :], prod[:, h, 2, :], prod[:, h, 3, :], ALU.add).then_inc(S["sum34"], 1)

            def memory_end(b):
                need(dve, "wo", b, CC)
                stt(out=dif[:, :], in0=pb[:, 0:L], scalar=mod_b[:, 8:9], in1=inv_s[:, :], op0=ALU.mult,
                    op1=ALU.mult).then_inc(S["yv"], 1)
                need(dve, "yv", b, 1)
                tt(x3[:, :], xb[:, :], dif[:, :], ALU.add).then_inc(S["x3"], 1)

            def mix(b):
                centre(b, "4", x3, centb, pb)
                scale(b, "4", centb, vepsb, pb)

            def mix_in(b):
                need(dve, "h4", b, 1)
                tt(dif[:, :], hb[:, 1:L + 1], hb[:, 0:L], ALU.subtract).then_inc(S["dif"], 1)
                need(dve, "dif", b, 1)
                need(dve, "rk_ps", b, 0)
                stt(out=xr[:, :], in0=dif[:, :], scalar=mu[:, 0:1], in1=hb[:, 0:L], op0=ALU.mult, op1=ALU.add).then_inc(S["xr"], 1)
                stt(out=xk[:, :], in0=dif[:, :], scalar=mu[:, 1:2], in1=hb[:, 0:L], op0=ALU.mult, op1=ALU.add).then_inc(S["xk"], 1)

            def mix_out(b):
                need(dve, "vv_ps", b, 1)
                need(dve, "rsig", b, 1)
                stt(out=xr[:, :], in0=pb_v[:, 0:L], scalar=mod_b[:, 11:12], in1=rsig[:, :], op0=ALU.mult,
                    op1=ALU.mult).then_inc(S["rv"], 1)
                need(dve, "rv", b, 1)
                need(dve, "xo_ps", b, 0)
                tt(x4[:, :], x3[:, :], xr[:, :], ALU.add).then_inc(S["x4"], 1)

            def step(a, b):
                if a is not None:
                    head(a)
                    project(a)
                if b is not None:
                    head_b(b)
                    memory_a(b, 0)
                if a is not None:
                    for n in range(ST):
                        maxima(a, n)
                    split_max(a)
                if b is not None:
                    memory_a(b, 1)
                    memory_b(b, 0)
                    memory_b(b, 1)
                    memory_a(b, 2)
                if a is not None:
                    attn_norm(a)
                    norm2(a)
                if b is not None:
                    memory_a(b, 3)
                    memory_b(b, 2)
                    memory_b(b, 3)
                    memory_end(b)
                    mix(b)
                if a is not None:
                    route(a)
                    for n in range(8):
                        expert_pair(a, n)
                    experts_out(a)
                if b is not None:
                    mix_in(b)
                    mix_out(b)

            run(dve, step)


DVE_TRIG = 11
DVE_SETUP = 29


def run(eng, step):
    step(0, None)
    step(1, 0)
    with eng.Fori(2, B) as a:
        step(a, a - 1)
    step(None, B - 1)


_INS = ['L0_attn_x', 'L0_attn_Wqkv', 'L0_attn_bqkv', 'L0_attn_Wout', 'L0_attn_bout', 'L0_attn_rel_emb',
        'L0_ffn_router_w', 'L0_ffn_router_b', 'L0_ffn_gate_up_proj', 'L0_ffn_gate_up_bias', 'L0_ffn_down_proj',
        'L0_ffn_down_bias', 'L0_c', 'L0_wmod', 'L1_attn_Wk', 'L1_attn_Wv', 'L1_attn_Wo', 'L1_attn_gate',
        'L1_attn_freqs', 'L1_ffn_W_r', 'L1_ffn_W_k', 'L1_ffn_W_v', 'L1_ffn_mu_r', 'L1_ffn_mu_k', 'L1_c', 'L1_wmod']


def kernel(**inputs):
    import numpy as _np
    import concourse.bacc as _bacc
    from concourse import mybir as _mybir
    from concourse.bass_utils import run_bass_kernel_spmd as _run

    nc = _bacc.Bacc("TRN2", target_bir_lowering=False, num_devices=1)
    arrays, args = {}, []
    for name in _INS:
        a = _np.ascontiguousarray(inputs[name])
        arrays[f"in_{name}_dram"] = a
        args.append(nc.dram_tensor(f"in_{name}_dram", a.shape, _mybir.dt.from_np(a.dtype), kind="ExternalInput").ap())
    args.append(nc.dram_tensor("out_dram", (B, L, D), _mybir.dt.float32, kind="ExternalOutput").ap())
    build(nc, *args)
    r = _run(nc, [arrays], core_ids=[0])
    return r.results[0]["out_dram"]
```

```python
from contextlib import ExitStack

import concourse.bass as bass
from concourse import mybir

F32 = mybir.dt.float32
BF16 = mybir.dt.bfloat16
I32 = mybir.dt.int32
ALU = mybir.AluOpType
ACT = mybir.ActivationFunctionType
AX_X = mybir.AxisListType.X

P = 128
B = 16
L = 256
D = 128
NT = L // P
H = 16
DH = D // H
E = 16
TOPK = 4
HD = 1024
CT = HD // P
CC = 4
ST = 8
VW = 32
NPT = 3
EPS = 1e-5
ALPHA, LIMIT = 1.702, 7.0
TWO_PI = 6.283185307179586
TWO_PI_IN = 6.283185
PI_IN = 3.1415925
MAGIC = 12582912.0
C1, C2, C3 = 6.28125, 0.0019350051879882812, 3.0199159819567e-07
BIG = 3.0e38

PER = dict(
    x_in=16, xt_ps=1, xt=1, mean1=1, cent1=1, sq1=1, var1=1, veps1=1, rstd1=1, rbc1=1, norm1=1, h1=1,
    qk_ps=1, v_ps=1, q_sb=1, k_sb=1, v_sb=NT, part0=1, rest0=1, part1=1, part2=1, qk_rows=16 * 18,
    s_ps=ST, s_max=ST, neg=1, mp0=1, mr0=1, mp1=1, mp2=1, m_ps=1, m_sb=1, m_rows=16,
    st_ps=ST, prob=ST, pv=ST, o_raw=2, or_ps=1, den=1, o_sb=NT, ot_ps=1, ot_sb=1, y_ps=1, ya=1, x1=1,
    mean2=1, cent2=1, sq2=1, var2=1, veps2=1, rstd2=1, rbc2=1, norm2=1, h2=1,
    lg_ps=1, lg=1, top8=NT, shift=1, repl=NT, ex=1, exm=NT, esum=1, rsum=1, sc=1,
    sp0=1, sr0=1, sp1=1, sp2=1, sct_ps=1, sctf=1, sctb=1, bc_ps=4, bc=4,
    gu_ps=8, gc=16, upr=16, sig=8, gsc=8, upc=8, gl=8, act=8, dn=8, y2=1, x2=1, mod_a=1, mod_h=1,
    mod_b=1, mean3=1, cent3=1, sq3=1, var3=1, veps3=1, rstd3=1, rbc3=1, norm3=1, h3=1,
    k_ps=CC, v2_ps=CC, turn=CC, frac=CC, sin=CC, fabs=CC, cos=CC, vpos=2 * CC, vas=2 * CC,
    in1=CC, in2=CC, in3=CC, in4=CC, cu1=CC, cu2=CC, cu3=CC, cu4=CC,
    pr1=CC, pr2=CC, pr3=CC, pr4=CC, sum12=CC, sum34=CC, wo=CC, yv=1, x3=1,
    mean4=1, cent4=1, sq4=1, var4=1, veps4=1, rstd4=1, rbc4=1, norm4=1, h4=1,
    dif=1, xr=1, xk=1, rk_ps=1, rsig=1, krel=1, ksq=1, vv_ps=1, rv=1, x4=1, xo_ps=1, xo=1, out=16,
)


def build(nc, x, Wqkv, bqkv, Wout, bout, rel_emb, router_w, router_b, gup, gub, down, downb, c0, wmod0,
          Wk, Wv, Wo, gate, freqs, W_r, W_k, W_v, mu_r, mu_k, c1, wmod1, out):
    with ExitStack() as ctx:
        def sb(name, shape, dt=F32):
            return ctx.enter_context(nc.sbuf_tensor(name, shape, dt))

        wqkv = sb("wqkv", [P, 3 * D])
        wout = sb("wout", [P, D])
        wgu = sb("wgu", [P, E, 2, D])
        wdown = sb("wdown", [P, E, D])
        wrout = sb("wrout", [P, E])
        wk = sb("wk", [P, HD])
        wv = sb("wv", [P, HD])
        wo = sb("wo", [P, CT, D])
        ffn_w = sb("ffn_w", [P, 3, D])
        ident = sb("ident", [P, P])
        identb = sb("identb", [P, P], BF16)
        mean_w = sb("mean_w", [P, P])
        bcol = sb("bcol", [P, 4])
        mu = sb("mu", [P, 2])
        vbias = sb("vbias", [P, D])
        rbias = sb("rbias", [P, E])
        rel_in = sb("rel_in", [P, NT, DH])
        rel_rep = sb("rel_rep", [P, NT, DH, H])
        wqk = sb("wqk", [P, 2, DH, H])
        relb = sb("relb", [P, L])
        c_in = sb("c_in", [B, 2, D])
        c_sig = sb("c_sig", [B, 2, D])
        c_t = sb("c_t", [P, 2, B])
        mods = sb("mods", [P, 13, B])
        mod_abs = sb("mod_abs", [P, 2, B])
        mod_sgn = sb("mod_sgn", [P, 2, B])
        sel = sb("sel", [P, E, P], BF16)
        gub_t = sb("gub_t", [P, 2, E])
        dbias = sb("dbias", [P, D])
        t_int = sb("t_int", [P, L], I32)
        t_f = sb("t_f", [P, L])
        inv_s = sb("inv_s", [P, L])
        mhalf = sb("mhalf", [P, NT])
        veps = sb("veps", [P, NT])
        rstd = sb("rstd", [P, NT])
        vepsb = sb("vepsb", [P, NT])
        rstdb = sb("rstdb", [P, NT])
        fcol = sb("fcol", [P, CT])
        gcol = sb("gcol", [P, 2, CT])
        cos_r = sb("cos_r", [P, CT, L])
        sin_r = sb("sin_r", [P, CT, L])
        keep = sb("keep", [P, 2 * L])
        half_pi = sb("half_pi", [P, 1])
        magic = sb("magic", [P, 1])

        x_in = sb("x_in", [P, NT, D])
        xt = sb("xt", [P, L])
        cent = sb("cent", [P, L])
        sq = sb("sq", [P, L])
        ht = sb("ht", [P, L])
        mod_a = sb("mod_a", [P, 13])
        qk = sb("qk", [P, 2, L])
        qk_part = sb("qk_part", [P, 3, 2, L], BF16)
        hta = sb("hta", [P, L])
        mod_h = sb("mod_h", [P, 13])
        vt = sb("vt", [P, NT, H, VW])
        o_raw = sb("o_raw", [P, H // 4, L])
        q_rows = sb("q_rows", [75, H, L], BF16)
        k_rows = sb("k_rows", [75, H, L], BF16)
        smax = sb("smax", [P, NT, H])
        negm = sb("negm", [P, NT, H])
        mrest = sb("mrest", [P, NT, H])
        mpart = sb("mpart", [P, NT, 3, H], BF16)
        m_sb = sb("m_sb", [3 * H, L], BF16)
        prob = sb("prob", [P, NPT, 4, L])
        rden = sb("rden", [P, NT, H])
        o_tok = sb("o_tok", [P, NT, H, DH])
        o_t = sb("o_t", [P, L])
        ya = sb("ya", [P, L])
        x1 = sb("x1", [P, L])
        lg = sb("lg", [P, NT, TOPK + E])
        top8 = sb("top8", [P, NT, 8])
        repl = sb("repl", [P, NT, TOPK + E])
        lsh = sb("lsh", [P, NT, E])
        ex = sb("ex", [P, NT, E])
        exm = sb("exm", [P, NT, E])
        esum = sb("esum", [P, NT])
        rsum = sb("rsum", [P, NT])
        sc = sb("sc", [P, NT, P])
        srest = sb("srest", [P, NT, E])
        sc_part = sb("sc_part", [P, NT, P], BF16)
        sct = sb("sct", [P, L])
        sctb = sb("sctb", [P, L], BF16)
        sc_all = sb("sc_all", [P, E, L])
        sig = sb("sig", [P, 2, 2 * L])
        gsc = sb("gsc", [P, 2, 2 * L])
        upc = sb("upc", [P, 2, 2 * L])
        x2 = sb("x2", [P, L])

        wmod = prob[:, :, :, :].rearrange("p s i q -> p (s i q)")[:, 0:12 * D].rearrange("p (l n) -> p l n", l=2)
        ffn_raw = sig[:, 0, 0:3 * D].rearrange("p (n c) -> p n c", n=3)
        bl = gsc[0:E, 0, 0:2 * D].rearrange("e (f g) -> e f g", g=2)
        bd = gsc[0:E, 0, 2 * D:4 * D].rearrange("e (g f) -> e g f", g=2)
        t_next = cent
        mhalf_w = sq

        mod_b = sb("mod_b", [P, 13])
        centb = sb("centb", [P, L])
        sqb = sb("sqb", [P, L])
        hb = sb("hb", [P, L + 1])
        xb = sb("xb", [P, L])
        turn = sb("turn", [P, 2 * L])
        frac = sb("frac", [P, 2, 2 * L])
        fabs = sb("fabs", [P, 2 * L])
        sin_t = sb("sin_t", [P, 2, 2, L + 1])
        cos_t = sb("cos_t", [P, 2, 2, L + 1])
        vpos = sb("vpos", [P, 2 * L])
        vas = sb("vas", [P, 2 * L])
        prod = sb("prod", [P, 2, 4, 2 * L])
        x3 = sb("x3", [P, L])
        dif = sb("dif", [P, L])
        xr = sb("xr", [P, L])
        xk = sb("xk", [P, L])
        rsig = sb("rsig", [P, L])
        ksq = sb("ksq", [P, L])
        x4 = sb("x4", [P, L])
        xo = sb("xo", [P, NT, D])

        ring = ctx.enter_context(nc.psum_tensor("ring", [P, 2, 1024], F32))
        pa = ctx.enter_context(nc.psum_tensor("pa", [P, 512], F32))
        pb_k = ctx.enter_context(nc.psum_tensor("pb_k", [P, 512], F32))
        pb_v = ctx.enter_context(nc.psum_tensor("pb_v", [P, 512], F32))
        pb = ctx.enter_context(nc.psum_tensor("pb", [P, 512], F32))
        o_ps = ring[:, 1, :].rearrange("p (n h d) -> p n h d", n=NT, h=H)

        S = {name: ctx.enter_context(nc.semaphore(name)) for name in PER}

        def setup_sem(name):
            return ctx.enter_context(nc.semaphore("set_" + name))

        ld_w, ld_mod, ld_gu, ld_bias, ld_small = (
            setup_sem(n) for n in ("ld_w", "ld_mod", "ld_gu", "ld_bias", "ld_small"))
        c_pool, c_act, c_pe, c_dve, c_fill = (
            setup_sem(n) for n in ("pool", "act", "pe", "dve", "fill"))
        N_W, N_SMALL = 9, 27

        def need(eng, name, b, k):
            v = b * PER[name] + k
            if not isinstance(v, int) or v > 0:
                eng.wait_ge(S[name], v)

        block = ctx.enter_context(nc.Block())

        @block.sync
        def _(sp):
            sp.dma_start(c_in[:, 0, :], c0).then_inc(ld_mod, 16)
            sp.dma_start(c_in[:, 1, :], c1).then_inc(ld_mod, 16)
            sp.dma_start(wmod[:, 0, :], wmod0).then_inc(ld_mod, 16)
            sp.dma_start(wmod[:, 1, :], wmod1).then_inc(ld_mod, 16)
            sp.dma_start(wqkv[:, :], Wqkv).then_inc(ld_w, 16)
            sp.dma_start(wout[:, :], Wout).then_inc(ld_w, 16)
            sp.dma_start(wrout[:, :], router_w).then_inc(ld_w, 16)
            sp.dma_start(wk[:, :], Wk).then_inc(ld_w, 16)
            sp.dma_start(wv[:, :], Wv).then_inc(ld_w, 16)
            sp.dma_start(wo[:, :, :], Wo.rearrange("(k p) m -> p k m", p=P)).then_inc(ld_w, 16)
            for n, w in enumerate((W_r, W_k, W_v)):
                sp.dma_start(ffn_raw[:, n, :], w).then_inc(ld_w, 16)
            sp.dma_start(sc_all[:, :, :], gup.rearrange("e h f -> h e f")).then_inc(ld_gu, 16)
            sp.dma_start(wdown[:, :, :], down.rearrange("e i h -> i e h")).then_inc(ld_gu, 16)
            def load_x(b):
                sp.wait_ge(ld_gu, 32)
                need(sp, "xt_ps", b, 0)
                src = x[bass.ds(b, 1)] if not isinstance(b, int) else x[b:b + 1]
                sp.dma_start(x_in[:, :, :], src.rearrange("a (n p) f -> p (a n) f", p=P)).then_inc(S["x_in"], 16)

            def spread(b):
                sp.wait_ge(ld_gu, 32)
                need(sp, "part2", b, 1)
                need(sp, "den", b, 0)
                for a in range(3):
                    for c in range(3):
                        r = (a * 3 + c) * DH
                        for rows, n, m in ((q_rows, 0, a), (k_rows, 1, c)):
                            sp.dma_start(rows[r:r + DH, :, :],
                                         qk_part[:, m, n, :]).then_inc(S["qk_rows"], 16)

            def spread_max(b):
                need(sp, "m_sb", b, 1)
                sp.dma_start(q_rows[72:75, :, :], m_sb[:, :]).then_inc(S["m_rows"], 16)

            def store(b):
                sp.wait_ge(ld_gu, 32)
                need(sp, "xo", b, 1)
                dst = out[bass.ds(b, 1)] if not isinstance(b, int) else out[b:b + 1]
                sp.dma_start(dst.rearrange("a (n p) f -> p (a n) f", p=P), xo[:, :, :]).then_inc(S["out"], 16)

            def head(nx):
                load_x(nx)
                spread(nx)

            def step(a, b, nx):
                if a is not None:
                    spread_max(a)
                if b is not None:
                    store(b)
                if nx is not None:
                    head(nx)

            run(sp, head, step)
            sp.wait_ge(S["out"], 16 * B)

        @block.gpsimd
        def _(pool):
            for t in (ident, identb, sel):
                pool.memset(t[tuple(slice(None) for _ in t.shape)], 0.0).then_inc(c_pool, 1)
            pool.wait_ge(c_pool, 3)
            for t in (ident, identb):
                pool.affine_select(out=t[:, :], in_=t[:, :], compare_op=ALU.not_equal, fill=1.0, base=0,
                                   pattern=[[-1, P]], channel_multiplier=1).then_inc(c_pool, 1)
            for n in range(3):
                pool.wait_ge(c_pool, 5 + n)
                pool.affine_select(out=sel[:, :, :], in_=sel[:, :, :], compare_op=ALU.not_equal, fill=1.0,
                                   base=-16 * n, pattern=[[-1, E], [0, P]], channel_multiplier=1).then_inc(c_pool, 1)
            pool.iota(t_int[:, :], pattern=[[1, L]], base=0, channel_multiplier=0).then_inc(c_pool, 1)
            pool.wait_ge(ld_gu, 32)
            pool.tensor_copy(wgu[:, :, 0, :], sc_all[:, :, 0:L:2]).then_inc(c_pool, 1)
            pool.tensor_copy(wgu[:, :, 1, :], sc_all[:, :, 1:L:2]).then_inc(c_pool, 1)

            pool.wait_ge(c_dve, DVE_TRIG + 1)
            pool.tensor_tensor(inv_s[:, :], t_next[:, :], mhalf_w[:, :], ALU.pow).then_inc(c_pool, 1)

            def deviation(b, n, v, r):
                need(pool, "veps" + n, b, 1)
                pool.tensor_tensor(r[:, :], v[:, :], mhalf[:, 0:NT], ALU.pow).then_inc(S["rstd" + n], 1)

            def rest_q(b):
                need(pool, "part0", b, 1)
                need(pool, "q_sb", b, 1)
                need(pool, "k_sb", b, 1)
                pool.tensor_tensor(qk[:, :, :], qk[:, :, :], qk_part[:, 0, :, :], ALU.subtract).then_inc(S["rest0"], 1)
                need(pool, "part1", b, 1)
                need(pool, "rest0", b, 1)
                pool.tensor_tensor(qk_part[:, 2, :, :], qk[:, :, :], qk_part[:, 1, :, :], ALU.subtract).then_inc(S["part2"], 1)

            def residual1(b):
                need(pool, "ya", b, 1)
                need(pool, "xt", b, 1)
                need(pool, "x2", b, 0)
                pool.tensor_tensor(x1[:, :], xt[:, :], ya[:, :], ALU.add).then_inc(S["x1"], 1)

            def expert_pair(b, n):
                sca = sc_all[:, 2 * n:2 * n + 2, :].rearrange("p e t -> p (e t)")
                if n % 2 == 0:
                    need(pool, "bc", b, n // 2 + 1)
                need(pool, "sig", b, n + 1)
                pool.tensor_tensor(gsc[:, n % 2, :], gsc[:, n % 2, :], sca, ALU.mult).then_inc(S["gsc"], 1)
                if n:
                    expert_last(b, n - 1)

            def expert_last(b, n):
                need(pool, "upc", b, n + 1)
                need(pool, "gl", b, n + 1)
                pool.tensor_tensor(upc[:, n % 2, :], upc[:, n % 2, :], gsc[:, n % 2, :], ALU.mult).then_inc(S["act"], 1)

            def memory_in(b, c):
                h = c % 2
                need(pool, "vpos", b, 2 * c + 2)
                need(pool, "wo", b, c - 1)
                pool.tensor_tensor(prod[:, h, 0, :], vpos[:, :],
                                   cos_r[:, 2 * c:2 * c + 2, :].rearrange("p k t -> p (k t)"), ALU.mult).then_inc(S["in1"], 1)
                pool.tensor_tensor(prod[:, h, 1, :], vpos[:, :],
                                   sin_r[:, 2 * c:2 * c + 2, :].rearrange("p k t -> p (k t)"), ALU.mult).then_inc(S["in2"], 1)

            def memory_out(b, c):
                h = c % 2
                for n, t in ((0, cos_r), (1, sin_r)):
                    need(pool, "cu" + str(n + 1), b, c + 1)
                    pool.tensor_tensor(prod[:, h, n, :], prod[:, h, n, :],
                                       t[:, 2 * c:2 * c + 2, :].rearrange("p k t -> p (k t)"), ALU.mult).then_inc(S["pr" + str(n + 1)], 1)
                need(pool, "pr1", b, c + 1)
                need(pool, "pr2", b, c + 1)
                pool.tensor_tensor(prod[:, h, 0, :], prod[:, h, 0, :], prod[:, h, 1, :], ALU.add).then_inc(S["sum12"], 1)

            def head_1(nx):
                deviation(nx, "1", veps, rstd)

            def head(nx):
                head_1(nx)
                rest_q(nx)

            def step(a, b, nx):
                if b is not None:
                    deviation(b, "3", vepsb, rstdb)
                    memory_in(b, 0)
                    memory_in(b, 1)
                    memory_out(b, 0)
                    memory_out(b, 1)
                    memory_in(b, 2)
                    memory_out(b, 2)
                    memory_in(b, 3)
                if a is not None:
                    residual1(a)
                    deviation(a, "2", veps, rstd)
                if b is not None:
                    memory_out(b, 3)
                    deviation(b, "4", vepsb, rstdb)
                if a is not None:
                    for n in range(3):
                        expert_pair(a, n)
                if nx is not None:
                    head_1(nx)
                if a is not None:
                    for n in range(3, 7):
                        expert_pair(a, n)
                if nx is not None:
                    rest_q(nx)
                if a is not None:
                    expert_pair(a, 7)
                    expert_last(a, 7)

            run(pool, head, step)

        @block.tensor
        def _(pe):
            mm = nc.tensor.matmul
            tr = nc.tensor.transpose
            pe.wait_ge(c_pool, 5)
            pe.wait_ge(c_dve, 1)
            for l in range(2):
                last = tr(pa[:, l * B:(l + 1) * B], c_in[:, l, :], ident[0:B, 0:B])
            last.then_inc(c_pe, 1)
            pe.wait_ge(c_dve, 2)
            for l in range(2):
                for k in range(6):
                    last = mm(pa[:, 64 + (l * 6 + k) * B:64 + (l * 6 + k + 1) * B], lhsT=wmod[:, l, k * D:(k + 1) * D],
                              rhs=c_t[:, l, :], start=True, stop=True, skip_group_check=True)
            last.then_inc(c_pe, 1)
            pe.wait_ge(ld_w, 16 * N_W)
            for n in range(3):
                last = tr(pb_k[:, n * D:(n + 1) * D], ffn_raw[:, n, :], ident[:, :])
            last.then_inc(c_pe, 1)
            pe.wait_ge(c_dve, 3)
            for n in range(NT):
                last = tr(pb_v[:, n * P:(n + 1) * P], rel_rep[:, n, :, :].rearrange("p d h -> p (d h)"), ident[:, :])
            last.then_inc(c_pe, 1)
            pe.wait_ge(c_dve, DVE_BIAS)
            for g in range(2):
                last = tr(pb[:, 448 + g * E:448 + (g + 1) * E], bd[:, g, :], ident[0:E, 0:E])
            last.then_inc(c_pe, 1)
            pe.wait_ge(c_dve, DVE_SETUP)

            def mean(b, n, src, src_sem, ps, free):
                need(pe, src_sem, b, 1)
                for name, c, k in free:
                    need(pe, name, c, k)
                mm(ps[:, 0:L], lhsT=mean_w[:, :], rhs=src, start=True, stop=True,
                   skip_group_check=True).then_inc(S["mean" + n], 1)

            def variance(b, n, ps, sqt):
                need(pe, "sq" + n, b, 1)
                for t in range(NT):
                    last = mm(ps[:, L + t:L + t + 1], lhsT=sqt[:, t * P:(t + 1) * P], rhs=mean_w[:, 0:1], start=True,
                              stop=True, skip_group_check=True)
                last.then_inc(S["var" + n], 1)

            def deviation(b, n, ps, rs):
                need(pe, "rstd" + n, b, 1)
                for t in range(NT):
                    last = mm(ps[:, L + t * P:L + (t + 1) * P], lhsT=rs[:, t:t + 1].to_broadcast([P, P]), rhs=ident[:, :],
                              start=True, stop=True, skip_group_check=True)
                last.then_inc(S["rbc" + n], 1)

            def head_1(nx):
                need(pe, "x_in", nx, 16)
                need(pe, "rsig", nx - 1, 0)
                need(pe, "ksq", nx - 1, 0)
                for n in range(NT):
                    last = tr(pb_k[:, n * P:(n + 1) * P], x_in[:, n, :], ident[:, :])
                last.then_inc(S["xt_ps"], 1)

            def head_2(nx):
                mean(nx, "1", xt[:, :], "xt", pb, (("norm4", nx - 1, 0),))

            def head_3(nx):
                variance(nx, "1", pb, sq)

            def head_4(nx):
                deviation(nx, "1", pb, rstd)

            def head_5(nx):
                need(pe, "h1", nx, 1)
                need(pe, "xo", nx - 1, 0)
                for n in range(2):
                    last = mm(pb_k[:, n * L:(n + 1) * L], lhsT=wqk[:, n, :, :].rearrange("p d h -> p (d h)"), rhs=hta[:, :],
                              start=True, stop=True, skip_group_check=True)
                last.then_inc(S["qk_ps"], 1)
                for n in range(NT):
                    last = mm(pb_v[:, n * D:(n + 1) * D], lhsT=hta[:, n * P:(n + 1) * P],
                              rhs=wqkv[:, 2 * D:3 * D], start=True, stop=True, skip_group_check=True)
                last.then_inc(S["v_ps"], 1)

            def scores(b, n):
                if n == 0:
                    need(pe, "qk_rows", b, 16 * 18)
                if n < 2:
                    need(pe, "gc", b, 0)
                    need(pe, "upr", b, 0)
                if n >= 2:
                    need(pe, "s_max", b, n - 1)
                for j in range(4):
                    h = 4 * (n % 4) + j
                    last = mm(ring[:, n % 2, j * L:(j + 1) * L], lhsT=q_rows[0:72, h, (n // 4) * P:(n // 4 + 1) * P],
                              rhs=k_rows[0:72, h, :], start=True, stop=True, skip_group_check=True)
                last.then_inc(S["s_ps"], 1)

            def turn_max(b):
                pe.wait_ge(c_dve, DVE_SETUP)
                need(pe, "mp2", b, 1)
                for n in range(NT):
                    last = tr(ring[0:3 * H, 0, :].bitcast(BF16)[:, n * P:(n + 1) * P],
                              mpart[:, n, :, :].rearrange("p a h -> p (a h)"), identb[:, :])
                last.then_inc(S["m_ps"], 1)

            def scores_t(b, n):
                if n == 0:
                    need(pe, "m_rows", b, 16)
                    need(pe, "s_max", b, ST)
                if n == 1:
                    need(pe, "m_sb", b, 1)
                if n >= 2:
                    need(pe, "prob", b, n - 1)
                for j in range(4):
                    h = 4 * (n // 2) + j
                    last = mm(ring[:, (n + 1) % 2, j * L:(j + 1) * L], lhsT=k_rows[0:75, h, (n % 2) * P:(n % 2 + 1) * P],
                              rhs=q_rows[0:75, h, :], start=True, stop=True, skip_group_check=True)
                last.then_inc(S["st_ps"], 1)

            def values(b, n):
                if n == 0:
                    need(pe, "y2", b, 0)
                if n == 4:
                    need(pe, "o_raw", b, 1)
                need(pe, "prob", b, n + 1)
                o = (n // 2) % 2 * L
                for j in range(4):
                    last = mm(pa[32 * j:32 * (j + 1), o:o + L], lhsT=vt[:, n % 2, 4 * (n // 2) + j, :],
                              rhs=prob[:, n % NPT, j, :], start=(n % 2 == 0), stop=(n % 2 == 1), skip_group_check=True)
                last.then_inc(S["pv"], 1)

            def turn_values(b):
                need(pe, "o_raw", b, 2)
                need(pe, "prob", b, ST - 1)
                for n in range(NT):
                    for g in range(H // 4):
                        last = tr(ring[:, 1, n * 512 + g * P:n * 512 + (g + 1) * P], o_raw[:, g, n * P:(n + 1) * P], ident[:, :])
                last.then_inc(S["or_ps"], 1)

            def attn_out_1(b):
                need(pe, "o_sb", b, NT)
                need(pe, "prob", b, ST)
                for n in range(NT):
                    last = tr(ring[:, 0, n * P:(n + 1) * P], o_tok[:, n, :, :].rearrange("p h d -> p (h d)"), ident[:, :])
                last.then_inc(S["ot_ps"], 1)

            def attn_out_2(b):
                need(pe, "ot_sb", b, 1)
                mm(ring[:, 1, 0:L], lhsT=wout[:, :], rhs=o_t[:, :], start=True, stop=True,
                   skip_group_check=True).then_inc(S["y_ps"], 1)

            def router(b):
                need(pe, "h2", b, 1)
                for n in range(NT):
                    last = mm(ring[:, 0, n * E:(n + 1) * E], lhsT=ht[:, n * P:(n + 1) * P], rhs=wrout[:, :],
                              start=True, stop=True, skip_group_check=True)
                last.then_inc(S["lg_ps"], 1)

            def turn_scores(b):
                need(pe, "sp2", b, 1)
                need(pe, "sc", b, 1)
                need(pe, "ya", b, 1)
                for n in range(NT):
                    tr(ring[:, 1, n * P:(n + 1) * P], sc[:, n, :], ident[:, :])
                for n in range(NT):
                    last = tr(ring[:, 1, 512:1024].bitcast(BF16)[:, n * P:(n + 1) * P], sc_part[:, n, :], identb[:, :])
                last.then_inc(S["sct_ps"], 1)

            def broadcast(b, n):
                if n == 0:
                    need(pe, "sctb", b, 1)
                    need(pe, "lg", b, 1)
                if n == 1:
                    need(pe, "sctf", b, 1)
                if n >= 2:
                    need(pe, "bc", b, n - 1)
                for j in range(4):
                    last = mm(ring[:, n % 2, j * L:(j + 1) * L], lhsT=sel[:, 4 * n + j, :], rhs=sctb[:, :],
                              start=True, stop=True, skip_group_check=True)
                last.then_inc(S["bc_ps"], 1)

            def gate_up(b, n):
                if n < 2:
                    need(pe, "bc", b, n + 3)
                else:
                    need(pe, "gc", b, 2 * (n - 1))
                    need(pe, "upr", b, 2 * (n - 1))
                for g in range(2):
                    for j in range(2):
                        last = mm(ring[:, n % 2, g * 512 + j * L:g * 512 + (j + 1) * L], lhsT=wgu[:, 2 * n + j, g, :],
                                  rhs=ht[:, :], start=True, stop=True, skip_group_check=True)
                last.then_inc(S["gu_ps"], 1)

            def down_bias(b):
                need(pe, "norm2", b, 1)
                need(pe, "sctf", b, 1)
                mm(pa[:, 0:L], lhsT=dbias[:, :], rhs=sct[:, :], start=True, stop=False, skip_group_check=True)

            def down_pair(b, n):
                need(pe, "act", b, n + 1)
                for j in range(2):
                    last = mm(pa[:, 0:L], lhsT=wdown[:, 2 * n + j, :], rhs=upc[:, n % 2, j * L:(j + 1) * L],
                              start=False, stop=(n == 7 and j == 1), skip_group_check=True)
                last.then_inc(S["dn"], 1)

            def phases(b, c):
                if c == 0:
                    need(pe, "h3", b, 1)
                    k = later(b)
                    need(pe, "q_sb", b, k)
                    need(pe, "k_sb", b, k)
                    need(pe, "v_sb", b, NT * k)
                    need(pe, "ksq", b, 0)
                    need(pe, "rsig", b, 0)
                    need(pe, "xo", b, 0)
                else:
                    need(pe, "turn", b, c)
                    need(pe, "frac", b, c)
                for j in range(2):
                    last = mm(pb_k[:, j * L:(j + 1) * L], lhsT=wk[:, (2 * c + j) * P:(2 * c + j + 1) * P], rhs=hb[:, 1:L + 1],
                              start=True, stop=True, skip_group_check=True)
                last.then_inc(S["k_ps"], 1)
                if c:
                    need(pe, "vpos", b, 2 * c)
                    need(pe, "vas", b, 2 * c)
                for j in range(2):
                    last = mm(pb_v[:, j * L:(j + 1) * L], lhsT=wv[:, (2 * c + j) * P:(2 * c + j + 1) * P], rhs=hb[:, 1:L + 1],
                              start=True, stop=True, skip_group_check=True)
                last.then_inc(S["v2_ps"], 1)

            def memory_wo(b, c):
                if c == 0:
                    need(pe, "norm3", b, 1)
                for m, s in ((0, "sum12"), (2, "sum34")):
                    need(pe, s, b, c + 1)
                    for j in range(2):
                        last = mm(pb[:, 0:L], lhsT=wo[:, 2 * c + j, :], rhs=prod[:, c % 2, m, j * L:(j + 1) * L],
                                  start=(c == 0 and m == 0 and j == 0), stop=(c == CC - 1 and m == 2 and j == 1),
                                  skip_group_check=True)
                last.then_inc(S["wo"], 1)

            def mix_1(b):
                need(pe, "xr", b, 1)
                need(pe, "frac", b, CC)
                need(pe, "turn", b, CC)
                mm(pb_k[:, 0:L], lhsT=ffn_w[:, 0, :], rhs=xr[:, :], start=True, stop=True, skip_group_check=True)
                need(pe, "xk", b, 1)
                mm(pb_k[:, L:2 * L], lhsT=ffn_w[:, 1, :], rhs=xk[:, :], start=True, stop=True,
                   skip_group_check=True).then_inc(S["rk_ps"], 1)

            def mix_2(b):
                need(pe, "ksq", b, 1)
                need(pe, "vpos", b, 2 * CC)
                need(pe, "vas", b, 2 * CC)
                mm(pb_v[:, 0:L], lhsT=ffn_w[:, 2, :], rhs=ksq[:, :], start=True, stop=True,
                   skip_group_check=True).then_inc(S["vv_ps"], 1)

            def mix_3(b):
                need(pe, "x4", b, 1)
                for n in range(NT):
                    last = tr(pb_v[:, L + n * P:L + (n + 1) * P], x4[:, n * P:(n + 1) * P], ident[:, :])
                last.then_inc(S["xo_ps"], 1)

            def head(nx):
                head_1(nx)
                head_2(nx)
                head_3(nx)
                head_4(nx)
                head_5(nx)

            def step(a, b, nx):
                on_a, on_b, on_x = a is not None, b is not None, nx is not None
                if on_b:
                    mean(b, "3", xb[:, :], "mod_b", pb, (("norm1", b, later(b)),))
                if on_a:
                    scores(a, 0)
                    scores(a, 1)
                if on_b:
                    variance(b, "3", pb, sqb)
                if on_a:
                    scores(a, 2)
                if on_b:
                    deviation(b, "3", pb, rstdb)
                if on_a:
                    for n in (3, 4, 5):
                        scores(a, n)
                if on_b:
                    phases(b, 0)
                if on_a:
                    scores(a, 6)
                    scores(a, 7)
                if on_b:
                    phases(b, 1)
                if on_a:
                    turn_max(a)
                    scores_t(a, 0)
                    scores_t(a, 1)
                    values(a, 0)
                    scores_t(a, 2)
                    values(a, 1)
                    scores_t(a, 3)
                    values(a, 2)
                if on_b:
                    memory_wo(b, 0)
                    phases(b, 2)
                if on_a:
                    scores_t(a, 4)
                    values(a, 3)
                    scores_t(a, 5)
                    values(a, 4)
                    scores_t(a, 6)
                    values(a, 5)
                    scores_t(a, 7)
                    values(a, 6)
                if on_b:
                    memory_wo(b, 1)
                    phases(b, 3)
                if on_a:
                    values(a, 7)
                    turn_values(a)
                if on_b:
                    memory_wo(b, 2)
                if on_a:
                    attn_out_1(a)
                    attn_out_2(a)
                    mean(a, "2", x1[:, :], "x1", pa, ())
                    variance(a, "2", pa, sq)
                    deviation(a, "2", pa, rstd)
                if on_b:
                    memory_wo(b, 3)
                    mean(b, "4", x3[:, :], "x3", pb, ())
                if on_b:
                    variance(b, "4", pb, sqb)
                if on_a:
                    router(a)
                if on_b:
                    deviation(b, "4", pb, rstdb)
                    mix_1(b)
                    mix_2(b)
                if on_a:
                    turn_scores(a)
                    broadcast(a, 0)
                    broadcast(a, 1)
                if on_b:
                    mix_3(b)
                if on_a:
                    broadcast(a, 2)
                    broadcast(a, 3)
                    down_bias(a)
                    gate_up(a, 0)
                    gate_up(a, 1)
                if on_x:
                    head_1(nx)
                if on_a:
                    down_pair(a, 0)
                    gate_up(a, 2)
                if on_x:
                    head_2(nx)
                if on_a:
                    down_pair(a, 1)
                    gate_up(a, 3)
                if on_x:
                    head_3(nx)
                if on_a:
                    down_pair(a, 2)
                    gate_up(a, 4)
                if on_x:
                    head_4(nx)
                if on_a:
                    down_pair(a, 3)
                    gate_up(a, 5)
                if on_x:
                    head_5(nx)
                if on_a:
                    down_pair(a, 4)
                    gate_up(a, 6)
                    down_pair(a, 5)
                    gate_up(a, 7)
                    down_pair(a, 6)
                    down_pair(a, 7)

            run(pe, head, step)

        @block.scalar
        def _(act):
            af = nc.scalar.activation
            for n in range(2):
                for d in range(DH):
                    act.dma_start(bcol[d * H:(d + 1) * H, n:n + 1],
                                  bqkv[n * D:(n + 1) * D].rearrange("(h d) -> h d", d=DH)[:, d:d + 1], allow_slow_non_contiguous=True).then_inc(ld_small, 16)
            act.dma_start(bcol[:, 3:4], bout.rearrange("(k p) -> p k", p=P), allow_slow_non_contiguous=True).then_inc(ld_small, 16)
            act.dma_start(mu[:, 0:1], mu_r.rearrange("(k p) -> p k", p=P), allow_slow_non_contiguous=True).then_inc(ld_small, 16)
            act.dma_start(mu[:, 1:2], mu_k.rearrange("(k p) -> p k", p=P), allow_slow_non_contiguous=True).then_inc(ld_small, 16)
            act.dma_start(vbias[:, :], bqkv[2 * D:3 * D].rearrange("(a n) -> a n", a=1).to_broadcast([P, D])).then_inc(ld_small, 16)
            act.dma_start(rbias[:, :], router_b.rearrange("(a n) -> a n", a=1).to_broadcast([P, E])).then_inc(ld_small, 16)
            act.dma_start(fcol[:, :], freqs.rearrange("(k a) d -> (a d) k", a=2), allow_slow_non_contiguous=True).then_inc(ld_small, 16)
            for g in range(2):
                for a in range(2):
                    act.dma_start(gcol[64 * a:64 * (a + 1), g, :],
                                  gate[a:H:2, g:g + 1].rearrange("k a -> a k").to_broadcast([64, CT]), allow_slow_non_contiguous=True).then_inc(ld_small, 16)
            act.dma_start(bl[:, :, :], gub.rearrange("e (f g) -> e f g", g=2)).then_inc(ld_bias, 16)
            act.wait_ge(c_fill, 1)
            act.dma_start(dbias[0:E, :], downb).then_inc(ld_small, 16)
            act.dma_start(rel_in[1:P, 0, :], rel_emb[0:P - 1, :]).then_inc(ld_bias, 16)
            act.dma_start(rel_in[:, 1, :], rel_emb[P - 1:2 * P - 1, :]).then_inc(ld_bias, 16)
            act.wait_ge(ld_mod, 64)
            af(c_sig[:, :, :], c_in[:, :, :], ACT.Sigmoid).then_inc(c_act, 1)
            act.wait_ge(c_dve, DVE_TRIG)
            ang = prod[:, 0, :, :].rearrange("p a b -> p (a b)")
            tmp = prod[:, 1, :, :].rearrange("p a b -> p (a b)")
            af(sin_r[:, :, :].rearrange("p k t -> p (k t)"), ang, ACT.Sin).then_inc(c_act, 1)
            af(tmp, ang, ACT.Abs).then_inc(c_act, 1)
            act.wait_ge(c_act, 3)
            af(cos_r[:, :, :].rearrange("p k t -> p (k t)"), tmp, ACT.Sin, scale=-1.0, bias=half_pi[:, 0:1]).then_inc(c_act, 1)
            act.wait_ge(c_dve, DVE_SETUP)

            def square(b, n, c, s):
                need(act, "cent" + n, b, 1)
                af(s[:, :], c[:, :], ACT.Square).then_inc(S["sq" + n], 1)

            def modulate(b, n, src, dst, mod, k):
                need(act, "norm" + n, b, 1)
                af(dst, src[:, :], ACT.Identity, scale=mod[:, k + 1:k + 2], bias=mod[:, k:k + 1]).then_inc(S["h" + n], 1)

            def head_1(b):
                square(b, "1", cent, sq)

            def head_2(b):
                need(act, "mod_h", b, 1)
                need(act, "v_ps", b, 0)
                modulate(b, "1", cent, hta[:, :], mod_h, 0)

            def part(b):
                need(act, "q_sb", b, 1)
                need(act, "k_sb", b, 1)
                need(act, "qk_rows", b, 0)
                af(qk_part[:, 0, :, :], qk[:, :, :], ACT.Copy).then_inc(S["part0"], 1)
                need(act, "rest0", b, 1)
                af(qk_part[:, 1, :, :], qk[:, :, :], ACT.Copy).then_inc(S["part1"], 1)

            def copy_max(b):
                need(act, "m_ps", b, 1)
                need(act, "m_rows", b, 0)
                af(m_sb[:, :], ring[0:3 * H, 0, :].bitcast(BF16)[:, 0:L], ACT.Copy).then_inc(S["m_sb"], 1)

            def exps(b, n):
                need(act, "st_ps", b, n + 1)
                if n < NPT:
                    need(act, "pv", b, 0)
                else:
                    need(act, "pv", b, n - NPT + 1)
                af(prob[:, n % NPT, :, :].rearrange("p i q -> p (i q)"), ring[:, (n + 1) % 2, :],
                   ACT.Exp).then_inc(S["prob"], 1)

            def copy_values(b, n):
                need(act, "pv", b, 4 * n + 4)
                need(act, "or_ps", b, 0)
                af(o_raw[:, 2 * n:2 * n + 2, :].rearrange("p g q -> p (g q)"), pa[:, :], ACT.Copy).then_inc(S["o_raw"], 1)

            def attn_tail(b):
                need(act, "ot_ps", b, 1)
                need(act, "y_ps", b, 0)
                af(o_t[:, :], ring[:, 0, 0:L], ACT.Copy).then_inc(S["ot_sb"], 1)
                need(act, "y_ps", b, 1)
                need(act, "x1", b, 0)
                need(act, "mod_a", b, 1)
                af(ya[:, :], ring[:, 1, 0:L], ACT.Identity, scale=mod_a[:, 2:3], bias=mod_a[:, 12:13]).then_inc(S["ya"], 1)

            def second_norm(b):
                square(b, "2", cent, sq)
                modulate(b, "2", cent, ht[:, :], mod_a, 3)

            def route(b):
                need(act, "shift", b, 1)
                need(act, "exm", b, 0)
                af(ex[:, :, :], lsh[:, :, :], ACT.Exp).then_inc(S["ex"], 1)

            def copy_scores(b):
                need(act, "sct_ps", b, 1)
                need(act, "bc_ps", b, 0)
                af(sctb[:, :], ring[:, 1, 512:1024].bitcast(BF16)[:, 0:L], ACT.Copy).then_inc(S["sctb"], 1)
                need(act, "dn", b, 0)
                af(sct[:, :], ring[:, 1, 0:L], ACT.Copy).then_inc(S["sctf"], 1)

            def copy_broadcast(b, n):
                need(act, "bc_ps", b, n + 1)
                need(act, "gsc", b, 0)
                af(sc_all[:, 4 * n:4 * n + 4, :].rearrange("p e t -> p (e t)"), ring[:, n % 2, :],
                   ACT.Copy).then_inc(S["bc"], 1)

            def up(b, n):
                need(act, "gu_ps", b, n + 1)
                need(act, "dn", b, n - 1)
                for j in range(2):
                    af(upc[:, n % 2, j * L:(j + 1) * L], ring[:, n % 2, 512 + j * L:512 + (j + 1) * L], ACT.Identity,
                       bias=gub_t[:, 1, 2 * n + j:2 * n + j + 1]).then_inc(S["upr"], 1)

            def sigmoid(b, n):
                need(act, "gc", b, 2 * n + 2)
                need(act, "gl", b, n - 1)
                af(sig[:, n % 2, :], gsc[:, n % 2, :], ACT.Sigmoid, scale=ALPHA).then_inc(S["sig"], 1)

            def head_b(b):
                square(b, "3", centb, sqb)
                need(act, "dif", b, 0)
                need(act, "xr", b, 0)
                need(act, "xk", b, 0)
                modulate(b, "3", centb, hb[:, 1:L + 1], mod_b, 6)

            def phase(b, c):
                h = c % 2
                need(act, "k_ps", b, c + 1)
                need(act, "frac", b, c)
                af(turn[:, :], pb_k[:, :], ACT.Identity, bias=magic[:, 0:1]).then_inc(S["turn"], 1)
                need(act, "v2_ps", b, c + 1)
                need(act, "in1", b, c)
                need(act, "in2", b, c)
                for j in range(2):
                    af(vpos[:, j * L:(j + 1) * L], pb_v[:, j * L:(j + 1) * L], ACT.Copy,
                       scale=gcol[:, 0, 2 * c + j:2 * c + j + 1]).then_inc(S["vpos"], 1)
                need(act, "in3", b, c)
                need(act, "in4", b, c)
                for j in range(2):
                    af(vas[:, j * L:(j + 1) * L], pb_v[:, j * L:(j + 1) * L], ACT.Copy,
                       scale=gcol[:, 1, 2 * c + j:2 * c + j + 1]).then_inc(S["vas"], 1)
                need(act, "frac", b, c + 1)
                need(act, "pr4", b, c - 1)
                need(act, "in4", b, c - 1)
                af(sin_t[:, h, :, 1:L + 1], frac[:, h, :].rearrange("p (k t) -> p k t", k=2), ACT.Sin,
                   scale=-TWO_PI_IN).then_inc(S["sin"], 1)
                need(act, "cos", b, c)
                af(fabs[:, :], frac[:, h, :], ACT.Abs).then_inc(S["fabs"], 1)
                need(act, "fabs", b, c + 1)
                need(act, "pr3", b, c - 1)
                need(act, "in3", b, c - 1)
                af(cos_t[:, h, :, 1:L + 1], fabs[:, :].rearrange("p (k t) -> p k t", k=2), ACT.Sin,
                   scale=-TWO_PI_IN, bias=half_pi[:, 0:1]).then_inc(S["cos"], 1)

            def mix(b):
                square(b, "4", centb, sqb)
                modulate(b, "4", centb, hb[:, 1:L + 1], mod_b, 9)

            def mix_1(b):
                need(act, "rk_ps", b, 1)
                need(act, "rv", b, 0)
                af(rsig[:, :], pb_k[:, 0:L], ACT.Sigmoid).then_inc(S["rsig"], 1)
                need(act, "vv_ps", b, 0)
                af(ksq[:, :], pb_k[:, L:2 * L], ACT.Relu).then_inc(S["krel"], 1)
                need(act, "krel", b, 1)
                af(ksq[:, :], ksq[:, :], ACT.Square).then_inc(S["ksq"], 1)

            def mix_2(b):
                need(act, "xo_ps", b, 1)
                need(act, "out", b, 0)
                af(xo[:, :, :].rearrange("p n f -> p (n f)"), pb_v[:, L:2 * L], ACT.Copy).then_inc(S["xo"], 1)

            def head(nx):
                head_1(nx)
                head_2(nx)
                part(nx)

            def step(a, b, nx):
                on_a, on_b, on_x = a is not None, b is not None, nx is not None
                if on_b:
                    head_b(b)
                    phase(b, 0)
                    phase(b, 1)
                if on_a:
                    copy_max(a)
                    for n in range(4):
                        exps(a, n)
                if on_b:
                    phase(b, 2)
                if on_a:
                    copy_values(a, 0)
                    for n in range(4, ST):
                        exps(a, n)
                if on_b:
                    phase(b, 3)
                if on_a:
                    copy_values(a, 1)
                    attn_tail(a)
                    second_norm(a)
                if on_b:
                    mix(b)
                if on_a:
                    route(a)
                if on_b:
                    mix_1(b)
                if on_a:
                    copy_scores(a)
                    copy_broadcast(a, 0)
                    copy_broadcast(a, 1)
                if on_b:
                    mix_2(b)
                if on_a:
                    copy_broadcast(a, 2)
                    copy_broadcast(a, 3)
                    for n in range(3):
                        up(a, n)
                        sigmoid(a, n)
                if on_x:
                    head_1(nx)
                if on_a:
                    for n in (3, 4):
                        up(a, n)
                        sigmoid(a, n)
                if on_x:
                    head_2(nx)
                if on_a:
                    for n in (5, 6):
                        up(a, n)
                        sigmoid(a, n)
                if on_x:
                    part(nx)
                if on_a:
                    up(a, 7)
                    sigmoid(a, 7)

            run(act, head, step)

        @block.vector
        def _(dve):
            tt = nc.vector.tensor_tensor
            ts = nc.vector.tensor_scalar
            stt = nc.vector.scalar_tensor_tensor
            count = [0]

            def done(ins, wait=True):
                count[0] += 1
                ins.then_inc(c_dve, 1)
                if wait:
                    dve.wait_ge(c_dve, count[0])

            dve.memset(mean_w[:, :], 1.0 / D)
            dve.memset(q_rows[64:75, :, :], 1.0)
            dve.memset(k_rows[64:75, :, :], 1.0)
            dve.memset(vt[:, :, :, DH + 1:VW], 0.0)
            dve.memset(vt[:, :, :, DH:DH + 1], 1.0)
            dve.memset(lg[:, :, 0:TOPK], BIG)
            dve.memset(sc[:, :, :], 0.0)
            dve.memset(sc_part[:, :, :], 0.0)
            dve.memset(hb[:, 0:1], 0.0)
            dve.memset(sin_t[:, :, :, 0:1], 0.0)
            dve.memset(cos_t[:, :, :, 0:1], 0.0)
            dve.memset(keep[:, :], 1.0)
            dve.memset(half_pi[:, :], TWO_PI / 4)
            dve.memset(magic[:, :], MAGIC)
            dve.memset(rel_in[:, :, :], 0.0)
            dve.memset(mhalf[:, :], -0.5)
            dve.memset(mhalf_w[:, :], -0.5)
            dve.memset(dbias[:, :], 0.0).then_inc(c_fill, 1)
            dve.wait_ge(c_act, 1)
            done(tt(c_in[:, :, :], c_in[:, :, :], c_sig[:, :, :], ALU.mult))
            dve.wait_ge(c_pe, 1)
            done(nc.vector.tensor_copy(c_t[:, :, :].rearrange("p l b -> p (l b)"), pa[:, 0:2 * B]))
            dve.wait_ge(ld_bias, 48)
            done(nc.vector.tensor_copy(rel_rep[:, :, :, :], rel_in[:, :, :].rearrange("p n (d a) -> p n d a", a=1)
                                       .to_broadcast([P, NT, DH, H])))
            dve.memset(keep[:, 0:2 * L:L], 0.0)
            ang = prod[:, 0, :, :].rearrange("p a b -> p (a b)")
            tmp = prod[:, 1, :, :].rearrange("p a b -> p (a b)")
            dve.wait_ge(c_pool, 9)
            done(nc.vector.tensor_copy(t_f[:, :], t_int[:, :]))
            dve.wait_ge(ld_small, 16 * N_SMALL)
            for k in range(CT):
                last = ts(ang[:, k * L:(k + 1) * L], t_f[:, :], fcol[:, k:k + 1], None, ALU.mult)
            done(last)
            done(ts(tmp, ang, 1.0 / TWO_PI, MAGIC, ALU.mult, ALU.add))
            done(ts(tmp, tmp, MAGIC, None, ALU.subtract))
            for c in (C1, C2, C3):
                done(stt(out=ang, in0=tmp, scalar=-c, in1=ang, op0=ALU.mult, op1=ALU.add))
            done(ts(ang, ang, PI_IN, -PI_IN, ALU.min, ALU.max))
            assert count[0] == DVE_TRIG
            done(ts(t_next[:, :], t_f[:, :], 1.0, None, ALU.add))
            done(nc.vector.tensor_copy(bd[:, :, :], bl[:, :, :].rearrange("e f g -> e g f")))
            done(ts(bd[:, 1, :], bd[:, 1, :], 1.0, None, ALU.add))
            assert count[0] == DVE_BIAS
            dve.wait_ge(c_pe, 2)
            done(nc.vector.tensor_copy(mods[:, 0:12, :].rearrange("p k b -> p (k b)"), pa[:, 64:64 + 12 * B]))
            done(ts(mods[:, 1:12:3, :], mods[:, 1:12:3, :], 1.0, None, ALU.add))
            g4 = mods[:, 2:12:3, :]
            for l in range(2):
                g2 = mods[:, 6 * l + 2:6 * l + 6:3, :]
                done(ts(mod_abs[:, :, :], g2, -1.0, 0.25, ALU.mult, ALU.max))
                done(tt(mod_abs[:, :, :], mod_abs[:, :, :], g2, ALU.max))
                done(ts(mod_sgn[:, :, :], g2, 0.0, 2.0, ALU.is_ge, ALU.mult))
                done(stt(out=g2, in0=mod_sgn[:, :, :], scalar=1.0, in1=mod_abs[:, :, :], op0=ALU.subtract, op1=ALU.mult))
            done(ts(mods[:, 12, :], mods[:, 2, :], bcol[:, 3:4], None, ALU.mult))
            dve.wait_ge(c_pe, 4)
            done(nc.vector.tensor_copy(ffn_w[:, :, :].rearrange("p n c -> p (n c)"), pb_k[:, 0:3 * D]))
            done(nc.vector.tensor_copy(wqk[:, :, :, :], wqkv[:, 0:2 * D].rearrange("p (n h d) -> p n d h", n=2, d=DH)))
            done(ts(wk[:, :], wk[:, :], 10.0 / TWO_PI, None, ALU.mult))
            dve.wait_ge(c_act, 4)
            dve.wait_ge(c_pool, 12)
            dve.wait_ge(c_pe, 5)
            done(nc.vector.tensor_copy(gub_t[:, :, :].rearrange("p g e -> p (g e)"), pb[:, 448:448 + 2 * E]))
            done(ts(relb[:, :], pb_v[:, 0:L], bcol[:, 1:2], None, ALU.add))
            assert count[0] == DVE_SETUP, count[0]

            def centre(b, n, src, dst, ps):
                need(dve, "mean" + n, b, 1)
                other, same = {"1": ("h2", 0), "2": ("h1", 1), "3": ("h4", 0), "4": ("h3", 1)}[n]
                need(dve, other, b, same)
                tt(dst[:, :], src[:, :], ps[:, 0:L], ALU.subtract).then_inc(S["cent" + n], 1)

            def epsilon(b, n, v, ps):
                need(dve, "var" + n, b, 1)
                ts(v[:, :], ps[:, L:L + NT], EPS, None, ALU.add).then_inc(S["veps" + n], 1)

            def scale(b, n, c, ps):
                need(dve, "rbc" + n, b, 1)
                tt(c[:, :], c[:, :], ps[:, L:2 * L], ALU.mult).then_inc(S["norm" + n], 1)

            def at_batch(t, b):
                return t[:, :, b:b + 1] if isinstance(b, int) else t[:, :, bass.ds(b, 1)]

            def head_1(b):
                need(dve, "xt_ps", b, 1)
                need(dve, "x1", b, 0)
                nc.vector.tensor_copy(xt[:, :], pb_k[:, 0:L]).then_inc(S["xt"], 1)
                need(dve, "xt", b, 1)
                need(dve, "h1", b, 0)
                nc.vector.tensor_copy(mod_h[:, :].rearrange("p (k a) -> p k a", a=1), at_batch(mods, b)).then_inc(S["mod_h"], 1)

            def head_2(b):
                centre(b, "1", xt, cent, pb)

            def head_3(b):
                epsilon(b, "1", veps, pb)

            def head_4(b):
                scale(b, "1", cent, pb)

            def head_5(b):
                need(dve, "qk_ps", b, 1)
                need(dve, "part2", b, 0)
                ts(qk[:, 0, :], pb_k[:, 0:L], bcol[:, 0:1], float(DH) ** -0.5, ALU.add, ALU.mult).then_inc(S["q_sb"], 1)
                tt(qk[:, 1, :], pb_k[:, L:2 * L], relb[:, :], ALU.add).then_inc(S["k_sb"], 1)
                need(dve, "v_ps", b, 1)
                need(dve, "pv", b, 0)
                for n in range(NT):
                    tt(vt[:, n, :, 0:DH], pb_v[:, n * D:(n + 1) * D].rearrange("p (h d) -> p h d", d=DH),
                       vbias[:, :].rearrange("p (h d) -> p h d", d=DH), ALU.add).then_inc(S["v_sb"], 1)

            def maxima(b, n):
                need(dve, "s_ps", b, n + 1)
                nc.vector.tensor_reduce(smax[:, n // 4, 4 * (n % 4):4 * (n % 4) + 4],
                                        ring[:, n % 2, :].rearrange("p (h k) -> p h k", h=4), AX_X, ALU.max).then_inc(S["s_max"], 1)

            def split_max(b):
                need(dve, "s_max", b, ST)
                ts(negm[:, :, :], smax[:, :, :], -1.0, None, ALU.mult).then_inc(S["neg"], 1)
                need(dve, "neg", b, 1)
                nc.vector.tensor_copy(mpart[:, :, 0, :], negm[:, :, :]).then_inc(S["mp0"], 1)
                need(dve, "mp0", b, 1)
                tt(mrest[:, :, :], negm[:, :, :], mpart[:, :, 0, :], ALU.subtract).then_inc(S["mr0"], 1)
                need(dve, "mr0", b, 1)
                nc.vector.tensor_copy(mpart[:, :, 1, :], mrest[:, :, :]).then_inc(S["mp1"], 1)
                need(dve, "mp1", b, 1)
                tt(mpart[:, :, 2, :], mrest[:, :, :], mpart[:, :, 1, :], ALU.subtract).then_inc(S["mp2"], 1)

            def attn_norm(b):
                need(dve, "or_ps", b, 1)
                nc.vector.reciprocal(rden[:, :, :], o_ps[:, :, :, DH]).then_inc(S["den"], 1)
                need(dve, "den", b, 1)
                need(dve, "ot_ps", b, 0)
                for n in range(NT):
                    tt(o_tok[:, n, :, :], o_ps[:, n, :, 0:DH],
                       rden[:, n, :].rearrange("p (h a) -> p h a", a=1).to_broadcast([P, H, DH]), ALU.mult).then_inc(S["o_sb"], 1)

            def route(b):
                need(dve, "lg_ps", b, 1)
                rb = rbias[:, :].rearrange("p (a e) -> p a e", a=1).to_broadcast([P, NT, E])
                tt(lg[:, :, TOPK:], ring[:, 0, 0:NT * E].rearrange("p (n e) -> p n e", e=E), rb, ALU.add).then_inc(S["lg"], 1)
                dve.wait_ge(c_dve, DVE_SETUP)
                need(dve, "lg", b, 1)
                for n in range(NT):
                    nc.vector.max(top8[:, n, :], lg[:, n, :]).then_inc(S["top8"], 1)
                need(dve, "top8", b, NT)
                tt(lsh[:, :, :], lg[:, :, TOPK:], top8[:, :, 4:5].to_broadcast([P, NT, E]), ALU.subtract).then_inc(S["shift"], 1)
                for n in range(NT):
                    nc.vector.match_replace(out=repl[:, n, :], in_to_replace=top8[:, n, :], in_values=lg[:, n, :],
                                            imm_value=-BIG).then_inc(S["repl"], 1)

            def route_2(b):
                need(dve, "repl", b, NT)
                need(dve, "ex", b, 1)
                for n in range(NT):
                    stt(out=exm[:, n, :], in0=repl[:, n, TOPK:], scalar=-BIG, in1=ex[:, n, :], op0=ALU.is_equal,
                        op1=ALU.mult).then_inc(S["exm"], 1)
                need(dve, "exm", b, NT)
                nc.vector.tensor_reduce(esum[:, :], exm[:, :, :], AX_X, ALU.add).then_inc(S["esum"], 1)
                need(dve, "esum", b, 1)
                nc.vector.reciprocal(rsum[:, :], esum[:, :]).then_inc(S["rsum"], 1)
                need(dve, "rsum", b, 1)
                need(dve, "sct_ps", b, 0)
                tt(sc[:, :, 0:E], exm[:, :, :], rsum[:, :].rearrange("p (n a) -> p n a", a=1).to_broadcast([P, NT, E]),
                   ALU.mult).then_inc(S["sc"], 1)
                need(dve, "sc", b, 1)
                nc.vector.tensor_copy(sc_part[:, :, 0:E], sc[:, :, 0:E]).then_inc(S["sp0"], 1)
                need(dve, "sp0", b, 1)
                tt(srest[:, :, :], sc[:, :, 0:E], sc_part[:, :, 0:E], ALU.subtract).then_inc(S["sr0"], 1)
                need(dve, "sr0", b, 1)
                nc.vector.tensor_copy(sc_part[:, :, E:2 * E], srest[:, :, :]).then_inc(S["sp1"], 1)
                need(dve, "sp1", b, 1)
                tt(sc_part[:, :, 2 * E:3 * E], srest[:, :, :], sc_part[:, :, E:2 * E], ALU.subtract).then_inc(S["sp2"], 1)

            def gate(b, n):
                need(dve, "gu_ps", b, n + 1)
                need(dve, "act", b, n - 1)
                for j in range(2):
                    ts(gsc[:, n % 2, j * L:(j + 1) * L], ring[:, n % 2, j * L:(j + 1) * L],
                       gub_t[:, 0, 2 * n + j:2 * n + j + 1], LIMIT, ALU.add, ALU.min).then_inc(S["gc"], 1)

            def gate_up(b, n):
                need(dve, "upr", b, 2 * n + 2)
                ts(upc[:, n % 2, :], upc[:, n % 2, :], LIMIT + 1.0, 1.0 - LIMIT, ALU.min, ALU.max).then_inc(S["upc"], 1)
                need(dve, "gsc", b, n + 1)
                tt(gsc[:, n % 2, :], sig[:, n % 2, :], gsc[:, n % 2, :], ALU.mult).then_inc(S["gl"], 1)

            def experts_out(b):
                need(dve, "dn", b, 8)
                ts(ya[:, :], pa[:, 0:L], mod_a[:, 5:6], None, ALU.mult).then_inc(S["y2"], 1)
                need(dve, "y2", b, 1)
                need(dve, "mod_b", b, 0)
                tt(x2[:, :], x1[:, :], ya[:, :], ALU.add).then_inc(S["x2"], 1)

            def head_b(b):
                need(dve, "x2", b, 1)
                nc.vector.tensor_copy(mod_b[:, :].rearrange("p (k a) -> p k a", a=1), at_batch(mods, b))
                nc.vector.tensor_copy(xb[:, :], x2[:, :]).then_inc(S["mod_b"], 1)
                need(dve, "mod_b", b, 1)
                centre(b, "3", xb, centb, pb)

            def memory_a(b, c):
                h = c % 2
                need(dve, "turn", b, c + 1)
                need(dve, "fabs", b, c - 1)
                stt(out=frac[:, h, :], in0=turn[:, :], scalar=MAGIC, in1=pb_k[:, :], op0=ALU.subtract,
                    op1=ALU.subtract).then_inc(S["frac"], 1)

            def memory_b(b, c):
                h = c % 2
                need(dve, "wo", b, c - 1)
                for n, s in ((0, "cu1"), (1, "cu2")):
                    need(dve, "in" + str(n + 1), b, c + 1)
                    nc.vector.tensor_tensor_scan(prod[:, h, n, :], keep[:, :], prod[:, h, n, :], 0.0, ALU.mult,
                                                 ALU.add).then_inc(S[s], 1)
                need(dve, "vas", b, 2 * c + 2)
                v = vas[:, :].rearrange("p (k t) -> p k t", k=2)
                need(dve, "cos", b, c + 1)
                for n, t in ((2, cos_t), (3, sin_t)):
                    tt(prod[:, h, n, :].rearrange("p (k t) -> p k t", k=2), v, t[:, h, :, 0:L], ALU.mult).then_inc(S["in" + str(n + 1)], 1)

            def memory_c(b, c):
                h = c % 2
                for n in (2, 3):
                    need(dve, "in" + str(n + 1), b, c + 1)
                    nc.vector.tensor_tensor_scan(prod[:, h, n, :], keep[:, :], prod[:, h, n, :], 0.0, ALU.mult,
                                                 ALU.add).then_inc(S["cu" + str(n + 1)], 1)
                for n, t in ((2, cos_t), (3, sin_t)):
                    need(dve, "cu" + str(n + 1), b, c + 1)
                    cv = prod[:, h, n, :].rearrange("p (k t) -> p k t", k=2)
                    tt(cv, cv, t[:, h, :, 1:L + 1], ALU.mult).then_inc(S["pr" + str(n + 1)], 1)
                need(dve, "pr3", b, c + 1)
                need(dve, "pr4", b, c + 1)
                tt(prod[:, h, 2, :], prod[:, h, 2, :], prod[:, h, 3, :], ALU.add).then_inc(S["sum34"], 1)

            def memory_end(b):
                need(dve, "wo", b, CC)
                stt(out=dif[:, :], in0=pb[:, 0:L], scalar=mod_b[:, 8:9], in1=inv_s[:, :], op0=ALU.mult,
                    op1=ALU.mult).then_inc(S["yv"], 1)
                need(dve, "yv", b, 1)
                tt(x3[:, :], xb[:, :], dif[:, :], ALU.add).then_inc(S["x3"], 1)

            def mix_in(b):
                need(dve, "h4", b, 1)
                tt(dif[:, :], hb[:, 1:L + 1], hb[:, 0:L], ALU.subtract).then_inc(S["dif"], 1)
                need(dve, "dif", b, 1)
                need(dve, "rk_ps", b, 0)
                stt(out=xr[:, :], in0=dif[:, :], scalar=mu[:, 0:1], in1=hb[:, 0:L], op0=ALU.mult, op1=ALU.add).then_inc(S["xr"], 1)
                stt(out=xk[:, :], in0=dif[:, :], scalar=mu[:, 1:2], in1=hb[:, 0:L], op0=ALU.mult, op1=ALU.add).then_inc(S["xk"], 1)

            def mix_out(b):
                need(dve, "vv_ps", b, 1)
                need(dve, "rsig", b, 1)
                stt(out=xr[:, :], in0=pb_v[:, 0:L], scalar=mod_b[:, 11:12], in1=rsig[:, :], op0=ALU.mult,
                    op1=ALU.mult).then_inc(S["rv"], 1)
                need(dve, "rv", b, 1)
                need(dve, "xo_ps", b, 0)
                tt(x4[:, :], x3[:, :], xr[:, :], ALU.add).then_inc(S["x4"], 1)

            def head(nx):
                head_1(nx)
                head_2(nx)
                head_3(nx)
                head_4(nx)
                head_5(nx)

            def step(a, b, nx):
                on_a, on_b, on_x = a is not None, b is not None, nx is not None
                if on_b:
                    head_b(b)
                if on_a:
                    need(dve, "x2", a, 0)
                    nc.vector.tensor_copy(mod_a[:, :].rearrange("p (k a) -> p k a", a=1), at_batch(mods, a)).then_inc(S["mod_a"], 1)
                    maxima(a, 0)
                    maxima(a, 1)
                if on_b:
                    epsilon(b, "3", vepsb, pb)
                if on_a:
                    maxima(a, 2)
                if on_b:
                    scale(b, "3", centb, pb)
                if on_a:
                    for n in (3, 4, 5):
                        maxima(a, n)
                if on_b:
                    memory_a(b, 0)
                if on_a:
                    maxima(a, 6)
                    maxima(a, 7)
                    split_max(a)
                if on_b:
                    memory_a(b, 1)
                    memory_b(b, 0)
                    memory_c(b, 0)
                    memory_b(b, 1)
                    memory_a(b, 2)
                    memory_c(b, 1)
                    memory_b(b, 2)
                    memory_a(b, 3)
                    memory_c(b, 2)
                if on_a:
                    attn_norm(a)
                if on_b:
                    memory_b(b, 3)
                if on_a:
                    centre(a, "2", x1, cent, pa)
                if on_b:
                    memory_c(b, 3)
                if on_a:
                    epsilon(a, "2", veps, pa)
                    scale(a, "2", cent, pa)
                if on_b:
                    memory_end(b)
                    centre(b, "4", x3, centb, pb)
                    epsilon(b, "4", vepsb, pb)
                if on_a:
                    route(a)
                if on_b:
                    scale(b, "4", centb, pb)
                if on_a:
                    route_2(a)
                if on_b:
                    mix_in(b)
                    mix_out(b)
                if on_a:
                    gate(a, 0)
                    gate(a, 1)
                    gate_up(a, 0)
                if on_x:
                    head_1(nx)
                if on_a:
                    gate(a, 2)
                    gate_up(a, 1)
                if on_x:
                    head_2(nx)
                if on_a:
                    gate(a, 3)
                    gate_up(a, 2)
                if on_x:
                    head_3(nx)
                if on_a:
                    gate(a, 4)
                    gate_up(a, 3)
                if on_x:
                    head_4(nx)
                if on_a:
                    gate(a, 5)
                    gate_up(a, 4)
                if on_x:
                    head_5(nx)
                if on_a:
                    gate(a, 6)
                    gate_up(a, 5)
                    gate(a, 7)
                    gate_up(a, 6)
                    gate_up(a, 7)
                    experts_out(a)

            run(dve, head, step)


DVE_TRIG = 11
DVE_BIAS = 14
DVE_SETUP = 30


def later(b):
    return 1 if isinstance(b, int) and b == B - 1 else 2


def run(eng, head, step):
    head(0)
    step(0, None, 1)
    step(1, 0, 2)
    with eng.Fori(2, B - 1) as i:
        step(i, i - 1, i + 1)
    step(B - 1, B - 2, None)
    step(None, B - 1, None)


_INS = ['L0_attn_x', 'L0_attn_Wqkv', 'L0_attn_bqkv', 'L0_attn_Wout', 'L0_attn_bout', 'L0_attn_rel_emb',
        'L0_ffn_router_w', 'L0_ffn_router_b', 'L0_ffn_gate_up_proj', 'L0_ffn_gate_up_bias', 'L0_ffn_down_proj',
        'L0_ffn_down_bias', 'L0_c', 'L0_wmod', 'L1_attn_Wk', 'L1_attn_Wv', 'L1_attn_Wo', 'L1_attn_gate',
        'L1_attn_freqs', 'L1_ffn_W_r', 'L1_ffn_W_k', 'L1_ffn_W_v', 'L1_ffn_mu_r', 'L1_ffn_mu_k', 'L1_c', 'L1_wmod']


def kernel(**inputs):
    import numpy as _np
    import concourse.bacc as _bacc
    from concourse import mybir as _mybir
    from concourse.bass_utils import run_bass_kernel_spmd as _run

    nc = _bacc.Bacc("TRN2", target_bir_lowering=False, num_devices=1)
    arrays, args = {}, []
    for name in _INS:
        a = _np.ascontiguousarray(inputs[name])
        arrays[f"in_{name}_dram"] = a
        args.append(nc.dram_tensor(f"in_{name}_dram", a.shape, _mybir.dt.from_np(a.dtype), kind="ExternalInput").ap())
    args.append(nc.dram_tensor("out_dram", (B, L, D), _mybir.dt.float32, kind="ExternalOutput").ap())
    build(nc, *args)
    r = _run(nc, [arrays], core_ids=[0])
    return r.results[0]["out_dram"]
```

```python
from contextlib import ExitStack

import concourse.bass as bass
from concourse import mybir

F32 = mybir.dt.float32
BF16 = mybir.dt.bfloat16
I32 = mybir.dt.int32
ALU = mybir.AluOpType
ACT = mybir.ActivationFunctionType
AX_X = mybir.AxisListType.X

P = 128
B = 16
L = 256
D = 128
NT = L // P
H = 16
DH = D // H
E = 16
TOPK = 4
HD = 1024
CT = HD // P
CC = 4
ST = 8
VW = 32
NPT = 3
NG = 3
NU = 4
BY_DVE = (3, 5, 6, 7)
EPS = 1e-5
ALPHA, LIMIT = 1.702, 7.0
TWO_PI = 6.283185307179586
TWO_PI_IN = 6.283185
PI_IN = 3.1415925
MAGIC = 12582912.0
C1, C2, C3 = 6.28125, 0.0019350051879882812, 3.0199159819567e-07
BIG = 3.0e38

PER = dict(
    x_in=16, xt_ps=1, xt=1, mean1=1, cent1=1, sq1=1, var1=1, veps1=1, rstd1=1, rbc1=1, norm1=1, h1=1,
    qk_ps=1, v_ps=1, q_sb=1, k_sb=1, v_sb=NT, part0=1, rest0=1, part1=1, part2=1, qk_rows=16 * 18,
    s_ps=ST, s_max=ST, neg=1, mp0=1, mr0=1, mp1=1, mp2=1, m_ps=1, m_sb=1, m_rows=16,
    st_ps=ST, prob=ST, pv=ST, o_raw=2, or_ps=1, den=1, o_sb=NT, ot_ps=1, ot_sb=1, y_ps=1, ya=1, x1=1,
    mean2=1, cent2=1, sq2=1, var2=1, veps2=1, rstd2=1, rbc2=1, norm2=1, h2=1,
    lg_ps=1, lg=1, top8=NT, shift=1, repl=NT, ex=1, exm=NT, esum=1, rsum=1, sc=1,
    sp0=1, sr0=1, sp1=1, sp2=1, sct_ps=1, sctf=1, sctb=1, bc_ps=4, bc=4,
    gu_ps=8, gc=16, upr=16, sig=8, gsc=8, upc=8, gl=8, act=8, dn=8, y2=1, x2=1, mod_a=1, mod_h=1,
    mod_b=1, mean3=1, cent3=1, sq3=1, var3=1, veps3=1, rstd3=1, rbc3=1, norm3=1, h3=1,
    k_ps=CC, v2_ps=CC, turn=CC, frac=CC, sin=CC, fabs=CC, cos=CC, val=CC,
    in1=CC, in2=CC, in3=CC, in4=CC, cu1=CC, cu2=CC, cu3=CC, cu4=CC,
    pr1=CC, pr2=CC, pr3=CC, pr4=CC, sum12=CC, sum34=CC, wo=CC, yv=1, x3=1,
    mean4=1, cent4=1, sq4=1, var4=1, veps4=1, rstd4=1, rbc4=1, norm4=1, h4=1,
    dif=1, xr=1, xk=1, rk_ps=1, rsig=1, krel=1, ksq=1, vv_ps=1, rv=1, x4=1, xo_ps=1, xo=1, out=16,
)


def build(nc, x, Wqkv, bqkv, Wout, bout, rel_emb, router_w, router_b, gup, gub, down, downb, c0, wmod0,
          Wk, Wv, Wo, gate, freqs, W_r, W_k, W_v, mu_r, mu_k, c1, wmod1, out):
    with ExitStack() as ctx:
        def sb(name, shape, dt=F32):
            return ctx.enter_context(nc.sbuf_tensor(name, shape, dt))

        wqkv = sb("wqkv", [P, 3 * D])
        wout = sb("wout", [P, D])
        wgu = sb("wgu", [P, E, 2, D])
        wdown = sb("wdown", [P, E, D])
        wrout = sb("wrout", [P, E])
        wk = sb("wk", [P, HD])
        wv = sb("wv", [P, HD])
        wo = sb("wo", [P, 2, CT, D])
        ffn_w = sb("ffn_w", [P, 3, D])
        ident = sb("ident", [P, P])
        identb = sb("identb", [P, P], BF16)
        mean_w = sb("mean_w", [P, P])
        bcol = sb("bcol", [P, 4])
        mu = sb("mu", [P, 2])
        vbias = sb("vbias", [P, D])
        rbias = sb("rbias", [P, E])
        rel_in = sb("rel_in", [P, NT, DH])
        rel_rep = sb("rel_rep", [P, NT, DH, H])
        wqk = sb("wqk", [P, 2, DH, H])
        relb = sb("relb", [P, L])
        c_in = sb("c_in", [B, 2, D])
        c_sig = sb("c_sig", [B, 2, D])
        c_t = sb("c_t", [P, 2, B])
        mods = sb("mods", [P, 13, B])
        mod_abs = sb("mod_abs", [P, 2, B])
        mod_sgn = sb("mod_sgn", [P, 2, B])
        sel = sb("sel", [P, E, P], BF16)
        gub_t = sb("gub_t", [P, 2, E])
        dbias = sb("dbias", [P, D])
        inv_s = sb("inv_s", [P, L])
        mhalf = sb("mhalf", [P, NT])
        veps = sb("veps", [P, NT])
        rstd = sb("rstd", [P, NT])
        vepsh = sb("vepsh", [P, NT])
        rstdh = sb("rstdh", [P, NT])
        vepsb = sb("vepsb", [P, NT])
        rstdb = sb("rstdb", [P, NT])
        fcol = sb("fcol", [P, CT])
        gcol = sb("gcol", [P, 2, CT])
        cos_r = sb("cos_r", [P, CT, L])
        sin_r = sb("sin_r", [P, CT, L])
        keep = sb("keep", [P, 2 * L])
        half_pi = sb("half_pi", [P, 1])
        magic = sb("magic", [P, 1])

        x_in = sb("x_in", [P, NT, D])
        xt = sb("xt", [P, L])
        cent = sb("cent", [P, L])
        centh = sb("centh", [P, L])
        sqh = sb("sqh", [P, L])
        sq = sb("sq", [P, L])
        ht = sb("ht", [P, L])
        mod_a = sb("mod_a", [P, 13])
        qk = sb("qk", [P, 2, L])
        qk_part = sb("qk_part", [P, 3, 2, L], BF16)
        hta = sb("hta", [P, L])
        mod_h = sb("mod_h", [P, 13])
        vt = sb("vt", [P, NT, H, VW])
        o_raw = sb("o_raw", [P, H // 4, L])
        q_rows = sb("q_rows", [75, H, L], BF16)
        k_rows = sb("k_rows", [75, H, L], BF16)
        smax = sb("smax", [P, NT, H])
        negm = sb("negm", [P, NT, H])
        mrest = sb("mrest", [P, NT, H])
        mpart = sb("mpart", [P, NT, 3, H], BF16)
        m_sb = sb("m_sb", [3 * H, L], BF16)
        prob = sb("prob", [P, NPT, 4, L])
        rden = sb("rden", [P, NT, H])
        o_tok = sb("o_tok", [P, NT, H, DH])
        o_t = sb("o_t", [P, L])
        ya = sb("ya", [P, L])
        x1 = sb("x1", [P, L])
        lg = sb("lg", [P, NT, TOPK + E])
        top8 = sb("top8", [P, NT, 8])
        repl = sb("repl", [P, NT, TOPK + E])
        lsh = sb("lsh", [P, NT, E])
        ex = sb("ex", [P, NT, E])
        exm = sb("exm", [P, NT, E])
        esum = sb("esum", [P, NT])
        rsum = sb("rsum", [P, NT])
        sc = sb("sc", [P, NT, P])
        srest = sb("srest", [P, NT, E])
        sc_part = sb("sc_part", [P, NT, P], BF16)
        sct = sb("sct", [P, L])
        sctb = sb("sctb", [P, L], BF16)
        sc_all = sb("sc_all", [P, E, L])
        sig = sb("sig", [P, NG, 2 * L])
        gsc = sb("gsc", [P, NG, 2 * L])
        slots = prob[:, :, :, :].rearrange("p s i q -> p (s i q)").rearrange("p (n c) -> p n c", c=2 * L)
        upc = slots[:, 0:NU, :]
        glu = slots[:, NU:NU + 2, :]
        x2 = sb("x2", [P, L])

        wmod = prob[:, :, :, :].rearrange("p s i q -> p (s i q)")[:, 0:12 * D].rearrange("p (l n) -> p l n", l=2)
        ffn_raw = sig[:, 0, 0:3 * D].rearrange("p (n c) -> p n c", n=3)
        bl = gsc[0:E, 0, 0:2 * D].rearrange("e (f g) -> e f g", g=2)
        bd = gsc[0:E, 0, 2 * D:4 * D].rearrange("e (g f) -> e g f", g=2)
        t_next = cent
        mhalf_w = sq

        mod_b = sb("mod_b", [P, 13])
        centb = sb("centb", [P, L])
        sqb = sb("sqb", [P, L])
        hb = sb("hb", [P, L + 1])
        turn = sb("turn", [P, 2 * L])
        frac = sb("frac", [P, 2, 2 * L])
        fabs = sb("fabs", [P, 2 * L])
        sin_t = sb("sin_t", [P, 2, 2, L + 1])
        cos_t = sb("cos_t", [P, 2, 2, L + 1])
        val = sc_all[:, 0:4, :].rearrange("p e t -> p (e t)").rearrange("p (n c) -> p n c", c=2 * L)
        prod = sb("prod", [P, 2, 4, 2 * L])
        x3 = sb("x3", [P, L])
        dif = sb("dif", [P, L])
        xr = sb("xr", [P, L])
        xk = sb("xk", [P, L])
        rsig = sb("rsig", [P, L])
        ksq = sb("ksq", [P, L])
        x4 = sb("x4", [P, L])
        xo = sb("xo", [P, NT, D])

        t_int = xr[:, :].bitcast(I32)
        t_f = xk

        ring = ctx.enter_context(nc.psum_tensor("ring", [P, 2, 1024], F32))
        pa = ctx.enter_context(nc.psum_tensor("pa", [P, 512], F32))
        pb_k = ctx.enter_context(nc.psum_tensor("pb_k", [P, 512], F32))
        pb_v = ctx.enter_context(nc.psum_tensor("pb_v", [P, 512], F32))
        pb = ctx.enter_context(nc.psum_tensor("pb", [P, 512], F32))
        o_ps = ring[:, 1, :].rearrange("p (n h d) -> p n h d", n=NT, h=H)

        S = {name: ctx.enter_context(nc.semaphore(name)) for name in PER}

        def setup_sem(name):
            return ctx.enter_context(nc.semaphore("set_" + name))

        ld_w, ld_mod, ld_gu, ld_bias, ld_small = (
            setup_sem(n) for n in ("ld_w", "ld_mod", "ld_gu", "ld_bias", "ld_small"))
        c_pool, c_act, c_pe, c_dve, c_fill = (
            setup_sem(n) for n in ("pool", "act", "pe", "dve", "fill"))
        N_W, N_SMALL = 9, 27

        def need(eng, name, b, k):
            v = b * PER[name] + k
            if not isinstance(v, int) or v > 0:
                eng.wait_ge(S[name], v)

        block = ctx.enter_context(nc.Block())

        @block.sync
        def _(sp):
            sp.dma_start(c_in[:, 0, :], c0).then_inc(ld_mod, 16)
            sp.dma_start(c_in[:, 1, :], c1).then_inc(ld_mod, 16)
            sp.dma_start(wmod[:, 0, :], wmod0).then_inc(ld_mod, 16)
            sp.dma_start(wmod[:, 1, :], wmod1).then_inc(ld_mod, 16)
            sp.dma_start(wqkv[:, :], Wqkv).then_inc(ld_w, 16)
            sp.dma_start(wout[:, :], Wout).then_inc(ld_w, 16)
            sp.dma_start(wrout[:, :], router_w).then_inc(ld_w, 16)
            sp.dma_start(wk[:, :], Wk).then_inc(ld_w, 16)
            sp.dma_start(wv[:, :], Wv).then_inc(ld_w, 16)
            sp.dma_start(wo[:, 0, :, :], Wo.rearrange("(k p) m -> p k m", p=P)).then_inc(ld_w, 16)
            for n, w in enumerate((W_r, W_k, W_v)):
                sp.dma_start(ffn_raw[:, n, :], w).then_inc(ld_w, 16)
            sp.dma_start(sc_all[:, :, :], gup.rearrange("e h f -> h e f")).then_inc(ld_gu, 16)
            sp.dma_start(wdown[:, :, :], down.rearrange("e i h -> i e h")).then_inc(ld_gu, 16)
            def load_x(b):
                sp.wait_ge(ld_gu, 32)
                need(sp, "xt_ps", b, 0)
                src = x[bass.ds(b, 1)] if not isinstance(b, int) else x[b:b + 1]
                sp.dma_start(x_in[:, :, :], src.rearrange("a (n p) f -> p (a n) f", p=P)).then_inc(S["x_in"], 16)

            def spread(b):
                sp.wait_ge(ld_gu, 32)
                need(sp, "part2", b, 1)
                need(sp, "den", b, 0)
                for a in range(3):
                    for c in range(3):
                        r = (a * 3 + c) * DH
                        for rows, n, m in ((q_rows, 0, a), (k_rows, 1, c)):
                            sp.dma_start(rows[r:r + DH, :, :],
                                         qk_part[:, m, n, :]).then_inc(S["qk_rows"], 16)

            def spread_max(b):
                need(sp, "m_sb", b, 1)
                sp.dma_start(q_rows[72:75, :, :], m_sb[:, :]).then_inc(S["m_rows"], 16)

            def store(b):
                sp.wait_ge(ld_gu, 32)
                need(sp, "xo", b, 1)
                dst = out[bass.ds(b, 1)] if not isinstance(b, int) else out[b:b + 1]
                sp.dma_start(dst.rearrange("a (n p) f -> p (a n) f", p=P), xo[:, :, :]).then_inc(S["out"], 16)

            def head(nx):
                load_x(nx)
                spread(nx)

            def step(a, b, nx):
                if nx is not None:
                    load_x(nx)
                if a is not None:
                    spread_max(a)
                if nx is not None:
                    spread(nx)
                if b is not None:
                    store(b)

            run(sp, head, step)
            sp.wait_ge(S["out"], 16 * B)

        @block.gpsimd
        def _(pool):
            for t in (ident, identb, sel):
                pool.memset(t[tuple(slice(None) for _ in t.shape)], 0.0).then_inc(c_pool, 1)
            pool.wait_ge(c_pool, 3)
            for t in (ident, identb):
                pool.affine_select(out=t[:, :], in_=t[:, :], compare_op=ALU.not_equal, fill=1.0, base=0,
                                   pattern=[[-1, P]], channel_multiplier=1).then_inc(c_pool, 1)
            for n in range(3):
                pool.wait_ge(c_pool, 5 + n)
                pool.affine_select(out=sel[:, :, :], in_=sel[:, :, :], compare_op=ALU.not_equal, fill=1.0,
                                   base=-16 * n, pattern=[[-1, E], [0, P]], channel_multiplier=1).then_inc(c_pool, 1)
            pool.iota(t_int[:, :], pattern=[[1, L]], base=0, channel_multiplier=0).then_inc(c_pool, 1)
            pool.wait_ge(ld_gu, 32)
            pool.tensor_copy(wgu[:, :, 0, :], sc_all[:, :, 0:L:2]).then_inc(c_pool, 1)
            pool.tensor_copy(wgu[:, :, 1, :], sc_all[:, :, 1:L:2]).then_inc(c_pool, 1)

            pool.wait_ge(c_dve, DVE_TRIG + 1)
            pool.tensor_tensor(inv_s[:, :], t_next[:, :], mhalf_w[:, :], ALU.pow).then_inc(c_pool, 1)

            def deviation(b, n, v, r):
                need(pool, "veps" + n, b, 1)
                pool.tensor_tensor(r[:, :], v[:, :], mhalf[:, 0:NT], ALU.pow).then_inc(S["rstd" + n], 1)

            def rest_q(b):
                need(pool, "part0", b, 1)
                need(pool, "q_sb", b, 1)
                need(pool, "k_sb", b, 1)
                pool.tensor_tensor(qk[:, :, :], qk[:, :, :], qk_part[:, 0, :, :], ALU.subtract).then_inc(S["rest0"], 1)

            def rest_q_2(b):
                need(pool, "part1", b, 1)
                need(pool, "rest0", b, 1)
                pool.tensor_tensor(qk_part[:, 2, :, :], qk[:, :, :], qk_part[:, 1, :, :], ALU.subtract).then_inc(S["part2"], 1)

            def residual1(b):
                need(pool, "ya", b, 1)
                need(pool, "xt", b, 1)
                need(pool, "x2", b, 0)
                pool.tensor_tensor(x1[:, :], xt[:, :], ya[:, :], ALU.add).then_inc(S["x1"], 1)

            def expert_pair(b, n):
                sca = sc_all[:, 2 * n:2 * n + 2, :].rearrange("p e t -> p (e t)")
                if n % 2 == 0:
                    need(pool, "bc", b, n // 2 + 1)
                need(pool, "sig", b, n + 1)
                pool.tensor_tensor(gsc[:, n % NG, :], gsc[:, n % NG, :], sca, ALU.mult).then_inc(S["gsc"], 1)
                if n:
                    expert_last(b, n - 1)

            def expert_last(b, n):
                if n in BY_DVE:
                    return
                need(pool, "act", b, n)
                need(pool, "upc", b, n + 1)
                need(pool, "gl", b, n + 1)
                pool.tensor_tensor(upc[:, n % NU, :], upc[:, n % NU, :], glu[:, n % 2, :], ALU.mult).then_inc(S["act"], 1)

            def memory_in(b, c):
                h = c % 2
                need(pool, "val", b, c + 1)
                need(pool, "wo", b, c - 1)
                pool.tensor_tensor(prod[:, h, 0, :], val[:, h, :],
                                   cos_r[:, 2 * c:2 * c + 2, :].rearrange("p k t -> p (k t)"), ALU.mult).then_inc(S["in1"], 1)
                pool.tensor_tensor(prod[:, h, 1, :], val[:, h, :],
                                   sin_r[:, 2 * c:2 * c + 2, :].rearrange("p k t -> p (k t)"), ALU.mult).then_inc(S["in2"], 1)

            def memory_out(b, c):
                h = c % 2
                for n, t in ((0, cos_r), (1, sin_r)):
                    need(pool, "cu" + str(n + 1), b, c + 1)
                    pool.tensor_tensor(prod[:, h, n, :], prod[:, h, n, :],
                                       t[:, 2 * c:2 * c + 2, :].rearrange("p k t -> p (k t)"), ALU.mult).then_inc(S["pr" + str(n + 1)], 1)
                need(pool, "pr1", b, c + 1)
                need(pool, "pr2", b, c + 1)
                pool.tensor_tensor(prod[:, h, 0, :], prod[:, h, 0, :], prod[:, h, 1, :], ALU.add).then_inc(S["sum12"], 1)

            def head_1(nx):
                deviation(nx, "1", vepsh, rstdh)

            def head(nx):
                head_1(nx)
                rest_q(nx)
                rest_q_2(nx)

            def step(a, b, nx):
                on_a, on_b, on_x = a is not None, b is not None, nx is not None
                if on_b:
                    deviation(b, "3", vepsb, rstdb)
                    memory_in(b, 0)
                    memory_in(b, 1)
                    memory_out(b, 0)
                    memory_out(b, 1)
                    memory_in(b, 2)
                    memory_out(b, 2)
                    memory_in(b, 3)
                if on_b:
                    memory_out(b, 3)
                if on_a:
                    residual1(a)
                if on_a:
                    deviation(a, "2", veps, rstd)
                if on_x:
                    head_1(nx)
                    rest_q(nx)
                if on_b:
                    deviation(b, "4", vepsb, rstdb)
                if on_x:
                    rest_q_2(nx)
                if on_a:
                    for n in range(E // 2):
                        expert_pair(a, n)
                    expert_last(a, E // 2 - 1)

            run(pool, head, step)

        @block.tensor
        def _(pe):
            mm = nc.tensor.matmul
            tr = nc.tensor.transpose
            pe.wait_ge(c_pool, 5)
            pe.wait_ge(c_dve, 1)
            for l in range(2):
                last = tr(pa[:, l * B:(l + 1) * B], c_in[:, l, :], ident[0:B, 0:B])
            last.then_inc(c_pe, 1)
            pe.wait_ge(c_dve, 2)
            for l in range(2):
                for k in range(6):
                    last = mm(pa[:, 64 + (l * 6 + k) * B:64 + (l * 6 + k + 1) * B], lhsT=wmod[:, l, k * D:(k + 1) * D],
                              rhs=c_t[:, l, :], start=True, stop=True, skip_group_check=True)
            last.then_inc(c_pe, 1)
            pe.wait_ge(ld_w, 16 * N_W)
            for n in range(3):
                last = tr(pb_k[:, n * D:(n + 1) * D], ffn_raw[:, n, :], ident[:, :])
            last.then_inc(c_pe, 1)
            pe.wait_ge(c_dve, 3)
            for n in range(NT):
                last = tr(pb_v[:, n * P:(n + 1) * P], rel_rep[:, n, :, :].rearrange("p d h -> p (d h)"), ident[:, :])
            last.then_inc(c_pe, 1)
            pe.wait_ge(c_dve, DVE_BIAS)
            for g in range(2):
                last = tr(pb[:, 448 + g * E:448 + (g + 1) * E], bd[:, g, :], ident[0:E, 0:E])
            last.then_inc(c_pe, 1)
            pe.wait_ge(c_dve, DVE_SETUP)

            def mean(b, n, src, src_sem, ps, free):
                need(pe, src_sem, b, 1)
                for name, c, k in free:
                    need(pe, name, c, k)
                mm(ps[:, 0:L], lhsT=mean_w[:, :], rhs=src, start=True, stop=True,
                   skip_group_check=True).then_inc(S["mean" + n], 1)

            def variance(b, n, ps, sqt):
                need(pe, "sq" + n, b, 1)
                for t in range(NT):
                    last = mm(ps[:, L + t:L + t + 1], lhsT=sqt[:, t * P:(t + 1) * P], rhs=mean_w[:, 0:1], start=True,
                              stop=True, skip_group_check=True)
                last.then_inc(S["var" + n], 1)

            def deviation(b, n, ps, rs):
                need(pe, "rstd" + n, b, 1)
                for t in range(NT):
                    last = mm(ps[:, L + t * P:L + (t + 1) * P], lhsT=rs[:, t:t + 1].to_broadcast([P, P]), rhs=ident[:, :],
                              start=True, stop=True, skip_group_check=True)
                last.then_inc(S["rbc" + n], 1)

            def head_1(nx):
                need(pe, "x_in", nx, 16)
                need(pe, "turn", nx - 1, 0)
                need(pe, "frac", nx - 1, 0)
                for n in range(NT):
                    last = tr(pb_k[:, n * P:(n + 1) * P], x_in[:, n, :], ident[:, :])
                last.then_inc(S["xt_ps"], 1)

            def head_2(nx):
                mean(nx, "1", xt[:, :], "xt", pb_v, (("val", nx - 1, 0),))

            def head_3(nx):
                variance(nx, "1", pb_v, sqh)

            def head_4(nx):
                deviation(nx, "1", pb_v, rstdh)

            def head_5(nx):
                need(pe, "h1", nx, 1)
                for n in range(2):
                    last = mm(pb_k[:, n * L:(n + 1) * L], lhsT=wqk[:, n, :, :].rearrange("p d h -> p (d h)"), rhs=hta[:, :],
                              start=True, stop=True, skip_group_check=True)
                last.then_inc(S["qk_ps"], 1)
                for n in range(NT):
                    last = mm(pb_v[:, n * D:(n + 1) * D], lhsT=hta[:, n * P:(n + 1) * P],
                              rhs=wqkv[:, 2 * D:3 * D], start=True, stop=True, skip_group_check=True)
                last.then_inc(S["v_ps"], 1)

            def scores(b, n):
                if n == 0:
                    need(pe, "qk_rows", b, 16 * 18)
                if n < 2:
                    need(pe, "gc", b, 0)
                    need(pe, "upr", b, 0)
                if n >= 2:
                    need(pe, "s_max", b, n - 1)
                for j in range(4):
                    h = 4 * (n % 4) + j
                    last = mm(ring[:, n % 2, j * L:(j + 1) * L], lhsT=q_rows[0:72, h, (n // 4) * P:(n // 4 + 1) * P],
                              rhs=k_rows[0:72, h, :], start=True, stop=True, skip_group_check=True)
                last.then_inc(S["s_ps"], 1)

            def turn_max(b):
                pe.wait_ge(c_dve, DVE_SETUP)
                need(pe, "mp2", b, 1)
                for n in range(NT):
                    last = tr(ring[0:3 * H, 0, :].bitcast(BF16)[:, n * P:(n + 1) * P],
                              mpart[:, n, :, :].rearrange("p a h -> p (a h)"), identb[:, :])
                last.then_inc(S["m_ps"], 1)

            def scores_t(b, n):
                if n == 0:
                    need(pe, "m_rows", b, 16)
                    need(pe, "s_max", b, ST)
                if n == 1:
                    need(pe, "m_sb", b, 1)
                if n >= 2:
                    need(pe, "prob", b, n - 1)
                for j in range(4):
                    h = 4 * (n // 2) + j
                    last = mm(ring[:, (n + 1) % 2, j * L:(j + 1) * L], lhsT=k_rows[0:75, h, (n % 2) * P:(n % 2 + 1) * P],
                              rhs=q_rows[0:75, h, :], start=True, stop=True, skip_group_check=True)
                last.then_inc(S["st_ps"], 1)

            def values(b, n):
                if n == 0:
                    need(pe, "y2", b, 0)
                if n == 4:
                    need(pe, "o_raw", b, 1)
                need(pe, "prob", b, n + 1)
                o = (n // 2) % 2 * L
                for j in range(4):
                    last = mm(pa[32 * j:32 * (j + 1), o:o + L], lhsT=vt[:, n % 2, 4 * (n // 2) + j, :],
                              rhs=prob[:, n % NPT, j, :], start=(n % 2 == 0), stop=(n % 2 == 1), skip_group_check=True)
                last.then_inc(S["pv"], 1)

            def turn_values(b):
                need(pe, "o_raw", b, 2)
                need(pe, "prob", b, ST - 1)
                for n in range(NT):
                    for g in range(H // 4):
                        last = tr(ring[:, 1, n * 512 + g * P:n * 512 + (g + 1) * P], o_raw[:, g, n * P:(n + 1) * P], ident[:, :])
                last.then_inc(S["or_ps"], 1)

            def attn_out_1(b):
                need(pe, "o_sb", b, NT)
                need(pe, "prob", b, ST)
                for n in range(NT):
                    last = tr(ring[:, 0, n * P:(n + 1) * P], o_tok[:, n, :, :].rearrange("p h d -> p (h d)"), ident[:, :])
                last.then_inc(S["ot_ps"], 1)

            def attn_out_2(b):
                need(pe, "ot_sb", b, 1)
                mm(ring[:, 1, 0:L], lhsT=wout[:, :], rhs=o_t[:, :], start=True, stop=True,
                   skip_group_check=True).then_inc(S["y_ps"], 1)

            def router(b):
                need(pe, "h2", b, 1)
                for n in range(NT):
                    last = mm(ring[:, 0, n * E:(n + 1) * E], lhsT=ht[:, n * P:(n + 1) * P], rhs=wrout[:, :],
                              start=True, stop=True, skip_group_check=True)
                last.then_inc(S["lg_ps"], 1)

            def turn_scores(b):
                need(pe, "sp2", b, 1)
                need(pe, "sc", b, 1)
                need(pe, "ya", b, 1)
                for n in range(NT):
                    tr(ring[:, 1, n * P:(n + 1) * P], sc[:, n, :], ident[:, :])
                for n in range(NT):
                    last = tr(ring[:, 1, 512:1024].bitcast(BF16)[:, n * P:(n + 1) * P], sc_part[:, n, :], identb[:, :])
                last.then_inc(S["sct_ps"], 1)

            def broadcast(b, n):
                if n == 0:
                    need(pe, "sctb", b, 1)
                    need(pe, "lg", b, 1)
                if n == 1:
                    need(pe, "sctf", b, 1)
                if n >= 2:
                    need(pe, "bc", b, n - 1)
                for j in range(4):
                    last = mm(ring[:, n % 2, j * L:(j + 1) * L], lhsT=sel[:, 4 * n + j, :], rhs=sctb[:, :],
                              start=True, stop=True, skip_group_check=True)
                last.then_inc(S["bc_ps"], 1)

            def gate_up(b, n):
                if n < 2:
                    need(pe, "bc", b, n + 3)
                else:
                    need(pe, "gc", b, 2 * (n - 1))
                    need(pe, "upr", b, 2 * (n - 1))
                for g in range(2):
                    for j in range(2):
                        last = mm(ring[:, n % 2, g * 512 + j * L:g * 512 + (j + 1) * L], lhsT=wgu[:, 2 * n + j, g, :],
                                  rhs=ht[:, :], start=True, stop=True, skip_group_check=True)
                last.then_inc(S["gu_ps"], 1)

            def down_bias(b):
                need(pe, "norm2", b, 1)
                need(pe, "sctf", b, 1)
                mm(pa[:, 0:L], lhsT=dbias[:, :], rhs=sct[:, :], start=True, stop=False, skip_group_check=True)

            def down_pair(b, n):
                need(pe, "act", b, n + 1)
                for j in range(2):
                    last = mm(pa[:, 0:L], lhsT=wdown[:, 2 * n + j, :], rhs=upc[:, n % NU, j * L:(j + 1) * L],
                              start=False, stop=(n == 7 and j == 1), skip_group_check=True)
                last.then_inc(S["dn"], 1)

            def phases(b, c):
                if c == 0:
                    need(pe, "h3", b, 1)
                    k = later(b)
                    need(pe, "q_sb", b, k)
                    need(pe, "k_sb", b, k)
                    need(pe, "v_sb", b, NT * k)
                    need(pe, "ksq", b, 0)
                    need(pe, "rsig", b, 0)
                    need(pe, "xo", b, 0)
                else:
                    need(pe, "turn", b, c)
                    need(pe, "frac", b, c)
                for j in range(2):
                    last = mm(pb_k[:, j * L:(j + 1) * L], lhsT=wk[:, (2 * c + j) * P:(2 * c + j + 1) * P], rhs=hb[:, 1:L + 1],
                              start=True, stop=True, skip_group_check=True)
                last.then_inc(S["k_ps"], 1)

            def phase_values(b, c):
                if c:
                    need(pe, "val", b, c)
                for j in range(2):
                    last = mm(pb_v[:, j * L:(j + 1) * L], lhsT=wv[:, (2 * c + j) * P:(2 * c + j + 1) * P], rhs=hb[:, 1:L + 1],
                              start=True, stop=True, skip_group_check=True)
                last.then_inc(S["v2_ps"], 1)

            def memory_wo(b, c):
                if c == 0:
                    need(pe, "norm3", b, 1)
                for g, s in ((0, "sum12"), (1, "sum34")):
                    need(pe, s, b, c + 1)
                    for j in range(2):
                        last = mm(pb[:, 0:L], lhsT=wo[:, g, 2 * c + j, :], rhs=prod[:, c % 2, 2 * g, j * L:(j + 1) * L],
                                  start=(c == 0 and g == 0 and j == 0), stop=(c == CC - 1 and g == 1 and j == 1),
                                  skip_group_check=True)
                last.then_inc(S["wo"], 1)

            def mix_1(b, nx):
                need(pe, "xr", b, 1)
                need(pe, "frac", b, CC)
                need(pe, "turn", b, CC)
                if nx is not None:
                    need(pe, "q_sb", nx, 1)
                    need(pe, "k_sb", nx, 1)
                mm(pb_k[:, 0:L], lhsT=ffn_w[:, 0, :], rhs=xr[:, :], start=True, stop=True, skip_group_check=True)
                need(pe, "xk", b, 1)
                mm(pb_k[:, L:2 * L], lhsT=ffn_w[:, 1, :], rhs=xk[:, :], start=True, stop=True,
                   skip_group_check=True).then_inc(S["rk_ps"], 1)

            def mix_2(b, nx):
                need(pe, "ksq", b, 1)
                if nx is not None:
                    need(pe, "v_sb", nx, NT)
                need(pe, "val", b, CC)
                mm(pb_v[:, 0:L], lhsT=ffn_w[:, 2, :], rhs=ksq[:, :], start=True, stop=True,
                   skip_group_check=True).then_inc(S["vv_ps"], 1)

            def mix_3(b):
                need(pe, "x4", b, 1)
                for n in range(NT):
                    last = tr(pb_v[:, L + n * P:L + (n + 1) * P], x4[:, n * P:(n + 1) * P], ident[:, :])
                last.then_inc(S["xo_ps"], 1)

            def head(nx):
                head_1(nx)
                head_2(nx)
                head_3(nx)
                head_4(nx)
                head_5(nx)
                scores(nx, 0)
                scores(nx, 1)

            def step(a, b, nx):
                on_a, on_b, on_x = a is not None, b is not None, nx is not None
                if on_b:
                    mean(b, "3", x2[:, :], "x2", pb, (("norm4", b, 0),))
                    variance(b, "3", pb, sqb)
                if on_a:
                    scores(a, 2)
                if on_b:
                    deviation(b, "3", pb, rstdb)
                if on_a:
                    scores(a, 3)
                    scores(a, 4)
                if on_b:
                    phases(b, 0)
                if on_a:
                    scores(a, 5)
                if on_b:
                    phase_values(b, 0)
                if on_a:
                    scores(a, 6)
                if on_b:
                    phases(b, 1)
                if on_a:
                    scores(a, 7)
                if on_b:
                    phase_values(b, 1)
                if on_a:
                    turn_max(a)
                if on_b:
                    phases(b, 2)
                    phase_values(b, 2)
                if on_a:
                    scores_t(a, 0)
                    scores_t(a, 1)
                if on_b:
                    memory_wo(b, 0)
                    phases(b, 3)
                    phase_values(b, 3)
                if on_a:
                    values(a, 0)
                    scores_t(a, 2)
                    values(a, 1)
                    scores_t(a, 3)
                    values(a, 2)
                    scores_t(a, 4)
                    values(a, 3)
                if on_b:
                    memory_wo(b, 1)
                if on_a:
                    scores_t(a, 5)
                    values(a, 4)
                    scores_t(a, 6)
                    values(a, 5)
                    scores_t(a, 7)
                    values(a, 6)
                    values(a, 7)
                if on_a:
                    turn_values(a)
                if on_x:
                    head_1(nx)
                if on_a:
                    attn_out_1(a)
                    attn_out_2(a)
                if on_b:
                    memory_wo(b, 2)
                if on_a:
                    mean(a, "2", x1[:, :], "x1", pa, ())
                if on_x:
                    head_2(nx)
                if on_a:
                    variance(a, "2", pa, sq)
                if on_x:
                    head_3(nx)
                if on_a:
                    deviation(a, "2", pa, rstd)
                if on_x:
                    head_4(nx)
                if on_a:
                    router(a)
                if on_b:
                    memory_wo(b, 3)
                if on_x:
                    head_5(nx)
                if on_b:
                    mean(b, "4", x3[:, :], "x3", pb, ())
                if on_a:
                    turn_scores(a)
                    broadcast(a, 0)
                if on_b:
                    variance(b, "4", pb, sqb)
                if on_a:
                    broadcast(a, 1)
                if on_b:
                    deviation(b, "4", pb, rstdb)
                if on_a:
                    broadcast(a, 2)
                    broadcast(a, 3)
                    down_bias(a)
                    gate_up(a, 0)
                if on_a:
                    gate_up(a, 1)
                if on_b:
                    mix_1(b, nx)
                if on_a:
                    gate_up(a, 2)
                    gate_up(a, 3)
                if on_b:
                    mix_2(b, nx)
                if on_a:
                    for n in range(4, E // 2):
                        gate_up(a, n)
                        down_pair(a, n - 4)
                        if on_b and n == 5:
                            mix_3(b)
                    down_pair(a, 4)
                    down_pair(a, 5)
                    down_pair(a, 6)
                    down_pair(a, 7)
                    if on_x:
                        scores(nx, 0)
                        scores(nx, 1)
                elif on_b:
                    mix_3(b)

            run(pe, head, step)

        @block.scalar
        def _(act):
            af = nc.scalar.activation
            for n in range(2):
                for d in range(DH):
                    act.dma_start(bcol[d * H:(d + 1) * H, n:n + 1],
                                  bqkv[n * D:(n + 1) * D].rearrange("(h d) -> h d", d=DH)[:, d:d + 1], allow_slow_non_contiguous=True).then_inc(ld_small, 16)
            act.dma_start(bcol[:, 3:4], bout.rearrange("(k p) -> p k", p=P), allow_slow_non_contiguous=True).then_inc(ld_small, 16)
            act.dma_start(mu[:, 0:1], mu_r.rearrange("(k p) -> p k", p=P), allow_slow_non_contiguous=True).then_inc(ld_small, 16)
            act.dma_start(mu[:, 1:2], mu_k.rearrange("(k p) -> p k", p=P), allow_slow_non_contiguous=True).then_inc(ld_small, 16)
            act.dma_start(vbias[:, :], bqkv[2 * D:3 * D].rearrange("(a n) -> a n", a=1).to_broadcast([P, D])).then_inc(ld_small, 16)
            act.dma_start(rbias[:, :], router_b.rearrange("(a n) -> a n", a=1).to_broadcast([P, E])).then_inc(ld_small, 16)
            act.dma_start(fcol[:, :], freqs.rearrange("(k a) d -> (a d) k", a=2), allow_slow_non_contiguous=True).then_inc(ld_small, 16)
            for g in range(2):
                for a in range(2):
                    act.dma_start(gcol[64 * a:64 * (a + 1), g, :],
                                  gate[a:H:2, g:g + 1].rearrange("k a -> a k").to_broadcast([64, CT]), allow_slow_non_contiguous=True).then_inc(ld_small, 16)
            act.dma_start(bl[:, :, :], gub.rearrange("e (f g) -> e f g", g=2)).then_inc(ld_bias, 16)
            act.wait_ge(c_fill, 1)
            act.dma_start(dbias[0:E, :], downb).then_inc(ld_small, 16)
            act.dma_start(rel_in[1:P, 0, :], rel_emb[0:P - 1, :]).then_inc(ld_bias, 16)
            act.dma_start(rel_in[:, 1, :], rel_emb[P - 1:2 * P - 1, :]).then_inc(ld_bias, 16)
            act.wait_ge(ld_mod, 64)
            af(c_sig[:, :, :], c_in[:, :, :], ACT.Sigmoid).then_inc(c_act, 1)
            act.wait_ge(c_dve, DVE_TRIG)
            ang = prod[:, 0, :, :].rearrange("p a b -> p (a b)")
            tmp = prod[:, 1, :, :].rearrange("p a b -> p (a b)")
            af(sin_r[:, :, :].rearrange("p k t -> p (k t)"), ang, ACT.Sin).then_inc(c_act, 1)
            af(tmp, ang, ACT.Abs).then_inc(c_act, 1)
            act.wait_ge(c_act, 3)
            af(cos_r[:, :, :].rearrange("p k t -> p (k t)"), tmp, ACT.Sin, scale=-1.0, bias=half_pi[:, 0:1]).then_inc(c_act, 1)
            act.wait_ge(c_dve, DVE_SETUP)

            def square(b, n, c, s):
                need(act, "cent" + n, b, 1)
                af(s[:, :], c[:, :], ACT.Square).then_inc(S["sq" + n], 1)

            def modulate(b, n, src, dst, mod, k):
                need(act, "norm" + n, b, 1)
                af(dst, src[:, :], ACT.Identity, scale=mod[:, k + 1:k + 2], bias=mod[:, k:k + 1]).then_inc(S["h" + n], 1)

            def head_1(b):
                square(b, "1", centh, sqh)

            def head_2(b):
                need(act, "mod_h", b, 1)
                need(act, "v_ps", b, 0)
                modulate(b, "1", centh, hta[:, :], mod_h, 0)

            def part(b):
                need(act, "q_sb", b, 1)
                need(act, "k_sb", b, 1)
                need(act, "qk_rows", b, 0)
                af(qk_part[:, 0, :, :], qk[:, :, :], ACT.Copy).then_inc(S["part0"], 1)

            def part_2(b):
                need(act, "rest0", b, 1)
                af(qk_part[:, 1, :, :], qk[:, :, :], ACT.Copy).then_inc(S["part1"], 1)

            def copy_max(b):
                need(act, "m_ps", b, 1)
                need(act, "m_rows", b, 0)
                af(m_sb[:, :], ring[0:3 * H, 0, :].bitcast(BF16)[:, 0:L], ACT.Copy).then_inc(S["m_sb"], 1)

            def exps(b, n):
                need(act, "st_ps", b, n + 1)
                if n == 0:
                    need(act, "dn", b, 0)
                if n < NPT:
                    need(act, "pv", b, 0)
                else:
                    need(act, "pv", b, n - NPT + 1)
                af(prob[:, n % NPT, :, :].rearrange("p i q -> p (i q)"), ring[:, (n + 1) % 2, :],
                   ACT.Exp).then_inc(S["prob"], 1)

            def copy_values(b, n):
                need(act, "pv", b, 4 * n + 4)
                need(act, "or_ps", b, 0)
                af(o_raw[:, 2 * n:2 * n + 2, :].rearrange("p g q -> p (g q)"), pa[:, :], ACT.Copy).then_inc(S["o_raw"], 1)

            def attn_tail(b):
                need(act, "ot_ps", b, 1)
                need(act, "y_ps", b, 0)
                af(o_t[:, :], ring[:, 0, 0:L], ACT.Copy).then_inc(S["ot_sb"], 1)
                need(act, "y_ps", b, 1)
                need(act, "x1", b, 0)
                need(act, "mod_a", b, 1)
                af(ya[:, :], ring[:, 1, 0:L], ACT.Identity, scale=mod_a[:, 2:3], bias=mod_a[:, 12:13]).then_inc(S["ya"], 1)

            def second_norm_1(b):
                square(b, "2", cent, sq)

            def second_norm_2(b):
                modulate(b, "2", cent, ht[:, :], mod_a, 3)

            def route(b):
                need(act, "shift", b, 1)
                need(act, "exm", b, 0)
                af(ex[:, :, :], lsh[:, :, :], ACT.Exp).then_inc(S["ex"], 1)

            def copy_scores(b):
                need(act, "sct_ps", b, 1)
                need(act, "bc_ps", b, 0)
                af(sctb[:, :], ring[:, 1, 512:1024].bitcast(BF16)[:, 0:L], ACT.Copy).then_inc(S["sctb"], 1)
                need(act, "dn", b, 0)
                af(sct[:, :], ring[:, 1, 0:L], ACT.Copy).then_inc(S["sctf"], 1)

            def copy_broadcast(b, n):
                need(act, "bc_ps", b, n + 1)
                need(act, "gsc", b, 0)
                for k in range(4):
                    need(act, "in" + str(k + 1), b, 0)
                af(sc_all[:, 4 * n:4 * n + 4, :].rearrange("p e t -> p (e t)"), ring[:, n % 2, :],
                   ACT.Copy).then_inc(S["bc"], 1)

            def up(b, n):
                need(act, "gu_ps", b, n + 1)
                need(act, "dn", b, n - NU + 1)
                for j in range(2):
                    af(upc[:, n % NU, j * L:(j + 1) * L], ring[:, n % 2, 512 + j * L:512 + (j + 1) * L], ACT.Identity,
                       bias=gub_t[:, 1, 2 * n + j:2 * n + j + 1]).then_inc(S["upr"], 1)

            def sigmoid(b, n):
                need(act, "gc", b, 2 * n + 2)
                need(act, "gl", b, n - NG + 1)
                af(sig[:, n % NG, :], gsc[:, n % NG, :], ACT.Sigmoid, scale=ALPHA).then_inc(S["sig"], 1)

            def head_b(b):
                square(b, "3", centb, sqb)
                need(act, "dif", b, 0)
                need(act, "xr", b, 0)
                need(act, "xk", b, 0)
                need(act, "mod_b", b, 1)
                modulate(b, "3", centb, hb[:, 1:L + 1], mod_b, 6)

            def phase(b, c):
                need(act, "k_ps", b, c + 1)
                need(act, "frac", b, c)
                af(turn[:, :], pb_k[:, :], ACT.Identity, bias=magic[:, 0:1]).then_inc(S["turn"], 1)
                need(act, "v2_ps", b, c + 1)
                for n in range(4):
                    need(act, "in" + str(n + 1), b, c - 1)
                need(act, "gsc", b, E // 2)
                af(val[:, c % 2, :], pb_v[:, :], ACT.Copy).then_inc(S["val"], 1)

            def tables(b, c):
                h = c % 2
                need(act, "frac", b, c + 1)
                need(act, "pr4", b, c - 1)
                need(act, "in4", b, c - 1)
                af(sin_t[:, h, :, 1:L + 1], frac[:, h, :].rearrange("p (k t) -> p k t", k=2), ACT.Sin,
                   scale=-TWO_PI_IN).then_inc(S["sin"], 1)
                need(act, "cos", b, c)
                af(fabs[:, :], frac[:, h, :], ACT.Abs).then_inc(S["fabs"], 1)
                need(act, "fabs", b, c + 1)
                need(act, "pr3", b, c - 1)
                need(act, "in3", b, c - 1)
                af(cos_t[:, h, :, 1:L + 1], fabs[:, :].rearrange("p (k t) -> p k t", k=2), ACT.Sin,
                   scale=-TWO_PI_IN, bias=half_pi[:, 0:1]).then_inc(S["cos"], 1)

            def fourth_norm_1(b):
                square(b, "4", centb, sqb)

            def fourth_norm_2(b):
                modulate(b, "4", centb, hb[:, 1:L + 1], mod_b, 9)

            def mix_1(b):
                need(act, "rk_ps", b, 1)
                need(act, "rv", b, 0)
                af(rsig[:, :], pb_k[:, 0:L], ACT.Sigmoid).then_inc(S["rsig"], 1)
                need(act, "vv_ps", b, 0)
                af(ksq[:, :], pb_k[:, L:2 * L], ACT.Relu).then_inc(S["krel"], 1)
                need(act, "krel", b, 1)
                af(ksq[:, :], ksq[:, :], ACT.Square).then_inc(S["ksq"], 1)

            def mix_2(b):
                need(act, "xo_ps", b, 1)
                need(act, "out", b, 0)
                af(xo[:, :, :].rearrange("p n f -> p (n f)"), pb_v[:, L:2 * L], ACT.Copy).then_inc(S["xo"], 1)

            def head(nx):
                head_1(nx)
                head_2(nx)
                part(nx)
                part_2(nx)

            def step(a, b, nx):
                on_a, on_b, on_x = a is not None, b is not None, nx is not None
                if on_b:
                    head_b(b)
                    phase(b, 0)
                    tables(b, 0)
                if on_a:
                    copy_max(a)
                if on_b:
                    for c in (1, 2):
                        phase(b, c)
                        tables(b, c)
                if on_a:
                    for n in range(4):
                        exps(a, n)
                if on_b:
                    phase(b, 3)
                if on_a:
                    exps(a, 4)
                    copy_values(a, 0)
                    for n in range(5, ST):
                        exps(a, n)
                    copy_values(a, 1)
                if on_b:
                    tables(b, 3)
                if on_a:
                    attn_tail(a)
                    second_norm_1(a)
                if on_x:
                    head_1(nx)
                if on_a:
                    second_norm_2(a)
                if on_x:
                    head_2(nx)
                if on_a:
                    route(a)
                if on_x:
                    part(nx)
                if on_a:
                    copy_scores(a)
                if on_b:
                    fourth_norm_1(b)
                if on_a:
                    copy_broadcast(a, 0)
                if on_x:
                    part_2(nx)
                if on_a:
                    copy_broadcast(a, 1)
                    copy_broadcast(a, 2)
                if on_b:
                    fourth_norm_2(b)
                if on_a:
                    copy_broadcast(a, 3)
                    for n in (0, 1):
                        up(a, n)
                        sigmoid(a, n)
                if on_b:
                    mix_1(b)
                if on_a:
                    for n in (2, 3, 4, 5):
                        up(a, n)
                        sigmoid(a, n)
                if on_b:
                    mix_2(b)
                if on_a:
                    for n in (6, 7):
                        up(a, n)
                        sigmoid(a, n)

            run(act, head, step)

        @block.vector
        def _(dve):
            tt = nc.vector.tensor_tensor
            ts = nc.vector.tensor_scalar
            stt = nc.vector.scalar_tensor_tensor
            count = [0]

            def done(ins, wait=True):
                count[0] += 1
                ins.then_inc(c_dve, 1)
                if wait:
                    dve.wait_ge(c_dve, count[0])

            dve.memset(mean_w[:, :], 1.0 / D)
            dve.memset(q_rows[64:75, :, :], 1.0)
            dve.memset(k_rows[64:75, :, :], 1.0)
            dve.memset(vt[:, :, :, DH + 1:VW], 0.0)
            dve.memset(vt[:, :, :, DH:DH + 1], 1.0)
            dve.memset(lg[:, :, 0:TOPK], BIG)
            dve.memset(sc[:, :, :], 0.0)
            dve.memset(sc_part[:, :, :], 0.0)
            dve.memset(hb[:, 0:1], 0.0)
            dve.memset(sin_t[:, :, :, 0:1], 0.0)
            dve.memset(cos_t[:, :, :, 0:1], 0.0)
            dve.memset(keep[:, :], 1.0)
            dve.memset(half_pi[:, :], TWO_PI / 4)
            dve.memset(magic[:, :], MAGIC)
            dve.memset(rel_in[:, :, :], 0.0)
            dve.memset(mhalf[:, :], -0.5)
            dve.memset(mhalf_w[:, :], -0.5)
            dve.memset(dbias[:, :], 0.0).then_inc(c_fill, 1)
            dve.wait_ge(c_act, 1)
            done(tt(c_in[:, :, :], c_in[:, :, :], c_sig[:, :, :], ALU.mult))
            dve.wait_ge(c_pe, 1)
            done(nc.vector.tensor_copy(c_t[:, :, :].rearrange("p l b -> p (l b)"), pa[:, 0:2 * B]))
            dve.wait_ge(ld_bias, 48)
            done(nc.vector.tensor_copy(rel_rep[:, :, :, :], rel_in[:, :, :].rearrange("p n (d a) -> p n d a", a=1)
                                       .to_broadcast([P, NT, DH, H])))
            dve.memset(keep[:, 0:2 * L:L], 0.0)
            ang = prod[:, 0, :, :].rearrange("p a b -> p (a b)")
            tmp = prod[:, 1, :, :].rearrange("p a b -> p (a b)")
            dve.wait_ge(c_pool, 9)
            done(nc.vector.tensor_copy(t_f[:, :], t_int[:, :]))
            dve.wait_ge(ld_small, 16 * N_SMALL)
            for k in range(CT):
                last = ts(ang[:, k * L:(k + 1) * L], t_f[:, :], fcol[:, k:k + 1], None, ALU.mult)
            done(last)
            done(ts(tmp, ang, 1.0 / TWO_PI, MAGIC, ALU.mult, ALU.add))
            done(ts(tmp, tmp, MAGIC, None, ALU.subtract))
            for c in (C1, C2, C3):
                done(stt(out=ang, in0=tmp, scalar=-c, in1=ang, op0=ALU.mult, op1=ALU.add))
            done(ts(ang, ang, PI_IN, -PI_IN, ALU.min, ALU.max))
            assert count[0] == DVE_TRIG
            done(ts(t_next[:, :], t_f[:, :], 1.0, None, ALU.add))
            dve.wait_ge(ld_w, 16 * N_W)
            for g in (1, 0):
                for k in range(CT):
                    last = ts(wo[:, g, k, :], wo[:, 0, k, :], gcol[:, g, k:k + 1], None, ALU.mult)
            done(last)
            done(nc.vector.tensor_copy(bd[:, :, :], bl[:, :, :].rearrange("e f g -> e g f")))
            done(ts(bd[:, 1, :], bd[:, 1, :], 1.0, None, ALU.add))
            assert count[0] == DVE_BIAS
            dve.wait_ge(c_pe, 2)
            done(nc.vector.tensor_copy(mods[:, 0:12, :].rearrange("p k b -> p (k b)"), pa[:, 64:64 + 12 * B]))
            done(ts(mods[:, 1:12:3, :], mods[:, 1:12:3, :], 1.0, None, ALU.add))
            for l in range(2):
                g2 = mods[:, 6 * l + 2:6 * l + 6:3, :]
                done(ts(mod_abs[:, :, :], g2, -1.0, 0.25, ALU.mult, ALU.max))
                done(tt(mod_abs[:, :, :], mod_abs[:, :, :], g2, ALU.max))
                done(ts(mod_sgn[:, :, :], g2, 0.0, 2.0, ALU.is_ge, ALU.mult))
                done(stt(out=g2, in0=mod_sgn[:, :, :], scalar=1.0, in1=mod_abs[:, :, :], op0=ALU.subtract, op1=ALU.mult))
            done(ts(mods[:, 12, :], mods[:, 2, :], bcol[:, 3:4], None, ALU.mult))
            dve.wait_ge(c_pe, 4)
            done(nc.vector.tensor_copy(ffn_w[:, :, :].rearrange("p n c -> p (n c)"), pb_k[:, 0:3 * D]))
            done(nc.vector.tensor_copy(wqk[:, :, :, :], wqkv[:, 0:2 * D].rearrange("p (n h d) -> p n d h", n=2, d=DH)))
            done(ts(wk[:, :], wk[:, :], 10.0 / TWO_PI, None, ALU.mult))
            dve.wait_ge(c_act, 4)
            dve.wait_ge(c_pool, 12)
            dve.wait_ge(c_pe, 5)
            done(nc.vector.tensor_copy(gub_t[:, :, :].rearrange("p g e -> p (g e)"), pb[:, 448:448 + 2 * E]))
            done(ts(relb[:, :], pb_v[:, 0:L], bcol[:, 1:2], None, ALU.add))
            assert count[0] == DVE_SETUP, count[0]

            def centre(b, n, src, dst, ps):
                need(dve, "mean" + n, b, 1)
                other, same = {"1": ("h1", 0), "2": ("h2", 0), "3": ("h4", 0), "4": ("h3", 1)}[n]
                need(dve, other, b, same)
                tt(dst[:, :], src[:, :], ps[:, 0:L], ALU.subtract).then_inc(S["cent" + n], 1)

            def epsilon(b, n, v, ps):
                need(dve, "var" + n, b, 1)
                ts(v[:, :], ps[:, L:L + NT], EPS, None, ALU.add).then_inc(S["veps" + n], 1)

            def scale(b, n, c, ps):
                need(dve, "rbc" + n, b, 1)
                tt(c[:, :], c[:, :], ps[:, L:2 * L], ALU.mult).then_inc(S["norm" + n], 1)

            def at_batch(t, b):
                return t[:, :, b:b + 1] if isinstance(b, int) else t[:, :, bass.ds(b, 1)]

            def head_1(b):
                need(dve, "xt_ps", b, 1)
                need(dve, "x1", b, 0)
                nc.vector.tensor_copy(xt[:, :], pb_k[:, 0:L]).then_inc(S["xt"], 1)
                need(dve, "xt", b, 1)
                need(dve, "h1", b, 0)
                nc.vector.tensor_copy(mod_h[:, :].rearrange("p (k a) -> p k a", a=1), at_batch(mods, b)).then_inc(S["mod_h"], 1)

            def head_2(b):
                centre(b, "1", xt, centh, pb_v)

            def head_3(b):
                epsilon(b, "1", vepsh, pb_v)

            def head_4(b):
                scale(b, "1", centh, pb_v)

            def head_5(b):
                need(dve, "qk_ps", b, 1)
                need(dve, "part2", b, 0)
                ts(qk[:, 0, :], pb_k[:, 0:L], bcol[:, 0:1], float(DH) ** -0.5, ALU.add, ALU.mult).then_inc(S["q_sb"], 1)
                tt(qk[:, 1, :], pb_k[:, L:2 * L], relb[:, :], ALU.add).then_inc(S["k_sb"], 1)
                need(dve, "v_ps", b, 1)
                need(dve, "pv", b, 0)
                for n in range(NT):
                    tt(vt[:, n, :, 0:DH], pb_v[:, n * D:(n + 1) * D].rearrange("p (h d) -> p h d", d=DH),
                       vbias[:, :].rearrange("p (h d) -> p h d", d=DH), ALU.add).then_inc(S["v_sb"], 1)

            def maxima(b, n):
                need(dve, "s_ps", b, n + 1)
                nc.vector.tensor_reduce(smax[:, n // 4, 4 * (n % 4):4 * (n % 4) + 4],
                                        ring[:, n % 2, :].rearrange("p (h k) -> p h k", h=4), AX_X, ALU.max).then_inc(S["s_max"], 1)

            def split_max(b):
                need(dve, "s_max", b, ST)
                ts(negm[:, :, :], smax[:, :, :], -1.0, None, ALU.mult).then_inc(S["neg"], 1)
                need(dve, "neg", b, 1)
                nc.vector.tensor_copy(mpart[:, :, 0, :], negm[:, :, :]).then_inc(S["mp0"], 1)
                need(dve, "mp0", b, 1)
                tt(mrest[:, :, :], negm[:, :, :], mpart[:, :, 0, :], ALU.subtract).then_inc(S["mr0"], 1)
                need(dve, "mr0", b, 1)
                nc.vector.tensor_copy(mpart[:, :, 1, :], mrest[:, :, :]).then_inc(S["mp1"], 1)
                need(dve, "mp1", b, 1)
                tt(mpart[:, :, 2, :], mrest[:, :, :], mpart[:, :, 1, :], ALU.subtract).then_inc(S["mp2"], 1)

            def attn_norm(b):
                need(dve, "or_ps", b, 1)
                nc.vector.reciprocal(rden[:, :, :], o_ps[:, :, :, DH]).then_inc(S["den"], 1)
                need(dve, "den", b, 1)
                need(dve, "ot_ps", b, 0)
                for n in range(NT):
                    tt(o_tok[:, n, :, :], o_ps[:, n, :, 0:DH],
                       rden[:, n, :].rearrange("p (h a) -> p h a", a=1).to_broadcast([P, H, DH]), ALU.mult).then_inc(S["o_sb"], 1)

            def route(b):
                need(dve, "lg_ps", b, 1)
                rb = rbias[:, :].rearrange("p (a e) -> p a e", a=1).to_broadcast([P, NT, E])
                tt(lg[:, :, TOPK:], ring[:, 0, 0:NT * E].rearrange("p (n e) -> p n e", e=E), rb, ALU.add).then_inc(S["lg"], 1)
                dve.wait_ge(c_dve, DVE_SETUP)
                need(dve, "lg", b, 1)
                for n in range(NT):
                    nc.vector.max(top8[:, n, :], lg[:, n, :]).then_inc(S["top8"], 1)
                need(dve, "top8", b, NT)
                tt(lsh[:, :, :], lg[:, :, TOPK:], top8[:, :, 4:5].to_broadcast([P, NT, E]), ALU.subtract).then_inc(S["shift"], 1)
                for n in range(NT):
                    nc.vector.match_replace(out=repl[:, n, :], in_to_replace=top8[:, n, :], in_values=lg[:, n, :],
                                            imm_value=-BIG).then_inc(S["repl"], 1)

            def route_2(b):
                need(dve, "repl", b, NT)
                need(dve, "ex", b, 1)
                for n in range(NT):
                    stt(out=exm[:, n, :], in0=repl[:, n, TOPK:], scalar=-BIG, in1=ex[:, n, :], op0=ALU.is_equal,
                        op1=ALU.mult).then_inc(S["exm"], 1)
                need(dve, "exm", b, NT)
                nc.vector.tensor_reduce(esum[:, :], exm[:, :, :], AX_X, ALU.add).then_inc(S["esum"], 1)
                need(dve, "esum", b, 1)
                nc.vector.reciprocal(rsum[:, :], esum[:, :]).then_inc(S["rsum"], 1)
                need(dve, "rsum", b, 1)
                need(dve, "sct_ps", b, 0)
                tt(sc[:, :, 0:E], exm[:, :, :], rsum[:, :].rearrange("p (n a) -> p n a", a=1).to_broadcast([P, NT, E]),
                   ALU.mult).then_inc(S["sc"], 1)
                need(dve, "sc", b, 1)
                nc.vector.tensor_copy(sc_part[:, :, 0:E], sc[:, :, 0:E]).then_inc(S["sp0"], 1)
                need(dve, "sp0", b, 1)
                tt(srest[:, :, :], sc[:, :, 0:E], sc_part[:, :, 0:E], ALU.subtract).then_inc(S["sr0"], 1)
                need(dve, "sr0", b, 1)
                nc.vector.tensor_copy(sc_part[:, :, E:2 * E], srest[:, :, :]).then_inc(S["sp1"], 1)
                need(dve, "sp1", b, 1)
                tt(sc_part[:, :, 2 * E:3 * E], srest[:, :, :], sc_part[:, :, E:2 * E], ALU.subtract).then_inc(S["sp2"], 1)

            def gate(b, n):
                need(dve, "gu_ps", b, n + 1)
                need(dve, "gl", b, n - NG + 1)
                for j in range(2):
                    ts(gsc[:, n % NG, j * L:(j + 1) * L], ring[:, n % 2, j * L:(j + 1) * L],
                       gub_t[:, 0, 2 * n + j:2 * n + j + 1], LIMIT, ALU.add, ALU.min).then_inc(S["gc"], 1)

            def clip_up(b, n):
                need(dve, "upr", b, 2 * n + 2)
                ts(upc[:, n % NU, :], upc[:, n % NU, :], LIMIT + 1.0, 1.0 - LIMIT, ALU.min, ALU.max).then_inc(S["upc"], 1)

            def gated(b, n):
                need(dve, "gsc", b, n + 1)
                need(dve, "act", b, n - 1)
                tt(glu[:, n % 2, :], sig[:, n % NG, :], gsc[:, n % NG, :], ALU.mult).then_inc(S["gl"], 1)

            def expert_last(b, n):
                if n in BY_DVE:
                    need(dve, "act", b, n)
                    need(dve, "upc", b, n + 1)
                    need(dve, "gl", b, n + 1)
                    tt(upc[:, n % NU, :], upc[:, n % NU, :], glu[:, n % 2, :], ALU.mult).then_inc(S["act"], 1)

            def experts_out(b):
                need(dve, "dn", b, 8)
                ts(ya[:, :], pa[:, 0:L], mod_a[:, 5:6], None, ALU.mult).then_inc(S["y2"], 1)
                need(dve, "y2", b, 1)
                need(dve, "x3", b, 0)
                tt(x2[:, :], x1[:, :], ya[:, :], ALU.add).then_inc(S["x2"], 1)

            def head_b(b):
                need(dve, "x2", b, 1)
                nc.vector.tensor_copy(mod_b[:, :].rearrange("p (k a) -> p k a", a=1), at_batch(mods, b)).then_inc(S["mod_b"], 1)
                centre(b, "3", x2, centb, pb)

            def memory_a(b, c):
                h = c % 2
                need(dve, "turn", b, c + 1)
                need(dve, "fabs", b, c - 1)
                stt(out=frac[:, h, :], in0=turn[:, :], scalar=MAGIC, in1=pb_k[:, :], op0=ALU.subtract,
                    op1=ALU.subtract).then_inc(S["frac"], 1)

            def memory_b(b, c):
                h = c % 2
                need(dve, "wo", b, c - 1)
                need(dve, "val", b, c + 1)
                v = val[:, h, :].rearrange("p (k t) -> p k t", k=2)
                need(dve, "cos", b, c + 1)
                for n, t in ((2, cos_t), (3, sin_t)):
                    tt(prod[:, h, n, :].rearrange("p (k t) -> p k t", k=2), v, t[:, h, :, 0:L], ALU.mult).then_inc(S["in" + str(n + 1)], 1)

            def memory_s(b, c):
                h = c % 2
                for n, s in ((0, "cu1"), (1, "cu2")):
                    need(dve, "in" + str(n + 1), b, c + 1)
                    nc.vector.tensor_tensor_scan(prod[:, h, n, :], keep[:, :], prod[:, h, n, :], 0.0, ALU.mult,
                                                 ALU.add).then_inc(S[s], 1)

            def memory_c(b, c):
                h = c % 2
                for n in (2, 3):
                    need(dve, "in" + str(n + 1), b, c + 1)
                    nc.vector.tensor_tensor_scan(prod[:, h, n, :], keep[:, :], prod[:, h, n, :], 0.0, ALU.mult,
                                                 ALU.add).then_inc(S["cu" + str(n + 1)], 1)

            def memory_d(b, c):
                h = c % 2
                for n, t in ((2, cos_t), (3, sin_t)):
                    need(dve, "cu" + str(n + 1), b, c + 1)
                    cv = prod[:, h, n, :].rearrange("p (k t) -> p k t", k=2)
                    tt(cv, cv, t[:, h, :, 1:L + 1], ALU.mult).then_inc(S["pr" + str(n + 1)], 1)
                need(dve, "pr3", b, c + 1)
                need(dve, "pr4", b, c + 1)
                tt(prod[:, h, 2, :], prod[:, h, 2, :], prod[:, h, 3, :], ALU.add).then_inc(S["sum34"], 1)

            def memory_end(b):
                need(dve, "wo", b, CC)
                stt(out=dif[:, :], in0=pb[:, 0:L], scalar=mod_b[:, 8:9], in1=inv_s[:, :], op0=ALU.mult,
                    op1=ALU.mult).then_inc(S["yv"], 1)
                need(dve, "yv", b, 1)
                tt(x3[:, :], x2[:, :], dif[:, :], ALU.add).then_inc(S["x3"], 1)

            def mix_in(b):
                need(dve, "h4", b, 1)
                tt(dif[:, :], hb[:, 1:L + 1], hb[:, 0:L], ALU.subtract).then_inc(S["dif"], 1)
                need(dve, "dif", b, 1)
                need(dve, "rk_ps", b, 0)
                stt(out=xr[:, :], in0=dif[:, :], scalar=mu[:, 0:1], in1=hb[:, 0:L], op0=ALU.mult, op1=ALU.add).then_inc(S["xr"], 1)
                stt(out=xk[:, :], in0=dif[:, :], scalar=mu[:, 1:2], in1=hb[:, 0:L], op0=ALU.mult, op1=ALU.add).then_inc(S["xk"], 1)

            def mix_out(b):
                need(dve, "vv_ps", b, 1)
                need(dve, "rsig", b, 1)
                stt(out=xr[:, :], in0=pb_v[:, 0:L], scalar=mod_b[:, 11:12], in1=rsig[:, :], op0=ALU.mult,
                    op1=ALU.mult).then_inc(S["rv"], 1)
                need(dve, "rv", b, 1)
                need(dve, "xo_ps", b, 0)
                tt(x4[:, :], x3[:, :], xr[:, :], ALU.add).then_inc(S["x4"], 1)

            def head(nx):
                head_1(nx)
                head_2(nx)
                head_3(nx)
                head_4(nx)
                head_5(nx)
                maxima(nx, 0)

            def step(a, b, nx):
                on_a, on_b, on_x = a is not None, b is not None, nx is not None
                if on_b:
                    head_b(b)
                if on_a:
                    need(dve, "x2", a, 0)
                    nc.vector.tensor_copy(mod_a[:, :].rearrange("p (k a) -> p k a", a=1), at_batch(mods, a)).then_inc(S["mod_a"], 1)
                    maxima(a, 1)
                if on_b:
                    epsilon(b, "3", vepsb, pb)
                if on_a:
                    maxima(a, 2)
                if on_b:
                    scale(b, "3", centb, pb)
                if on_a:
                    for n in (3, 4, 5):
                        maxima(a, n)
                if on_b:
                    memory_a(b, 0)
                if on_a:
                    maxima(a, 6)
                    maxima(a, 7)
                    split_max(a)
                if on_b:
                    memory_b(b, 0)
                    memory_a(b, 1)
                    memory_s(b, 0)
                    memory_c(b, 0)
                    memory_d(b, 0)
                    memory_a(b, 2)
                    memory_b(b, 1)
                    memory_s(b, 1)
                    memory_c(b, 1)
                    memory_d(b, 1)
                    memory_b(b, 2)
                    memory_s(b, 2)
                    memory_c(b, 2)
                    memory_d(b, 2)
                    memory_a(b, 3)
                    memory_s(b, 3)
                if on_a:
                    attn_norm(a)
                if on_b:
                    memory_b(b, 3)
                if on_x:
                    head_1(nx)
                if on_a:
                    centre(a, "2", x1, cent, pa)
                if on_x:
                    head_2(nx)
                if on_b:
                    memory_c(b, 3)
                if on_a:
                    epsilon(a, "2", veps, pa)
                if on_x:
                    head_3(nx)
                if on_b:
                    memory_d(b, 3)
                if on_a:
                    scale(a, "2", cent, pa)
                if on_x:
                    head_4(nx)
                if on_a:
                    route(a)
                    route_2(a)
                if on_b:
                    memory_end(b)
                if on_x:
                    head_5(nx)
                if on_b:
                    centre(b, "4", x3, centb, pb)
                    epsilon(b, "4", vepsb, pb)
                    scale(b, "4", centb, pb)
                    mix_in(b)
                if on_a:
                    gate(a, 0)
                    gate(a, 1)
                    clip_up(a, 0)
                    for n in range(2, E // 2):
                        gate(a, n)
                        gated(a, n - 2)
                        clip_up(a, n - 1)
                        expert_last(a, n - 2)
                        if on_b and n == 3:
                            mix_out(b)
                elif on_b:
                    mix_out(b)
                if on_a:
                    gated(a, E // 2 - 2)
                    clip_up(a, E // 2 - 1)
                    expert_last(a, E // 2 - 2)
                    gated(a, E // 2 - 1)
                    expert_last(a, E // 2 - 1)
                    experts_out(a)
                if on_x:
                    maxima(nx, 0)

            run(dve, head, step)


DVE_TRIG = 11
DVE_BIAS = 15
DVE_SETUP = 31


def later(b):
    return 1 if isinstance(b, int) and b == B - 1 else 2


def run(eng, head, step):
    head(0)
    step(0, None, 1)
    step(1, 0, 2)
    with eng.Fori(2, B - 1) as i:
        step(i, i - 1, i + 1)
    step(B - 1, B - 2, None)
    step(None, B - 1, None)


_INS = ['L0_attn_x', 'L0_attn_Wqkv', 'L0_attn_bqkv', 'L0_attn_Wout', 'L0_attn_bout', 'L0_attn_rel_emb',
        'L0_ffn_router_w', 'L0_ffn_router_b', 'L0_ffn_gate_up_proj', 'L0_ffn_gate_up_bias', 'L0_ffn_down_proj',
        'L0_ffn_down_bias', 'L0_c', 'L0_wmod', 'L1_attn_Wk', 'L1_attn_Wv', 'L1_attn_Wo', 'L1_attn_gate',
        'L1_attn_freqs', 'L1_ffn_W_r', 'L1_ffn_W_k', 'L1_ffn_W_v', 'L1_ffn_mu_r', 'L1_ffn_mu_k', 'L1_c', 'L1_wmod']


def kernel(**inputs):
    import numpy as _np
    import concourse.bacc as _bacc
    from concourse import mybir as _mybir
    from concourse.bass_utils import run_bass_kernel_spmd as _run

    nc = _bacc.Bacc("TRN2", target_bir_lowering=False, num_devices=1)
    arrays, args = {}, []
    for name in _INS:
        a = _np.ascontiguousarray(inputs[name])
        arrays[f"in_{name}_dram"] = a
        args.append(nc.dram_tensor(f"in_{name}_dram", a.shape, _mybir.dt.from_np(a.dtype), kind="ExternalInput").ap())
    args.append(nc.dram_tensor("out_dram", (B, L, D), _mybir.dt.float32, kind="ExternalOutput").ap())
    build(nc, *args)
    r = _run(nc, [arrays], core_ids=[0])
    return r.results[0]["out_dram"]
```
